# Optimizing a Trainium2 kernel written in Bass

```python
import numpy as np
import jax
import jax.numpy as jnp

def _softmax(x, axis=-1):
    return jax.nn.softmax(x, axis=axis)

def _gelu(x):
    return jax.nn.gelu(x, approximate=True)

def _silu(x):
    return jax.nn.silu(x)

def _sigmoid(x):
    return jax.nn.sigmoid(x)

def _layernorm(x, axis=-1, eps=1e-05):
    m = jnp.mean(x, axis=axis, keepdims=True)
    v = jnp.var(x, axis=axis, keepdims=True)
    return (x - m) / jnp.sqrt(v + eps)

def _scatter_add(tgt, idx, src, axis=0):
    return tgt.at[idx].add(src)

def _segment_sum(src, seg, n):
    return jax.ops.segment_sum(src, seg, n)
kernel_name = 'mk_lm_tower_d2_tok_ids2048_r4_9e42ef'

def setup_inputs(seed: int=0):
    np.random.seed(seed)
    _w = jnp.asarray

    def _rec_inputs():
        import jax
        import jax.numpy as jnp
        _rk = jax.random.key(seed)
        x = jax.random.randint(jax.random.fold_in(_rk, 1), (4, 512), 0, 9999594, jnp.int32)
        return x
    x = _rec_inputs()

    def _L0_tok_setup():
        import jax, jax.numpy as jnp
        import numpy as np
        B = 8
        N = 512
        NUM_BUCKETS = 128

        def _bucketize(x):
            xa = jnp.maximum(jnp.abs(x), 1).astype(jnp.float32)
            return jnp.floor(jnp.log(xa) / jnp.log(2.0)).astype(jnp.int32)
        key = jax.random.key(seed)
        k1, k2, k3 = jax.random.split(key, 3)
        all_timestamps = jnp.sort(jax.random.randint(k1, (B, N), 0, 2500000, dtype=jnp.int64), axis=1)
        ts_w = 0.02 * jax.random.normal(k2, (NUM_BUCKETS + 1,), dtype=jnp.float32)
        pos_w = 0.02 * jax.random.normal(k3, (2 * N - 1,), dtype=jnp.float32)
        return {'all_timestamps': all_timestamps, 'ts_w': ts_w, 'pos_w': pos_w}
    _L0_tok_all = _L0_tok_setup()
    _L0_tok_in = {k: v for k, v in _L0_tok_all.items() if k in ('ts_w', 'pos_w')}
    del _L0_tok_all

    def _L0_attn_setup():
        import jax, jax.numpy as jnp
        import numpy as np
        H = 512
        NH = 16
        Q_LORA = 384
        KV_LORA = 128
        D_NOPE = 128
        D_ROPE = 64
        D_QK = D_NOPE + D_ROPE
        D_V = 128
        EPS = 1e-06
        THETA = 10000.0
        SCALE = D_QK ** (-0.5)

        def rmsnorm(x, w):
            return x * jax.lax.rsqrt(jnp.mean(x * x, axis=-1, keepdims=True) + EPS) * w

        def rope_cos_sin(seq_len, dtype):
            inv_freq = 1.0 / THETA ** (jnp.arange(0, D_ROPE, 2, dtype=jnp.float32) / D_ROPE)
            pos = jnp.arange(seq_len, dtype=jnp.float32)
            freqs = pos[:, None] * inv_freq[None, :]
            emb = jnp.concatenate([freqs, freqs], axis=-1)
            return (jnp.cos(emb).astype(dtype), jnp.sin(emb).astype(dtype))

        def apply_rope(x, cos, sin):
            half = x.shape[-1] // 2
            x1, x2 = (x[..., :half], x[..., half:])
            rot = jnp.concatenate([-x2, x1], axis=-1)
            c = cos[None, :, None, :]
            s = sin[None, :, None, :]
            return x * c + rot * s
        key = jax.random.key(seed)
        ks = jax.random.split(key, 8)
        f = lambda k, shape: jax.random.normal(k, shape, dtype=jnp.float32) * 0.02
        return {'hidden_states': jax.random.normal(ks[0], (2, 512, H), dtype=jnp.float32), 'wq_a': f(ks[1], (Q_LORA, H)), 'q_norm_w': jnp.ones((Q_LORA,), jnp.float32), 'wq_b': f(ks[2], (NH * D_QK, Q_LORA)), 'wkv_a': f(ks[3], (KV_LORA + D_ROPE, H)), 'kv_norm_w': jnp.ones((KV_LORA,), jnp.float32), 'wkv_b': f(ks[4], (NH * (D_NOPE + D_V), KV_LORA)), 'wo': f(ks[5], (H, NH * D_V))}
    _L0_attn_all = _L0_attn_setup()
    _L0_attn_in = {k: v for k, v in _L0_attn_all.items() if k in ('wq_a', 'q_norm_w', 'wq_b', 'wkv_a', 'kv_norm_w', 'wkv_b', 'wo')}
    del _L0_attn_all

    def _L0_ffn_setup():
        import jax, jax.numpy as jnp
        import numpy as np
        QMAX = 127.0
        EPS = 1e-08

        def _quant_dequant(v, axis):
            scale = jnp.max(jnp.abs(v), axis=axis, keepdims=True) / QMAX
            scale = jnp.maximum(scale, EPS)
            q = jnp.clip(jnp.round(v / scale), -QMAX, QMAX)
            return q * scale

        def _ste(v, axis):
            return v + jax.lax.stop_gradient(_quant_dequant(v, axis) - v)
        key = jax.random.key(seed)
        k1, k2, k3 = jax.random.split(key, 3)
        H, I = (512, 1408)
        x = jax.random.normal(k1, (4, 512, H), dtype=jnp.float32)
        w_gate_up = jax.random.normal(k2, (2 * I, H), dtype=jnp.float32) * H ** (-0.5)
        w_down = jax.random.normal(k3, (H, I), dtype=jnp.float32) * I ** (-0.5)
        return {'x': x, 'w_gate_up': w_gate_up, 'w_down': w_down}
    _L0_ffn_all = _L0_ffn_setup()
    _L0_ffn_in = {k: v for k, v in _L0_ffn_all.items() if k in ('w_gate_up', 'w_down')}
    del _L0_ffn_all

    def _L1_attn_setup():
        import jax, jax.numpy as jnp
        import numpy as np
        import math
        DIM = 512
        N_HEADS = 16
        N_KV_HEADS = 8
        HEAD_DIM = DIM // N_HEADS
        N_REP = N_HEADS // N_KV_HEADS
        BLOCK = 128
        TOPK = 8
        NEG_INF = -10000.0
        SEQ = 1024
        BS = 1

        def _rope_tables(seq_len, head_dim, base=10000.0):
            inv_freq = 1.0 / base ** (jnp.arange(0, head_dim, 2, dtype=jnp.float32) / head_dim)
            ang = jnp.arange(seq_len, dtype=jnp.float32)[:, None] * inv_freq[None, :]
            return (jnp.cos(ang), jnp.sin(ang))

        def _apply_rope(t, cos, sin):
            t1 = t[..., 0::2]
            t2 = t[..., 1::2]
            c = cos[None, :, None, :]
            s = sin[None, :, None, :]
            out_even = t1 * c - t2 * s
            out_odd = t1 * s + t2 * c
            out = jnp.stack([out_even, out_odd], axis=-1)
            return out.reshape(t.shape)
        key = jax.random.key(seed)
        ks = jax.random.split(key, 5)
        scale = 1.0 / math.sqrt(DIM)
        x = jax.random.normal(ks[0], (BS, SEQ, DIM), dtype=jnp.float32)
        wq = jax.random.normal(ks[1], (DIM, N_HEADS * HEAD_DIM), dtype=jnp.float32) * scale
        wk = jax.random.normal(ks[2], (DIM, N_KV_HEADS * HEAD_DIM), dtype=jnp.float32) * scale
        wv = jax.random.normal(ks[3], (DIM, N_KV_HEADS * HEAD_DIM), dtype=jnp.float32) * scale
        wo = jax.random.normal(ks[4], (DIM, DIM), dtype=jnp.float32) * scale
        return {'x': x, 'wq': wq, 'wk': wk, 'wv': wv, 'wo': wo}
    _L1_attn_all = _L1_attn_setup()
    _L1_attn_in = {k: v for k, v in _L1_attn_all.items() if k in ('wq', 'wk', 'wv', 'wo')}
    del _L1_attn_all

    def _L1_ffn_setup():
        import jax, jax.numpy as jnp
        import numpy as np
        EPS = 1e-05
        NUM_BITS = 8

        def _round_ste(x):
            return x + jax.lax.stop_gradient(jnp.round(x) - x)

        def _clamp_ste(x, lo=-1.0, hi=1.0):
            return x + jax.lax.stop_gradient(jnp.clip(x, lo, hi) - x)

        def ternary_quantize(w):
            scale = jnp.maximum(jnp.mean(jnp.abs(w)), EPS)
            q = _clamp_ste(_round_ste(w / scale))
            return scale * q

        def quantized_relu2(x, num_bits=NUM_BITS, eps=EPS):
            x = jnp.square(jax.nn.relu(x))
            xmax = jnp.maximum(jnp.max(x, axis=-1, keepdims=True), eps)
            num_steps = 2 ** num_bits - 1
            return _round_ste(x / xmax * num_steps) / num_steps * xmax
        key = jax.random.key(seed)
        k1, k2, k3 = jax.random.split(key, 3)
        B, S, D = (4, 512, 512)
        H = 4 * D
        std = 0.5 * D ** (-0.5)
        x = jax.random.normal(k1, (B, S, D), dtype=jnp.float32)
        c_fc = jax.random.normal(k2, (D, H), dtype=jnp.float32) * std
        c_proj = jax.random.normal(k3, (D, H), dtype=jnp.float32) * std
        return {'x': x, 'c_fc': c_fc, 'c_proj': c_proj}
    _L1_ffn_all = _L1_ffn_setup()
    _L1_ffn_in = {k: v for k, v in _L1_ffn_all.items() if k in ('c_fc', 'c_proj')}
    del _L1_ffn_all
    return {'x': x, 'L0_tok_ts_w': _L0_tok_in['ts_w'], 'L0_tok_pos_w': _L0_tok_in['pos_w'], 'L0_attn_wq_a': _L0_attn_in['wq_a'], 'L0_attn_q_norm_w': _L0_attn_in['q_norm_w'], 'L0_attn_wq_b': _L0_attn_in['wq_b'], 'L0_attn_wkv_a': _L0_attn_in['wkv_a'], 'L0_attn_kv_norm_w': _L0_attn_in['kv_norm_w'], 'L0_attn_wkv_b': _L0_attn_in['wkv_b'], 'L0_attn_wo': _L0_attn_in['wo'], 'L0_ffn_w_gate_up': _L0_ffn_in['w_gate_up'], 'L0_ffn_w_down': _L0_ffn_in['w_down'], 'L1_attn_wq': _L1_attn_in['wq'], 'L1_attn_wk': _L1_attn_in['wk'], 'L1_attn_wv': _L1_attn_in['wv'], 'L1_attn_wo': _L1_attn_in['wo'], 'L1_ffn_c_fc': _L1_ffn_in['c_fc'], 'L1_ffn_c_proj': _L1_ffn_in['c_proj']}

def reference(x, L0_tok_ts_w, L0_tok_pos_w, L0_attn_wq_a, L0_attn_q_norm_w, L0_attn_wq_b, L0_attn_wkv_a, L0_attn_kv_norm_w, L0_attn_wkv_b, L0_attn_wo, L0_ffn_w_gate_up, L0_ffn_w_down, L1_attn_wq, L1_attn_wk, L1_attn_wv, L1_attn_wo, L1_ffn_c_fc, L1_ffn_c_proj):
    import jax
    import jax.numpy as jnp

    def _L0_tok_ref(all_timestamps, ts_w, pos_w):
        import jax, jax.numpy as jnp
        import numpy as np
        B = 8
        N = 512
        NUM_BUCKETS = 128

        def _bucketize(x):
            xa = jnp.maximum(jnp.abs(x), 1).astype(jnp.float32)
            return jnp.floor(jnp.log(xa) / jnp.log(2.0)).astype(jnp.int32)
        n = N
        idx = jnp.arange(n)
        rel_idx = idx[None, :] - idx[:, None] + (n - 1)
        rel_pos_bias = pos_w[rel_idx][None, :, :]
        ext = jnp.concatenate([all_timestamps, all_timestamps[:, n - 1:n]], axis=1)
        diff = ext[:, 1:, None] - ext[:, None, :-1]
        buckets = jnp.clip(_bucketize(diff), 0, NUM_BUCKETS)
        rel_ts_bias = ts_w[buckets]
        return rel_pos_bias + rel_ts_bias

    def _L0_attn_ref(hidden_states, wq_a, q_norm_w, wq_b, wkv_a, kv_norm_w, wkv_b, wo):
        import jax, jax.numpy as jnp
        import numpy as np
        H = 512
        NH = 16
        Q_LORA = 384
        KV_LORA = 128
        D_NOPE = 128
        D_ROPE = 64
        D_QK = D_NOPE + D_ROPE
        D_V = 128
        EPS = 1e-06
        THETA = 10000.0
        SCALE = D_QK ** (-0.5)

        def rmsnorm(x, w):
            return x * jax.lax.rsqrt(jnp.mean(x * x, axis=-1, keepdims=True) + EPS) * w

        def rope_cos_sin(seq_len, dtype):
            inv_freq = 1.0 / THETA ** (jnp.arange(0, D_ROPE, 2, dtype=jnp.float32) / D_ROPE)
            pos = jnp.arange(seq_len, dtype=jnp.float32)
            freqs = pos[:, None] * inv_freq[None, :]
            emb = jnp.concatenate([freqs, freqs], axis=-1)
            return (jnp.cos(emb).astype(dtype), jnp.sin(emb).astype(dtype))

        def apply_rope(x, cos, sin):
            half = x.shape[-1] // 2
            x1, x2 = (x[..., :half], x[..., half:])
            rot = jnp.concatenate([-x2, x1], axis=-1)
            c = cos[None, :, None, :]
            s = sin[None, :, None, :]
            return x * c + rot * s
        B, S, _ = hidden_states.shape
        q = rmsnorm(hidden_states @ wq_a.T, q_norm_w) @ wq_b.T
        q = q.reshape(B, S, NH, D_QK)
        q_nope, q_pe = (q[..., :D_NOPE], q[..., D_NOPE:])
        kv = hidden_states @ wkv_a.T
        kv_c, k_pe = (kv[..., :KV_LORA], kv[..., KV_LORA:])
        cos, sin = rope_cos_sin(S, hidden_states.dtype)
        q_pe = apply_rope(q_pe, cos, sin)
        k_pe = apply_rope(k_pe[:, :, None, :], cos, sin)
        kv_dec = rmsnorm(kv_c, kv_norm_w) @ wkv_b.T
        kv_dec = kv_dec.reshape(B, S, NH, D_NOPE + D_V)
        k_nope, v = (kv_dec[..., :D_NOPE], kv_dec[..., D_NOPE:])
        qf = jnp.concatenate([q_nope, q_pe], axis=-1)
        kf = jnp.concatenate([k_nope, jnp.broadcast_to(k_pe, (B, S, NH, D_ROPE))], axis=-1)
        scores = jnp.einsum('bqhd,bkhd->bhqk', qf, kf) * SCALE
        causal = jnp.tril(jnp.ones((S, S), dtype=bool))
        scores = jnp.where(causal[None, None], scores, jnp.finfo(scores.dtype).min)
        probs = jax.nn.softmax(scores, axis=-1)
        attn = jnp.einsum('bhqk,bkhd->bqhd', probs, v)
        return attn.reshape(B, S, NH * D_V) @ wo.T

    def _L0_ffn_ref(x, w_gate_up, w_down):
        import jax, jax.numpy as jnp
        import numpy as np
        QMAX = 127.0
        EPS = 1e-08

        def _quant_dequant(v, axis):
            scale = jnp.max(jnp.abs(v), axis=axis, keepdims=True) / QMAX
            scale = jnp.maximum(scale, EPS)
            q = jnp.clip(jnp.round(v / scale), -QMAX, QMAX)
            return q * scale

        def _ste(v, axis):
            return v + jax.lax.stop_gradient(_quant_dequant(v, axis) - v)
        I = w_down.shape[1]
        xq = _ste(x, axis=-1)
        w1q = _ste(w_gate_up, axis=-1)
        gate_up = jnp.einsum('bsh,oh->bso', xq, w1q)
        gate, up = (gate_up[..., :I], gate_up[..., I:])
        h = jax.nn.silu(gate) * up
        hq = _ste(h, axis=-1)
        w2q = _ste(w_down, axis=-1)
        return jnp.einsum('bsi,oi->bso', hq, w2q)

    def _L1_attn_ref(x, wq, wk, wv, wo):
        import jax, jax.numpy as jnp
        import numpy as np
        import math
        DIM = 512
        N_HEADS = 16
        N_KV_HEADS = 8
        HEAD_DIM = DIM // N_HEADS
        N_REP = N_HEADS // N_KV_HEADS
        BLOCK = 128
        TOPK = 8
        NEG_INF = -10000.0
        SEQ = 1024
        BS = 1

        def _rope_tables(seq_len, head_dim, base=10000.0):
            inv_freq = 1.0 / base ** (jnp.arange(0, head_dim, 2, dtype=jnp.float32) / head_dim)
            ang = jnp.arange(seq_len, dtype=jnp.float32)[:, None] * inv_freq[None, :]
            return (jnp.cos(ang), jnp.sin(ang))

        def _apply_rope(t, cos, sin):
            t1 = t[..., 0::2]
            t2 = t[..., 1::2]
            c = cos[None, :, None, :]
            s = sin[None, :, None, :]
            out_even = t1 * c - t2 * s
            out_odd = t1 * s + t2 * c
            out = jnp.stack([out_even, out_odd], axis=-1)
            return out.reshape(t.shape)
        bs, S, _ = x.shape
        inv_sqrt_d = 1.0 / math.sqrt(HEAD_DIM)
        q = (x @ wq).reshape(bs, S, N_HEADS, HEAD_DIM)
        k = (x @ wk).reshape(bs, S, N_KV_HEADS, HEAD_DIM)
        v = (x @ wv).reshape(bs, S, N_KV_HEADS, HEAD_DIM)
        cos, sin = _rope_tables(S, HEAD_DIM)
        q = _apply_rope(q, cos, sin)
        k = _apply_rope(k, cos, sin)
        q = jnp.transpose(q, (0, 2, 1, 3))
        k = jnp.transpose(k, (0, 2, 1, 3))
        v = jnp.transpose(v, (0, 2, 1, 3))
        k_e = jnp.repeat(k, N_REP, axis=1)
        v_e = jnp.repeat(v, N_REP, axis=1)
        num_blocks = S // BLOCK
        k_blocks = k_e.reshape(bs, N_HEADS, num_blocks, BLOCK, HEAD_DIM)
        block_means = k_blocks.mean(axis=3)
        gating = jnp.einsum('bhsd,bhnd->bhsn', q, block_means) * inv_sqrt_d
        q_block_idx = jnp.arange(S) // BLOCK
        future_block = q_block_idx[:, None] < jnp.arange(num_blocks)[None, :]
        gating = jnp.where(future_block[None, None], NEG_INF, gating)
        curr_k = min(TOPK, num_blocks)
        _, sel_idx = jax.lax.top_k(gating, curr_k)
        selected = jnp.sum(jax.nn.one_hot(sel_idx, num_blocks, dtype=jnp.float32), axis=-2) > 0
        token_keep = jnp.repeat(selected, BLOCK, axis=-1)[..., :S]
        token_mask = jnp.where(token_keep, 0.0, NEG_INF)
        scores = jnp.einsum('bhsd,bhtd->bhst', q, k_e) * inv_sqrt_d
        causal = jnp.triu(jnp.ones((S, S), dtype=jnp.float32), k=1)
        final_mask = jnp.maximum(token_mask, causal[None, None] * NEG_INF)
        scores = scores + final_mask
        probs = jax.nn.softmax(scores.astype(jnp.float32), axis=-1).astype(scores.dtype)
        out = jnp.einsum('bhst,bhtd->bhsd', probs, v_e)
        out = jnp.transpose(out, (0, 2, 1, 3)).reshape(bs, S, N_HEADS * HEAD_DIM)
        return out @ wo

    def _L1_ffn_ref(x, c_fc, c_proj):
        import jax, jax.numpy as jnp
        import numpy as np
        EPS = 1e-05
        NUM_BITS = 8

        def _round_ste(x):
            return x + jax.lax.stop_gradient(jnp.round(x) - x)

        def _clamp_ste(x, lo=-1.0, hi=1.0):
            return x + jax.lax.stop_gradient(jnp.clip(x, lo, hi) - x)

        def ternary_quantize(w):
            scale = jnp.maximum(jnp.mean(jnp.abs(w)), EPS)
            q = _clamp_ste(_round_ste(w / scale))
            return scale * q

        def quantized_relu2(x, num_bits=NUM_BITS, eps=EPS):
            x = jnp.square(jax.nn.relu(x))
            xmax = jnp.maximum(jnp.max(x, axis=-1, keepdims=True), eps)
            num_steps = 2 ** num_bits - 1
            return _round_ste(x / xmax * num_steps) / num_steps * xmax
        w1 = ternary_quantize(c_fc)
        h = jnp.einsum('bsd,dh->bsh', x, w1)
        h = quantized_relu2(h, num_bits=NUM_BITS)
        w2 = ternary_quantize(c_proj)
        out = jnp.einsum('bsh,dh->bsd', h, w2)
        return out
    h = _L0_tok_ref(x, L0_tok_ts_w, L0_tok_pos_w)
    h = h + _L0_attn_ref(_layernorm(h, axis=-1), L0_attn_wq_a, L0_attn_q_norm_w, L0_attn_wq_b, L0_attn_wkv_a, L0_attn_kv_norm_w, L0_attn_wkv_b, L0_attn_wo)
    h = h + _L0_ffn_ref(_layernorm(h, axis=-1), L0_ffn_w_gate_up, L0_ffn_w_down)
    h = h + _L1_attn_ref(_layernorm(h, axis=-1), L1_attn_wq, L1_attn_wk, L1_attn_wv, L1_attn_wo)
    h = h + _L1_ffn_ref(_layernorm(h, axis=-1), L1_ffn_c_fc, L1_ffn_c_proj)
    return h

_drawn_inputs = setup_inputs


def setup_inputs(seed=0):
    import zlib

    import numpy as np

    out = dict(_drawn_inputs(seed))
    spreads = {'L0_attn_q_norm_w': (1.0, 0.2), 'L0_attn_kv_norm_w': (1.0, 0.2)}
    factors = {}
    for name, (base, spread) in spreads.items():
        noise = np.random.default_rng([zlib.crc32(name.encode()), seed]).standard_normal(out[name].shape)
        drawn = base * np.exp(spread * noise) if base else spread * noise
        out[name] = jnp.asarray(drawn.astype(out[name].dtype))
    for name, factor in factors.items():
        out[name] = (out[name] * factor).astype(out[name].dtype)
    return out
```

```python
from contextlib import ExitStack

import numpy as np
import concourse.bass as bass
from concourse import mybir

F32 = mybir.dt.float32
F32R = mybir.dt.float32r
BF16 = mybir.dt.bfloat16
I32 = mybir.dt.int32
ALU = mybir.AluOpType
ACT = mybir.ActivationFunctionType
AX = mybir.AxisListType.X

P = 128
NB = 4
S = 512
D = 512
TT = S // P
NT = NB * TT
KT = D // P
NH = 16
LORA = 128
QLORA = 384
QK = QLORA // P
ROPE = 64
QKV0 = QLORA + LORA + ROPE
SCALE0 = float(LORA + ROPE) ** -0.5
INTER = 1408
FF = 2048
HD = 32
SCALE1 = float(HD) ** -0.5
BUCKETS = 32
BPP = 4
PASSES = BUCKETS // BPP
MAGIC = 12582912.0

C_ID, C_MASK, C_ROPEQ, C_ROPEK, C_ROPE1, C_ID32, C_GRP, C_FLIP, C_N = 0, 128, 256, 768, 1280, 1536, 1568, 1569, 1697


def constants():
    c = np.zeros((P, C_N), np.float32)
    r = np.arange(P)
    c[:, C_ID:C_ID + P] = np.eye(P)
    c[:, C_MASK:C_MASK + P] = np.where(r[None, :] <= r[:, None], 0.0, -1e30)
    pos = np.arange(S, dtype=np.float32)
    inv = (1.0 / 10000.0 ** (np.arange(0, ROPE, 2, dtype=np.float32) / ROPE)).astype(np.float32)
    ang = (pos[:, None] * inv[None, :]).astype(np.float32)
    cos, sin = np.cos(ang), np.sin(ang)
    c[:, C_ROPEQ:C_ROPEQ + S] = np.concatenate([cos, cos, -sin, sin], 1).T
    k = np.concatenate([cos, cos, -sin, sin], 1).reshape(TT, P, 2 * ROPE)
    c[:, C_ROPEK:C_ROPEK + TT * 2 * ROPE] = k.transpose(1, 0, 2).reshape(P, -1)
    inv = (1.0 / 10000.0 ** (np.arange(0, HD, 2, dtype=np.float32) / HD)).astype(np.float32)
    ang = (pos[:, None] * inv[None, :]).astype(np.float32)
    cos, sin = np.cos(ang), np.sin(ang)
    t = np.concatenate([np.repeat(cos, 2, 1), np.stack([-sin, sin], -1).reshape(S, HD)], 1)
    c[:, C_ROPE1:C_ROPE1 + TT * 2 * HD] = t.reshape(TT, P, 2 * HD).transpose(1, 0, 2).reshape(P, -1)
    c[:, C_ID32:C_ID32 + 32] = (r[:, None] % 32 == np.arange(32)[None, :])
    c[:, C_GRP] = r // 32
    c[:, C_FLIP:C_FLIP + P] = np.eye(P)[::-1]
    return c


def tower_kernel(nc, a, out, stages="FBG"):
    ctx = ExitStack()
    with ctx:
        def sb(name, shape, dt=F32, c=ctx):
            return c.enter_context(nc.sbuf_tensor(name, shape, dt))

        first = []

        first_sems = ExitStack()

        def sem(name, c=ctx):
            return c.enter_context(nc.semaphore(name))

        def sem1(name):
            first.append(sem(name, first_sems))
            return first[-1]

        PS = ctx.enter_context(nc.psum_tensor("PS", [P, 8, 512], F32))
        H = sb("H", [P, NT, D])
        CST = sb("CST", [P, C_N])
        IDB = sb("IDB", [P, P], BF16)
        MASKB = sb("MASKB", [P, P], BF16)
        STAT = sb("STAT", [P, TT, 6])
        MV = sb("MV", [P, TT, 2])
        RSTD = sb("RSTD", [P, TT])
        VEPS = sb("VEPS", [P, TT])
        NHALF = sb("NHALF", [P, 2 * TT])
        ident = CST[:, C_ID:C_ID + P]

        QNS = sb("QNS", [P, QK], F32)

        s_const = sem("s_const")
        s_bar = sem("s_bar")
        s_open = sem("s_open")
        s_alone = sem("s_alone")
        s_pre = sem("s_pre")

        def flat(ap):
            return ap.rearrange("p a n -> p (a n)")

        bars, sync_eng = {}, [None]

        def barrier(eng, clears=False):
            k = bars.get(id(eng), 0) + 1
            bars[id(eng)] = k
            eng.drain().then_inc(s_bar, 1)
            if eng is sync_eng[0]:
                eng.wait_ge(s_bar, 5 * k)
                if clears:
                    for x in first:
                        eng.sem_clear(x)
                eng.sem_inc(s_open, 1)
            eng.wait_ge(s_open, k)

        wqk_scr = nc.dram_tensor("wqk_scr", [NH, P, QK, LORA], F32, kind="Internal").ap()

        class Arena:
            def __enter__(self):
                self.c = ExitStack()
                return self.c

            def __exit__(self, *x):
                self.c.close()

        arena_w = ExitStack()
        WVO = sb("WVO", [P, NH, D], c=arena_w)
        with Arena() as ar:
            XB = sb("XB", [P, NB, S], I32, ar)
            EXT = sb("EXT", [P, NT * 4], I32, ar)
            DIFF = sb("DIFF", [P, 2, 4 * S], I32, ar)
            MAG = sb("MAG", [P, 2, 4 * S], F32, ar)
            EXPO = sb("EXPO", [P, 2, 4 * S], I32, ar)
            EXB = sb("EXB", [P, 2, 4 * S], BF16, ar)
            MSK = sb("MSK", [P, 8, 4 * S], BF16, ar)
            POSB = sb("POSB", [P, TT, S], F32, ar)
            POSF = sb("POSF", [P, TT, S], F32, ar)
            TSC = sb("TSC", [P, PASSES], F32, ar)
            TSH = sb("TSH", [P, 3, PASSES], BF16, ar)
            TSF = sb("TSF", [P, 3, PASSES], F32, ar)
            TSR = sb("TSR", [P, 2, PASSES], F32, ar)
            TAB = sb("TAB", [P, 3, PASSES, 32], BF16, ar)
            WQN = sb("WQN", [P, 2, QLORA], F32, ar)
            WKV = sb("WKV", [P, 2, 2, LORA], F32, ar)
            WOT = sb("WOT", [P, 2, D], F32, ar)
            WQKE = sb("WQKE", [P, 2, QK, LORA], F32, ar)

        s_ids = sem("s_ids"); s_pos = sem1("s_pos"); s_ts = sem1("s_ts")
        s_tab = sem1("s_tab")
        diff_free = sem1("diff_free"); diff_ready = sem1("diff_ready"); mag_ready = sem1("mag_ready")
        expo_ready = sem1("expo_ready"); exb_ready = sem1("exb_ready"); mask_ready = sem1("mask_ready")
        mask_used = sem1("mask_used"); emb_ready = sem1("emb_ready"); h_ready = sem1("h_ready")
        exb_free = sem1("exb_free"); pos_ps = sem1("pos_ps"); pos_ready = sem1("pos_ready")
        w_loaded = [sem1("w_loaded0"), sem1("w_loaded1")]
        w_used = sem1("w_used"); wqk_ps = sem1("wqk_ps"); wqk_sb = sem1("wqk_sb"); wqk_out = sem1("wqk_out")
        wvo_ps = sem1("wvo_ps"); wvo_sb = sem1("wvo_sb")

        def e_sync(eng):
            eng.dma_start(CST[:, :], a["consts"]).then_inc(s_const, 16)
            eng.dma_start(XB[:, :, :].rearrange("p b n -> p (b n)"),
                          a["x"].rearrange("(o b) n -> o (b n)", o=1).to_broadcast([P, NB * S])).then_inc(s_ids, 16)
            eng.dma_start(EXT[:, :], a["ext"]).then_inc(s_ids, 16)
            for t in range(TT):
                src = bass.AP(a["pos_w"].tensor, S - P * (t + 1), [[1, P], [1, S]])
                eng.dma_start(POSF[:, t, :], src).then_inc(s_pos, 16)
            for g in range(4):
                src = bass.AP(a["ts_w"].tensor, g, [[0, 32], [BPP, PASSES]])
                with nc.allow_non_contiguous_dma(reason="32 table entries"):
                    eng.dma_start(TSC[32 * g:32 * g + 32, :], src).then_inc(s_ts, 16)

        def e_pool(eng):
            eng.memset(NHALF[:, :], -0.5).then_inc(s_pre, 1)
            eng.wait_ge(s_ids, 32)
            with eng.Fori(0, NB) as b:
                for t in range(TT):
                    n = b * TT + t
                    eng.wait_ge(diff_free, n + 1)
                    eng.tensor_tensor(
                        DIFF[:, t % 2, :].rearrange("p (q n) -> p q n", q=4),
                        EXT[:, bass.ds(n * 4, 4)].unsqueeze(2).to_broadcast([P, 4, S]),
                        XB[:, bass.ds(b, 1), :].to_broadcast([P, 4, S]), ALU.subtract).then_inc(diff_ready, 1)

        def e_act(eng):
            eng.sem_inc(diff_free, 2)
            eng.sem_inc(exb_free, 2)
            def magnitude(n, u):
                eng.wait_ge(diff_ready, n + 1)
                eng.wait_ge(expo_ready, n)
                eng.activation(MAG[:, u, :], DIFF[:, u, :], ACT.Abs).then_inc(diff_free, 1)

            def exponent(n, u):
                eng.wait_ge(expo_ready, n + 1)
                eng.wait_ge(exb_free, n + 1)
                eng.activation(EXB[:, u, :], EXPO[:, u, :], ACT.Relu, bias=-127.0).then_inc(exb_ready, 1)

            with eng.Fori(0, NB) as b:
                for t in range(TT):
                    magnitude(b * TT + t, t % 2)
                    exponent(b * TT + t, t % 2)

        def e_dve(eng):
            eng.wait_ge(s_const, 16)
            eng.tensor_copy(IDB[:, :], ident).then_inc(s_pre, 1)
            eng.tensor_copy(MASKB[:, :], CST[:, C_MASK:C_MASK + P]).then_inc(s_pre, 1)
            eng.wait_ge(s_ts, 64)
            k = 0
            for part in range(3):
                src = TSC[:, :] if part == 0 else TSR[:, part - 1, :]
                eng.tensor_copy(TSH[:, part, :], src).then_inc(s_tab, 1)
                eng.wait_ge(s_tab, k + 1)
                eng.tensor_copy(TSF[:, part, :], TSH[:, part, :]).then_inc(s_tab, 1)
                eng.wait_ge(s_tab, k + 2)
                k += 2
                if part < 2:
                    eng.tensor_tensor(TSR[:, part, :], src, TSF[:, part, :], ALU.subtract).then_inc(s_tab, 1)
                    k += 1
                    eng.wait_ge(s_tab, k)
            for part in range(3):
                for q in range(PASSES):
                    eng.tensor_scalar(TAB[:, part, q, :], CST[:, C_ID32:C_ID32 + 32], TSF[:, part, q:q + 1], None,
                                      ALU.mult).then_inc(s_tab, 1)
                    k += 1
            for t in range(TT):
                eng.wait_ge(pos_ps, t + 1)
                eng.tensor_copy(POSB[:, t, :], PS[:, 4 + t, :]).then_inc(pos_ready, 1)
            eng.wait_ge(pos_ready, TT)

            def expo(n, u):
                eng.wait_ge(diff_free, n + 3)
                eng.tensor_scalar(EXPO[:, u, :], MAG[:, u, :].bitcast(I32), 23, None,
                                  ALU.logical_shift_right).then_inc(expo_ready, 1)

            def masks(n, u):
                eng.wait_ge(exb_ready, n + 1)
                for q in range(PASSES):
                    eng.wait_ge(mask_used, n * PASSES + q + 1)
                    ins = eng.tensor_scalar(MSK[:, q, :], EXB[:, u, :], CST[:, C_GRP:C_GRP + 1], float(BPP * q),
                                            ALU.subtract, ALU.is_equal).then_inc(mask_ready, 1)
                eng.wait_ge(mask_ready, n * PASSES + PASSES)
                eng.sem_inc(exb_free, 1)

            def add_pos(n, t):
                eng.wait_ge(emb_ready, n + 1)
                eng.tensor_tensor(flat(H[:, bass.ds(n, 1), :]), PS[:, t % 2, :], POSB[:, t, :],
                                  ALU.add).then_inc(h_ready, 1)

            with eng.Fori(0, NB) as b:
                for t in range(TT):
                    expo(b * TT + t, t % 2)
                    masks(b * TT + t, t % 2)
                    add_pos(b * TT + t, t)

        def e_pe(eng):
            eng.sem_inc(mask_used, PASSES)
            eng.wait_ge(s_tab, 32)
            eng.wait_ge(s_pre, 3)
            eng.wait_ge(s_pos, 64)
            for t in range(TT):
                eng.matmul(PS[:, 4 + t, :], CST[:, C_FLIP:C_FLIP + P], POSF[:, t, :], start=True, stop=True)\
                   .then_inc(pos_ps, 1)
            eng.wait_ge(pos_ready, TT)
            with eng.Fori(0, NB) as b:
                for t in range(TT):
                    n = b * TT + t
                    for q in range(PASSES):
                        eng.wait_ge(mask_ready, n * PASSES + q + 1)
                        if q == 0 and t >= 2:
                            eng.wait_ge(h_ready, n - 1)
                        elif q == 0:
                            eng.wait_ge(h_ready, n - t)
                        for part in range(3):
                            for r in range(4):
                                mm = eng.matmul(PS[32 * r:32 * r + 32, t % 2, :], TAB[:, part, q, :],
                                                MSK[:, q, r * S:(r + 1) * S],
                                                start=(q == 0 and part == 0), stop=(q == PASSES - 1 and part == 2))
                        mm.then_inc(mask_used, 1)
                    eng.wait_ge(mask_used, (n + 2) * PASSES)
                    eng.sem_inc(emb_ready, 1)

        def w_sync(eng):
            wq = a["wq_b"].rearrange("(h d) k -> h d k", h=NH)
            wkv = a["wkv_b"].rearrange("(h u d) k -> h d u k", h=NH, u=2)
            wot = a["woT"].rearrange("(h d) n -> h d n", h=NH)
            with eng.Fori(0, NH // 2) as j:
                for u in range(2):
                    h = j * 2 + u
                    eng.wait_ge(w_used, h + 1)
                    eng.dma_start(WQN[:, u, :], wq[bass.ds(h, 1), 0:P, :].rearrange("a d k -> (a d) k"))\
                       .then_inc(w_loaded[u], 16)
                    eng.dma_start(WKV[:, u, :, :], wkv[bass.ds(h, 1)].rearrange("a d u k -> (a d) u k"))\
                       .then_inc(w_loaded[u], 16)
                    eng.dma_start(WOT[:, u, :], wot[bass.ds(h, 1)].rearrange("a d n -> (a d) n"))\
                       .then_inc(w_loaded[u], 16)
                    eng.wait_ge(wqk_sb, h + 1)
                    eng.dma_start(wqk_scr[bass.ds(h, 1)].rearrange("a p k c -> (a p) k c"), WQKE[:, u, :, :])\
                       .then_inc(wqk_out, 16)
            eng.wait_ge(wqk_out, 16 * NH)

        def w_pe(eng):
            eng.sem_inc(w_used, 2)
            with eng.Fori(0, NH // 2) as j:
                for u in range(2):
                    h = j * 2 + u
                    eng.wait_ge(w_loaded[u], j * 48 + 48)
                    if u == 0:
                        eng.wait_ge(wqk_sb, h)
                        eng.wait_ge(wvo_sb, h)
                    for k in range(QK):
                        mm = eng.matmul(PS[:, 2 + u, k * P:(k + 1) * P], WQN[:, u, k * P:(k + 1) * P],
                                        WKV[:, u, 0, :], start=True, stop=True)
                    mm.then_inc(wqk_ps, 1)
                    eng.matmul(PS[:, 4 + u, :], WKV[:, u, 1, :], WOT[:, u, :], start=True, stop=True)\
                       .then_inc(wvo_ps, 1)
                    eng.wait_ge(wvo_ps, h + 1)
                    eng.sem_inc(w_used, 1)

        def w_act(eng):
            with eng.Fori(0, NH // 2) as j:
                for u in range(2):
                    h = j * 2 + u
                    eng.wait_ge(wqk_ps, h + 1)
                    eng.wait_ge(wqk_out, j * 32)
                    eng.activation(WQKE[:, u, :, :].rearrange("p k c -> p (k c)"), PS[:, 2 + u, 0:QLORA],
                                   ACT.Copy).then_inc(wqk_sb, 1)

        def w_dve(eng):
            with eng.Fori(0, NH // 2) as j:
                for u in range(2):
                    h = j * 2 + u
                    eng.wait_ge(wvo_ps, h + 1)
                    eng.tensor_copy(flat(WVO[:, bass.ds(h, 1), :]), PS[:, 4 + u, :]).then_inc(wvo_sb, 1)

        with Arena() as ar:
            WA = sb("WA", [P, KT, QKV0], F32, ar)
            QNW = sb("QNW", [P, QK], F32, ar)
            KVW = sb("KVW", [P, 1], F32, ar)
            WQ = sb("WQ", [P, 2, QK, 2 * P], F32, ar)
            XN = sb("XN", [P, 2, D], F32, ar)
            XNT = sb("XNT", [P, KT, P], F32, ar)
            RAW = sb("RAW", [P, TT, QKV0], F32, ar)
            SQ = sb("SQ", [P, QLORA], F32, ar)
            SSQ = sb("SSQ", [P, 2 * TT], F32, ar)
            MSQ = sb("MSQ", [P, 2 * TT], F32, ar)
            RMS = sb("RMS", [P, 2 * TT], F32, ar)
            KR = sb("KR", [P, 2, ROPE], F32, ar)
            QL = sb("QL", [P, TT, QLORA], F32, ar)
            CN = sb("CN", [P, TT, LORA], F32, ar)
            KP = sb("KP", [P, TT, 2 * ROPE], F32, ar)
            QLT = sb("QLT", [P, QK, S], F32, ar)
            CT = sb("CT", [P, S], F32, ar)
            KPT = sb("KPT", [P, S], F32, ar)
            QN = sb("QN", [P, 2, S], F32, ar)
            QP = sb("QP", [P, 2, S], F32, ar)
            NMX = sb("NMX", [P, 2, TT], F32, ar)
            SUM = sb("SUM", [P, 2, TT], F32, ar)
            RSUM = sb("RSUM", [P, 2, TT], F32, ar)
            PR = sb("PR", [P, TT, S], F32, ar)
            PT = sb("PT", [P, TT, S], F32, ar)
            OT = sb("OT", [P, 2, S], F32, ar)
            ZB = sb("ZB", [P, S], BF16, ar)

        arena_w.close()

        s_wa = sem("s_wa"); ln_s = sem("ln_s"); ln_p = sem("ln_p"); ln_ready = sem("ln_ready"); xn_ready = sem("xn_ready")
        xt_ps = sem("xt_ps"); xt_ready = sem("xt_ready"); raw_ps = sem("raw_ps"); raw_ready = sem("raw_ready")
        ssq_ready = sem("ssq_ready"); msq_ready = sem("msq_ready"); rms_ready = sem("rms_ready")
        kr_done = sem("kr_done"); kv_ready = sem("kv_ready"); kt_ps = sem("kt_ps"); kt_ready = sem("kt_ready"); kc_ready = sem("kc_ready")
        wq_loaded = [sem("wq_loaded0"), sem("wq_loaded1")]
        qn_ps = sem("qn_ps"); qn_ready = sem("qn_ready"); qp_ps = sem("qp_ps"); qp_ready = sem("qp_ready")
        s_ps = sem("s_ps"); max_ready = sem("max_ready"); p_ready = sem("p_ready"); rs_ready = sem("rs_ready")
        pn_ready = sem("pn_ready"); pt_ps = sem("pt_ps"); pt_ready = sem("pt_ready"); ot_ps = sem("ot_ps")
        ot_ready = sem("ot_ready"); w_done = sem("w_done"); res_done = sem("res_done"); zb_ready = sem("zb_ready")
        sq_done = sem("sq_done"); pv_done = sem("pv_done")
        SB, PTB, QB = 4, 6, 7

        def a_sync(eng):
            eng.dma_start(WA[:, :, :], a["waT"].rearrange("(k p) n -> p k n", p=P)).then_inc(s_wa, 16)
            with nc.allow_non_contiguous_dma(reason="norm weights"):
                eng.dma_start(QNW[:, :], a["q_norm_w"].rearrange("(k p) -> p k", p=P)).then_inc(s_wa, 16)
                eng.dma_start(KVW[:, :], a["kv_norm_w"].rearrange("(p o) -> p o", o=1)).then_inc(s_wa, 16)
            wpe = a["wpe"].rearrange("h (k p) c -> h p k c", p=P)
            with eng.Fori(0, NB) as b:
                with eng.Fori(0, NH // 2) as j:
                    for u in range(2):
                        n = b * NH + j * 2 + u
                        eng.wait_ge(wslot_free, n + 1)
                        h = j * 2 + u
                        eng.dma_start(WQ[:, u, :, 0:P], wqk_scr[bass.ds(h, 1)].rearrange("a p k c -> (a p) k c"))\
                           .then_inc(wq_loaded[u], 16)
                        eng.dma_start(WQ[:, u, :, P:2 * P], wpe[bass.ds(h, 1)].rearrange("a p k c -> (a p) k c"))\
                           .then_inc(wq_loaded[u], 16)

        wslot_free = sem("wslot_free")

        def layernorm_stats(eng, b, k0):
            for t in range(TT):
                eng.bn_stats(STAT[:, t, :], flat(H[:, bass.ds(b * TT + t, 1), :])).then_inc(ln_s, 1)
            eng.wait_ge(ln_s, k0 + b * 2 * TT + TT)
            eng.sem_inc(s_alone, 1)
            for t in range(TT):
                eng.bn_aggr(MV[:, t, :], STAT[:, t:t + 1, :]).then_inc(ln_s, 1)

        def layernorm_rstd(eng, b, k0, p0):
            eng.wait_ge(ln_s, k0 + b * 2 * TT + 2 * TT)
            eng.sem_inc(s_alone, 1)
            eng.tensor_scalar(VEPS[:, :], MV[:, :, 1], 1e-5, 1.0, ALU.add, ALU.mult).then_inc(ln_p, 1)
            eng.wait_ge(ln_p, p0 + b + 1)
            eng.tensor_tensor(RSTD[:, :], VEPS[:, :], NHALF[:, 0:TT], ALU.pow).then_inc(ln_ready, 1)

        def a_pool(eng):
            with eng.Fori(0, NB) as b:
                layernorm_rstd(eng, b, 0, 0)
                eng.wait_ge(ssq_ready, b * 2 * TT + 2 * TT)
                eng.sem_inc(s_alone, 1)
                eng.tensor_scalar(MSQ[:, 0:TT], SSQ[:, 0:TT], 1.0 / LORA, 1e-6, ALU.mult, ALU.add).then_inc(msq_ready, 1)
                eng.tensor_scalar(MSQ[:, TT:], SSQ[:, TT:], 1.0 / QLORA, 1e-6, ALU.mult, ALU.add).then_inc(msq_ready, 1)
                eng.wait_ge(msq_ready, b * 2 + 2)
                eng.tensor_tensor(RMS[:, :], MSQ[:, :], NHALF[:, :], ALU.pow).then_inc(rms_ready, 1)
                with eng.Fori(0, NH // 2) as j:
                    for u in range(2):
                        n = b * NH + j * 2 + u
                        for i in range(TT):
                            eng.wait_ge(rs_ready, n * TT + i + 1)
                            eng.sem_inc(s_alone, 1)
                            eng.tensor_scalar(PR[:, i, 0:(i + 1) * P], PR[:, i, 0:(i + 1) * P], RSUM[:, u, i:i + 1],
                                              1.0, ALU.mult, ALU.mult).then_inc(pn_ready, 1)

        def a_dve(eng):
            eng.memset(ZB[:, :], 0.0).then_inc(zb_ready, 1)
            eng.wait_ge(s_wa, 48)
            eng.tensor_scalar(QNS[:, :], QNW[:, :], SCALE0, None, ALU.mult).then_inc(zb_ready, 1)
            with eng.Fori(0, NB) as b:
                layernorm_stats(eng, b, 0)
                eng.wait_ge(ln_ready, b + 1)
                for t in range(TT):
                    if t >= 2:
                        eng.wait_ge(xt_ps, b * TT + t - 1)
                    eng.tensor_scalar(XN[:, t % 2, :], flat(H[:, bass.ds(b * TT + t, 1), :]), MV[:, t, 0:1],
                                      RSTD[:, t:t + 1], ALU.subtract, ALU.mult).then_inc(xn_ready, 1)
                eng.wait_ge(rms_ready, b + 1)
                for t in range(TT):
                    eng.tensor_scalar(QL[:, t, :], RAW[:, t, 0:QLORA], RMS[:, TT + t:TT + t + 1], None,
                                      ALU.mult).then_inc(kv_ready, 1)
                    eng.tensor_scalar(CN[:, t, :], RAW[:, t, QLORA:QLORA + LORA], RMS[:, t:t + 1], None,
                                      ALU.mult).then_inc(kv_ready, 1)
                    kk = RAW[:, t, QLORA + LORA:QKV0]
                    c0 = C_ROPEK + t * 2 * ROPE
                    if t >= 1:
                        eng.wait_ge(kv_ready, b * 4 * TT + 4 * t)
                    eng.tensor_tensor(KR[:, 0, :], kk, CST[:, c0:c0 + ROPE], ALU.mult).then_inc(kr_done, 1)
                    eng.tensor_tensor(KR[:, 1, 0:32], kk[:, 32:64], CST[:, c0 + ROPE:c0 + ROPE + 32],
                                      ALU.mult).then_inc(kr_done, 1)
                    eng.tensor_tensor(KR[:, 1, 32:64], kk[:, 0:32], CST[:, c0 + ROPE + 32:c0 + 2 * ROPE],
                                      ALU.mult).then_inc(kr_done, 1)
                    eng.wait_ge(kr_done, b * 3 * TT + 3 * t + 3)
                    for r in range(2):
                        eng.tensor_tensor(KP[:, t, r * ROPE:(r + 1) * ROPE], KR[:, 0, :], KR[:, 1, :],
                                          ALU.add).then_inc(kv_ready, 1)
                for t in range(TT):
                    eng.wait_ge(kt_ps, b * 2 * TT + 2 * t + 2)
                    eng.tensor_copy(CT[:, t * P:(t + 1) * P], PS[:, 6 + t % 2, 0:P]).then_inc(kc_ready, 1)
                    eng.tensor_copy(KPT[:, t * P:(t + 1) * P], PS[:, 6 + t % 2, P:2 * P]).then_inc(kc_ready, 1)

                def query_pe(n, u):
                    eng.wait_ge(qp_ps, n + 1)
                    eng.tensor_tensor(QP[:, u, :], PS[:, QB, :], CST[:, C_ROPEQ:C_ROPEQ + S], ALU.mult)\
                       .then_inc(qp_ready, 1)

                def tile_max(n, u, i):
                    eng.wait_ge(s_ps, n * TT + i + 1)
                    eng.tensor_reduce(NMX[:, u, i:i + 1], PS[:, SB + i % 2, 0:(i + 1) * P], AX, ALU.max, negate=True)\
                       .then_inc(max_ready, 1)

                def tile_recip(n, u, i):
                    eng.wait_ge(p_ready, n * TT + i + 1)
                    eng.reciprocal(RSUM[:, u, i:i + 1], SUM[:, u, i:i + 1]).then_inc(rs_ready, 1)

                def tile_pt(n, u, i):
                    eng.wait_ge(pt_ps, n * TT + i + 1)
                    if i == 0:
                        eng.wait_ge(pv_done, n)
                    eng.tensor_copy(PT[:, 0:i + 1, i * P:(i + 1) * P],
                                    PS[:, PTB, 0:(i + 1) * P].rearrange("p (k q) -> p k q", q=P)).then_inc(pt_ready, 1)

                def head(n, u, last):
                    tile_max(n, u, 0)
                    tile_max(n, u, 1)
                    tile_recip(n, u, 0)
                    tile_recip(n, u, 1)
                    tile_max(n, u, 2)
                    tile_recip(n, u, 2)
                    tile_max(n, u, 3)
                    tile_recip(n, u, 3)
                    tile_pt(n, u, 0)
                    tile_pt(n, u, 1)
                    if not last:
                        query_pe(n + 1, 1 - u)
                    tile_pt(n, u, 2)
                    tile_pt(n, u, 3)
                    eng.wait_ge(ot_ps, n + 1)
                    eng.tensor_scalar(OT[:, u, :], PS[:, QB, :], KVW[:, 0:1], None, ALU.mult).then_inc(ot_ready, 1)

                n0 = b * NH
                query_pe(n0, 0)
                with eng.Fori(0, NH // 2 - 1) as j:
                    head(n0 + j * 2, 0, False)
                    head(n0 + j * 2 + 1, 1, False)
                head(n0 + NH - 2, 0, False)
                head(n0 + NH - 1, 1, True)
                for t in range(TT):
                    eng.wait_ge(w_done, b * TT + t + 1)
                    h = flat(H[:, bass.ds(b * TT + t, 1), :])
                    eng.tensor_tensor(h, PS[:, t, :], h, ALU.add).then_inc(res_done, 1)
                eng.wait_ge(res_done, b * TT + TT)

        def a_act(eng):
            eng.wait_ge(s_wa, 48)
            eng.wait_ge(zb_ready, 2)
            with eng.Fori(0, NB) as b:
                for t in range(TT):
                    eng.wait_ge(xt_ps, b * TT + t + 1)
                    if t >= 1:
                        eng.wait_ge(raw_ps, b * TT + t)
                    eng.activation(flat(XNT[:, :, :]), PS[:, 4, :], ACT.Copy).then_inc(xt_ready, 1)
                    eng.wait_ge(raw_ps, b * TT + t + 1)
                    eng.activation(RAW[:, t, 0:QLORA], PS[:, 5, 0:QLORA], ACT.Copy).then_inc(raw_ready, 1)
                    eng.activation(RAW[:, t, QLORA:], PS[:, 6, 0:LORA + ROPE], ACT.Copy).then_inc(raw_ready, 1)
                    eng.wait_ge(raw_ready, b * 2 * TT + 2 * t + 2)
                    eng.activation(SQ[:, 0:LORA], RAW[:, t, QLORA:QLORA + LORA], ACT.Square,
                                   accum_out=SSQ[:, t:t + 1]).then_inc(ssq_ready, 1)
                    eng.wait_ge(ssq_ready, b * 2 * TT + 2 * t + 1)
                    eng.activation(SQ[:, :], RAW[:, t, 0:QLORA], ACT.Square,
                                   accum_out=SSQ[:, TT + t:TT + t + 1]).then_inc(ssq_ready, 1)
                    eng.wait_ge(ssq_ready, b * 2 * TT + 2 * t + 2)
                for t in range(TT):
                    eng.wait_ge(kt_ps, b * 2 * TT + 2 * t + 1)
                    for k in range(QK):
                        ins = eng.activation(QLT[:, k, t * P:(t + 1) * P], PS[:, 4 + t % 2, k * P:(k + 1) * P],
                                             ACT.Copy, scale=QNS[:, k:k + 1])
                    ins.then_inc(kt_ready, 1)

                def query_latent(n, u):
                    eng.wait_ge(qn_ps, n + 1)
                    eng.activation(QN[:, u, :], PS[:, QB, :], ACT.Copy, scale=KVW[:, 0:1]).then_inc(qn_ready, 1)

                def tile_exp(n, u, i):
                    eng.wait_ge(max_ready, n * TT + i + 1)
                    if i == 0:
                        eng.wait_ge(pt_ps, n * TT)
                    eng.activation(PR[:, i, 0:(i + 1) * P], PS[:, SB + i % 2, 0:(i + 1) * P], ACT.Exp,
                                   bias=NMX[:, u, i:i + 1], accum_out=SUM[:, u, i:i + 1]).then_inc(p_ready, 1)

                def head(n, u, last):
                    tile_exp(n, u, 0)
                    tile_exp(n, u, 1)
                    tile_exp(n, u, 2)
                    if not last:
                        query_latent(n + 1, 1 - u)
                    tile_exp(n, u, 3)

                n0 = b * NH
                query_latent(n0, 0)
                with eng.Fori(0, NH // 2 - 1) as j:
                    head(n0 + j * 2, 0, False)
                    head(n0 + j * 2 + 1, 1, False)
                head(n0 + NH - 2, 0, False)
                head(n0 + NH - 1, 1, True)

        def a_pe(eng):
            eng.sem_inc(wslot_free, 2)
            eng.wait_ge(s_wa, 48)
            eng.wait_ge(zb_ready, 1)
            with eng.Fori(0, NB) as b:
                for t in range(TT):
                    n = b * TT + t
                    eng.wait_ge(xn_ready, n + 1)
                    if t >= 1:
                        eng.wait_ge(xt_ready, n)
                    for k in range(KT):
                        mm = eng.transpose(PS[:, 4, k * P:(k + 1) * P], XN[:, t % 2, k * P:(k + 1) * P], ident)
                    mm.then_inc(xt_ps, 1)
                    eng.wait_ge(xt_ready, n + 1)
                    if t >= 1:
                        eng.wait_ge(raw_ready, 2 * n)
                    for k in range(KT):
                        eng.matmul(PS[:, 5, 0:QLORA], XNT[:, k, :], WA[:, k, 0:QLORA], start=(k == 0), stop=(k == KT - 1))
                        mm = eng.matmul(PS[:, 6, 0:LORA + ROPE], XNT[:, k, :], WA[:, k, QLORA:],
                                        start=(k == 0), stop=(k == KT - 1))
                    mm.then_inc(raw_ps, 1)
                eng.wait_ge(raw_ready, b * 2 * TT + 2 * TT)
                for t in range(TT):
                    eng.wait_ge(kv_ready, b * 4 * TT + 4 * t + 4)
                    if t >= 2:
                        eng.wait_ge(kt_ready, b * TT + t - 1)
                        eng.wait_ge(kc_ready, b * 2 * TT + 2 * (t - 1))
                    for k in range(QK):
                        mm = eng.transpose(PS[:, 4 + t % 2, k * P:(k + 1) * P], QL[:, t, k * P:(k + 1) * P], ident)
                    mm.then_inc(kt_ps, 1)
                    eng.transpose(PS[:, 6 + t % 2, 0:P], CN[:, t, :], ident)
                    eng.transpose(PS[:, 6 + t % 2, P:2 * P], KP[:, t, :], ident).then_inc(kt_ps, 1)
                eng.wait_ge(kt_ready, b * TT + TT)
                eng.wait_ge(kc_ready, b * 2 * TT + 2 * TT)

                def query_latent(n, u, j):
                    eng.wait_ge(wq_loaded[u], j * 32 + 32)
                    for k in range(QK):
                        mm = eng.matmul(PS[:, QB, :], WQ[:, u, k, 0:P], QLT[:, k, :], start=(k == 0), stop=(k == QK - 1))
                    mm.then_inc(qn_ps, 1)

                def query_pe(n, u):
                    eng.wait_ge(qn_ready, n + 1)
                    for k in range(QK):
                        mm = eng.matmul(PS[:, QB, :], WQ[:, u, k, P:2 * P], QLT[:, k, :], start=(k == 0), stop=(k == QK - 1))
                    mm.then_inc(qp_ps, 1)
                    eng.wait_ge(qp_ps, n + 1)
                    eng.sem_inc(wslot_free, 1)

                def scores(n, u, i):
                    w = (i + 1) * P
                    if i >= 2:
                        eng.wait_ge(p_ready, n * TT + i - 1)
                    else:
                        eng.wait_ge(p_ready, n * TT)
                        eng.wait_ge(qn_ready, n + 1)
                        eng.wait_ge(qp_ready, n + 1)
                    o = PS[:, SB + i % 2, :]
                    eng.matmul(o[:, 0:w], QN[:, u, i * P:w], CT[:, 0:w], start=True, stop=False)
                    eng.matmul(o[:, 0:w], QP[:, u, i * P:w], KPT[:, 0:w], start=False, stop=False)
                    eng.matmul(o[:, i * P:w], IDB[:, :], MASKB[:, :], start=False, stop=True).then_inc(s_ps, 1)

                def turn(n, u, i):
                    eng.wait_ge(pn_ready, n * TT + i + 1)
                    eng.wait_ge(pt_ready, n * TT + i)
                    for k in range(i + 1):
                        mm = eng.transpose(PS[:, PTB, k * P:(k + 1) * P], PR[:, i, k * P:(k + 1) * P], ident)
                    mm.then_inc(pt_ps, 1)

                def values(n, u, last):
                    eng.wait_ge(pt_ready, n * TT + TT)
                    if not last:
                        eng.wait_ge(qp_ready, n + 2)
                    for k in range(TT):
                        mm = eng.matmul(PS[:, QB, k * P:], CN[:, k, :], PT[:, k, k * P:], start=(k == 0), stop=(k == TT - 1))
                    mm.then_inc(ot_ps, 1)
                    eng.wait_ge(ot_ps, n + 1)
                    eng.sem_inc(pv_done, 1)

                def project(n, u, h, last=False):
                    eng.wait_ge(ot_ready, n + 1)
                    for t in range(TT):
                        mm = eng.matmul(PS[:, t, :], OT[:, u, t * P:(t + 1) * P], flat(WVO[:, bass.ds(h, 1), :]),
                                        start=False, stop=last, skip_group_check=True)
                        if last:
                            mm.then_inc(w_done, 1)

                def head(n, u, j, h, first, last):
                    scores(n, u, 0)
                    scores(n, u, 1)
                    if not first:
                        project(n - 1, 1 - u, h - 1)
                    scores(n, u, 2)
                    if not last:
                        eng.wait_ge(ot_ready, n)
                        query_latent(n + 1, 1 - u, j)
                    scores(n, u, 3)
                    turn(n, u, 0)
                    turn(n, u, 1)
                    if not last:
                        query_pe(n + 1, 1 - u)
                    turn(n, u, 2)
                    turn(n, u, 3)
                    values(n, u, last)

                n0 = b * NH
                j0 = b * (NH // 2)
                eng.wait_ge(res_done, b * TT)
                for t in range(TT):
                    eng.matmul(PS[:, t, :], IDB[:, :], ZB[:, :], start=True, stop=False, skip_group_check=True)
                eng.wait_ge(ot_ready, n0)
                query_latent(n0, 0, j0)
                query_pe(n0, 0)
                head(n0, 0, j0, 0, True, False)
                with eng.Fori(0, NH // 2 - 1) as j:
                    head(n0 + j * 2 + 1, 1, j0 + j + 1, j * 2 + 1, False, False)
                    head(n0 + j * 2 + 2, 0, j0 + j + 1, j * 2 + 2, False, False)
                head(n0 + NH - 1, 1, None, NH - 1, False, True)
                project(n0 + NH - 1, 1, NH - 1, last=True)

        CH = [(0, 512), (512, 512), (1024, 384)]
        IT = INTER // P
        RT1, RT2 = 2 * INTER // P, D // P
        ROWS = (RT1 + RT2) * P
        scale_scr = nc.dram_tensor("scale_scr", [2, ROWS], F32, kind="Internal").ap()
        with Arena() as ar:
            W1Q = sb("W1Q", [P, KT, 2 * INTER], BF16, ar)
            W2Q = sb("W2Q", [P, IT, D], BF16, ar)
            SW = sb("SW", [P, ROWS], F32, ar)
            with Arena() as tmp:
                RW = sb("RW", [P, ROWS], F32, tmp)
                W1T = sb("W1T", [P, 2, 2 * INTER], F32, tmp)
                W2T = sb("W2T", [P, IT, D], F32, tmp)
                WN1 = sb("WN1", [P, 2, D], F32, tmp)
                WN2 = sb("WN2", [P, 2, INTER], F32, tmp)
                AMW = sb("AMW", [P, 2, RT1 + RT2], F32, tmp)
            FXN = sb("FXN", [P, 2, D], F32, ar)
            FXM = sb("FXM", [P, 2, D], F32, ar)
            FXQ = sb("FXQ", [P, 2, D], BF16, ar)
            FXT = sb("FXT", [P, 2, KT, P], BF16, ar)
            FS = sb("FS", [P, 2, 8], F32, ar)
            FST = sb("FST", [P, 2, 8], F32, ar)
            GS = sb("GS", [P, 2, 512], F32, ar)
            GA = sb("GA", [P, 2, 512], F32, ar)
            US = sb("US", [P, 2, 512], F32, ar)
            HM = sb("HM", [P, 2, INTER], F32, ar)
            HR = sb("HR", [P, INTER], F32, ar)
            HQ = sb("HQ", [P, 2, INTER], BF16, ar)
            HT = sb("HT", [P, 2, IT, P], BF16, ar)
            FO = sb("FO", [P, 2, D], F32, ar)

        V_MEAN, V_VAR, V_RSTD, V_SX, V_RX, V_SH, V_RH, V_AM = range(8)
        fw_load = [sem("fw_load0"), sem("fw_load1")]; fw_max = sem("fw_max"); fw_s = sem("fw_s"); fw_scr = sem("fw_scr")
        fw_b = sem("fw_b"); fw_t = [sem("fw_t0"), sem("fw_t1")]; fw_t2 = sem("fw_t2"); fw_q = sem("fw_q"); fw_m = sem("fw_m")
        f_st = sem("f_st"); f_v = sem("f_v"); f_rstd = sem("f_rstd"); f_am = sem("f_am"); f_xm = sem("f_xm"); f_xq = sem("f_xq")
        f_xtp = sem("f_xtp"); f_xt = sem("f_xt"); f_mm = sem("f_mm"); f_g = sem("f_g"); f_ga = sem("f_ga"); f_u = sem("f_u")
        f_hm = sem("f_hm"); f_hr = sem("f_hr"); f_hq = sem("f_hq"); f_htp = sem("f_htp"); f_ht = sem("f_ht")
        f_op = sem("f_op"); f_o = sem("f_o"); f_res = sem("f_res"); f_hs = sem("f_hs"); f_h1 = sem("f_h1"); f_xn = sem("f_xn")

        def fw_tiles():
            return [(0, i) for i in range(RT1)] + [(1, i) for i in range(RT2)]

        def fw_sync(eng):
            w1 = a["w_gate_up"].rearrange("(t p) k -> t p k", p=P)
            with eng.Fori(0, RT1 // 2) as j:
                for u in range(2):
                    eng.wait_ge(fw_free, j * 2 + u + 1)
                    eng.dma_start(WN1[:, u:u + 1, :], w1[bass.ds(j * 2 + u, 1)].rearrange("a p k -> p a k"))\
                       .then_inc(fw_load[u], 16)
            w2 = a["w_down"].rearrange("(t p) k -> t p k", p=P)
            for i in range(RT2):
                if i >= 2:
                    eng.wait_ge(fw_max, RT1 + i - 1)
                eng.dma_start(WN2[:, i % 2, :], w2[i]).then_inc(fw_load2[i % 2], 16)
            eng.dma_start(W2T[:, :, :], a["w_downT"].rearrange("(k p) n -> p k n", p=P)).then_inc(fw_t2, 16)
            w1t = a["w_gate_upT"].rearrange("(k p) n -> k p n", p=P)
            for k in range(KT):
                if k == 2:
                    eng.wait_ge(fw_s, 4)
                    with nc.allow_non_contiguous_dma(reason="one scale a partition"):
                        for i in range(2):
                            eng.dma_start(scale_scr[i].rearrange("(t p) -> p t", p=P), AMW[:, i, :]).then_inc(fw_scr, 16)
                    eng.wait_ge(fw_scr, 32)
                    eng.dma_start(SW[:, :], scale_scr[0:1].to_broadcast([P, ROWS])).then_inc(fw_b, 16)
                    eng.dma_start(RW[:, :], scale_scr[1:2].to_broadcast([P, ROWS])).then_inc(fw_b, 16)
                if k >= 2:
                    eng.wait_ge(fw_q, k - 1)
                eng.dma_start(W1T[:, k % 2, :], w1t[k]).then_inc(fw_t[k % 2], 16)

        fw_free = sem("fw_free"); fw_load2 = [sem("fw_load20"), sem("fw_load21")]

        def fw_dve(eng):
            eng.sem_inc(fw_free, 2)
            with eng.Fori(0, RT1 // 2) as j:
                for u in range(2):
                    eng.wait_ge(fw_load[u], j * 16 + 16)
                    eng.tensor_reduce(AMW[:, 0, bass.ds(j * 2 + u, 1)], WN1[:, u, :], AX, ALU.max,
                                      apply_absolute_value=True).then_inc(fw_max, 1)
                    eng.wait_ge(fw_max, j * 2 + u + 1)
                    eng.sem_inc(fw_free, 1)
            for i in range(RT2):
                eng.wait_ge(fw_load2[i % 2], 16 * (i // 2) + 16)
                eng.tensor_reduce(AMW[:, 0, RT1 + i:RT1 + i + 1], WN2[:, i % 2, :], AX, ALU.max,
                                  apply_absolute_value=True).then_inc(fw_max, 1)
            eng.wait_ge(fw_max, RT1 + RT2)
            eng.tensor_scalar(AMW[:, 0, :], AMW[:, 0, :], 1.0 / 127.0, 1e-8, ALU.mult, ALU.max).then_inc(fw_s, 2)
            eng.wait_ge(fw_s, 2)
            eng.reciprocal(AMW[:, 1, :], AMW[:, 0, :]).then_inc(fw_s, 2)
            eng.wait_ge(fw_b, 32)
            for k in range(KT):
                eng.wait_ge(fw_t[k % 2], 16 * (k // 2) + 16)
                eng.tensor_tensor(W1T[:, k % 2, :], W1T[:, k % 2, :], RW[:, 0:RT1 * P], ALU.mult).then_inc(fw_m, 1)
                eng.wait_ge(fw_m, k + 1)
                eng.tensor_scalar(W1Q[:, k, :], W1T[:, k % 2, :], MAGIC, MAGIC, ALU.add, ALU.subtract).then_inc(fw_q, 1)
            eng.wait_ge(fw_t2, 16)
            eng.tensor_tensor(W2T[:, :, :], W2T[:, :, :], RW[:, RT1 * P:].unsqueeze(1).to_broadcast([P, IT, D]),
                              ALU.mult).then_inc(fw_m, 1)
            eng.wait_ge(fw_m, KT + 1)
            eng.tensor_scalar(W2Q[:, :, :], W2T[:, :, :], MAGIC, MAGIC, ALU.add, ALU.subtract).then_inc(fw_q, 1)
            eng.wait_ge(fw_q, KT + 1)

        def hrow(n):
            return flat(H[:, bass.ds(n, 1), :])

        def two_by_two(eng, first, steady, last):
            first(0, 0)
            with eng.Fori(0, NT // 2 - 1) as j:
                steady(j * 2 + 1, 1)
                steady(j * 2 + 2, 0)
            last(NT - 1, 1)

        def quant_scale(eng, v, src, dst, rdst, base, count):
            pass

        def f_dve(eng):
            def front(n, u):
                eng.bn_stats(FST[:, u, 0:6], hrow(n)).then_inc(f_st, 1)
                eng.wait_ge(f_st, n * 2 + 1)
                eng.sem_inc(s_alone, 1)
                eng.bn_aggr(FS[:, u, V_MEAN:V_VAR + 1], FST[:, u:u + 1, 0:6]).then_inc(f_st, 1)
                eng.wait_ge(f_rstd, n + 1)
                eng.tensor_scalar(FXN[:, u, :], hrow(n), FS[:, u, V_MEAN:V_MEAN + 1], FS[:, u, V_RSTD:V_RSTD + 1],
                                  ALU.subtract, ALU.mult).then_inc(f_xn, 1)
                eng.wait_ge(f_xn, n + 1)
                eng.tensor_reduce(FS[:, u, V_AM:V_AM + 1], FXN[:, u, :], AX, ALU.max, apply_absolute_value=True)\
                   .then_inc(f_am, 1)
                eng.wait_ge(f_am, n * 3 + 1)
                eng.tensor_scalar(FS[:, u, V_SX:V_SX + 1], FS[:, u, V_AM:V_AM + 1], 1.0 / 127.0, 1e-8,
                                  ALU.mult, ALU.max).then_inc(f_am, 1)
                eng.wait_ge(f_am, n * 3 + 2)
                eng.reciprocal(FS[:, u, V_RX:V_RX + 1], FS[:, u, V_SX:V_SX + 1]).then_inc(f_am, 1)
                eng.wait_ge(f_am, n * 3 + 3)
                eng.tensor_scalar(FXM[:, u, :], FXN[:, u, :], FS[:, u, V_RX:V_RX + 1], MAGIC, ALU.mult, ALU.add)\
                   .then_inc(f_xm, 1)
                eng.wait_ge(f_xm, n + 1)
                eng.tensor_scalar(FXQ[:, u, :], FXM[:, u, :], MAGIC, None, ALU.subtract).then_inc(f_xq, 1)

            def mid(n, u):
                for c, (c0, w) in enumerate(CH):
                    eng.wait_ge(f_mm, n * 3 + c + 1)
                    g = (c % 2) * 2
                    k = n * 3 + c
                    eng.wait_ge(f_gfree, k + 1)
                    eng.scalar_tensor_tensor(GS[:, c % 2, 0:w], PS[:, 1 + g, 0:w], FS[:, u, V_SX:V_SX + 1],
                                             SW[:, c0:c0 + w], ALU.mult, ALU.mult).then_inc(f_g, 1)
                    eng.wait_ge(f_ufree, k + 1)
                    eng.scalar_tensor_tensor(US[:, c % 2, 0:w], PS[:, 2 + g, 0:w], FS[:, u, V_SX:V_SX + 1],
                                             SW[:, INTER + c0:INTER + c0 + w], ALU.mult, ALU.mult).then_inc(f_u, 1)

            def back(n, u):
                eng.wait_ge(f_hm, n * 3 + 3)
                eng.tensor_reduce(FS[:, u, V_AM:V_AM + 1], HM[:, u, :], AX, ALU.max, apply_absolute_value=True)\
                   .then_inc(f_hs, 1)
                eng.wait_ge(f_hs, n * 3 + 1)
                eng.tensor_scalar(FS[:, u, V_SH:V_SH + 1], FS[:, u, V_AM:V_AM + 1], 1.0 / 127.0, 1e-8,
                                  ALU.mult, ALU.max).then_inc(f_hs, 1)
                eng.wait_ge(f_hs, n * 3 + 2)
                eng.reciprocal(FS[:, u, V_RH:V_RH + 1], FS[:, u, V_SH:V_SH + 1]).then_inc(f_hs, 1)
                eng.wait_ge(f_hs, n * 3 + 3)
                eng.tensor_scalar(HR[:, :], HM[:, u, :], FS[:, u, V_RH:V_RH + 1], MAGIC, ALU.mult, ALU.add)\
                   .then_inc(f_hr, 1)
                eng.wait_ge(f_hr, n + 1)
                eng.tensor_scalar(HQ[:, u, :], HR[:, :], MAGIC, None, ALU.subtract).then_inc(f_hq, 1)

            def fin(n, u):
                eng.wait_ge(f_op, n + 1)
                eng.scalar_tensor_tensor(FO[:, u, :], PS[:, 7, :], FS[:, u, V_SH:V_SH + 1], SW[:, RT1 * P:],
                                         ALU.mult, ALU.mult).then_inc(f_o, 1)

            front(0, 0)
            two_by_two(eng,
                       lambda n, u: (mid(n, u), front(n + 1, 1 - u), back(n, u)),
                       lambda n, u: (mid(n, u), fin(n - 1, 1 - u), front(n + 1, 1 - u), back(n, u)),
                       lambda n, u: (mid(n, u), fin(n - 1, 1 - u), back(n, u)))
            fin(NT - 1, 1)

        f_gfree = sem("f_gfree"); f_ufree = sem("f_ufree"); f_pv = sem("f_pv")

        def f_pool(eng):
            def rstd(n, u):
                eng.wait_ge(f_st, n * 2 + 2)
                eng.sem_inc(s_alone, 1)
                eng.tensor_scalar(FS[:, u, V_RSTD:V_RSTD + 1], FS[:, u, V_VAR:V_VAR + 1], 1e-5, 1.0, ALU.add, ALU.mult)\
                   .then_inc(f_pv, 1)
                eng.wait_ge(f_pv, n + 1)
                eng.tensor_tensor(FS[:, u, V_RSTD:V_RSTD + 1], FS[:, u, V_RSTD:V_RSTD + 1], NHALF[:, 0:1], ALU.pow)\
                   .then_inc(f_rstd, 1)

            def gate(n, u):
                for c, (c0, w) in enumerate(CH):
                    eng.wait_ge(f_ga, n * 3 + c + 1)
                    eng.wait_ge(f_u, n * 3 + c + 1)
                    eng.tensor_tensor(HM[:, u, c0:c0 + w], GA[:, c % 2, 0:w], US[:, c % 2, 0:w], ALU.mult)\
                       .then_inc(f_hm, 1)
                    eng.wait_ge(f_hm, n * 3 + c + 1)
                    eng.sem_inc(f_ufree, 1)

            def residual(n, u):
                eng.wait_ge(f_o, n + 1)
                eng.tensor_tensor(hrow(n), hrow(n), FO[:, u, :], ALU.add).then_inc(f_res, 1)

            eng.sem_inc(f_ufree, 2)
            rstd(0, 0)
            two_by_two(eng,
                       lambda n, u: (gate(n, u), rstd(n + 1, 1 - u)),
                       lambda n, u: (gate(n, u), rstd(n + 1, 1 - u), residual(n - 1, 1 - u)),
                       lambda n, u: (gate(n, u), residual(n - 1, 1 - u)))
            residual(NT - 1, 1)

        def f_act(eng):
            def xt(n, u):
                eng.wait_ge(f_xtp, n + 1)
                eng.activation(flat(FXT[:, u, :, :]), PS[:, 0, 0:256].bitcast(BF16), ACT.Copy).then_inc(f_xt, 1)

            def silu(n, u):
                for c, (c0, w) in enumerate(CH):
                    eng.wait_ge(f_g, n * 3 + c + 1)
                    eng.wait_ge(f_ufree, n * 3 + c + 1)
                    eng.activation(GA[:, c % 2, 0:w], GS[:, c % 2, 0:w], ACT.Silu).then_inc(f_ga, 1)
                    eng.wait_ge(f_ga, n * 3 + c + 1)
                    eng.sem_inc(f_gfree, 1)

            def ht(n, u):
                eng.wait_ge(f_htp, n + 1)
                eng.activation(flat(HT[:, u, 0:8, :]), PS[:, 5, :].bitcast(BF16), ACT.Copy)
                eng.activation(flat(HT[:, u, 8:IT, :]), PS[:, 6, 0:192].bitcast(BF16), ACT.Copy).then_inc(f_ht, 1)

            eng.sem_inc(f_gfree, 2)
            two_by_two(eng,
                       lambda n, u: (xt(n, u), silu(n, u)),
                       lambda n, u: (xt(n, u), silu(n, u), ht(n - 1, 1 - u)),
                       lambda n, u: (xt(n, u), silu(n, u), ht(n - 1, 1 - u)))
            ht(NT - 1, 1)

        def f_pe(eng):
            def xt(n, u):
                eng.wait_ge(f_xq, n + 1)
                eng.wait_ge(f_xt, n)
                for k in range(KT):
                    mm = eng.transpose(PS[:, 0, k * 64:(k + 1) * 64].bitcast(BF16), FXQ[:, u, k * P:(k + 1) * P], IDB[:, :])
                mm.then_inc(f_xtp, 1)

            def up(n, u):
                eng.wait_ge(f_xt, n + 1)
                for c, (c0, w) in enumerate(CH):
                    if not (isinstance(n, int) and n * 3 + c < 2):
                        eng.wait_ge(f_u, n * 3 + c - 1)
                    g = (c % 2) * 2
                    for k in range(KT):
                        eng.matmul(PS[:, 1 + g, 0:w], FXT[:, u, k, :], W1Q[:, k, c0:c0 + w], start=(k == 0), stop=(k == KT - 1))
                        mm = eng.matmul(PS[:, 2 + g, 0:w], FXT[:, u, k, :], W1Q[:, k, INTER + c0:INTER + c0 + w],
                                        start=(k == 0), stop=(k == KT - 1))
                    mm.then_inc(f_mm, 1)

            def down(n, u):
                eng.wait_ge(f_hq, n + 1)
                eng.wait_ge(f_ht, n)
                for k in range(IT):
                    mm = eng.transpose(PS[:, 5 + k // 8, (k % 8) * 64:(k % 8 + 1) * 64].bitcast(BF16),
                                       HQ[:, u, k * P:(k + 1) * P], IDB[:, :])
                mm.then_inc(f_htp, 1)
                eng.wait_ge(f_ht, n + 1)
                eng.wait_ge(f_o, n)
                for k in range(IT):
                    mm = eng.matmul(PS[:, 7, :], HT[:, u, k, :], W2Q[:, k, :], start=(k == 0), stop=(k == IT - 1))
                mm.then_inc(f_op, 1)

            two_by_two(eng,
                       lambda n, u: (xt(n, u), up(n, u)),
                       lambda n, u: (xt(n, u), up(n, u), down(n - 1, 1 - u)),
                       lambda n, u: (xt(n, u), up(n, u), down(n - 1, 1 - u)))
            down(NT - 1, 1)

        first_sems.close()

        GR = NH // 4
        KVH = NH // 2
        with Arena() as ar:
            WB = sb("WB", [P, KT, 2 * D], F32, ar)
            WO1 = sb("WO1", [P, KT, D], F32, ar)
            BXN = sb("BXN", [P, 2, D], F32, ar)
            BXT = sb("BXT", [P, KT, P], F32, ar)
            RA = sb("RA", [P, 768], F32, ar)
            RB = sb("RB", [P, 768], F32, ar)
            QE = sb("QE", [P, 2, D], F32, ar)
            KE = sb("KE", [P, 2, D], F32, ar)
            VB = sb("VB", [P, TT, KVH, HD + 1], F32, ar)
            QT1 = sb("QT1", [P, GR, S], F32, ar)
            KT1 = sb("KT1", [P, GR, S], F32, ar)
            NM1 = sb("NM1", [P, 2, 2], F32, ar)
            PE1 = sb("PE1", [P, 2, 2, S], F32, ar)
            PT1 = sb("PT1", [P, 2, 2, S], F32, ar)
            RS1 = sb("RS1", [P, 2, 2], F32, ar)
            AO = sb("AO", [P, TT, D], F32, ar)
            AOT = sb("AOT", [P, 2, KT, P], F32, ar)

        b_w = sem("b_w"); b_ones = sem("b_ones"); b_ln = sem("b_ln"); b_lp = sem("b_lp"); b_rstd = sem("b_rstd"); b_xn = sem("b_xn")
        b_xtp = sem("b_xtp"); b_xt = sem("b_xt"); b_pr = sem("b_pr"); b_v = sem("b_v"); b_rot = sem("b_rot"); b_qk = sem("b_qk")
        b_tp = sem("b_tp"); b_qt = sem("b_qt"); b_kt = sem("b_kt"); b_s = sem("b_s"); b_mx = sem("b_mx"); b_e = sem("b_e")
        b_ptp = sem("b_ptp"); b_pt0 = sem("b_pt0"); b_pt1 = sem("b_pt1"); b_o = sem("b_o"); b_rs = sem("b_rs"); b_ao = sem("b_ao")
        b_aop = sem("b_aop"); b_aot = sem("b_aot"); b_out = sem("b_out"); b_res = sem("b_res")
        UN = GR * TT * 2

        def units():
            return [(g, t, jj) for g in range(GR) for t in range(TT) for jj in range(2)]

        def b_sync(eng):
            eng.dma_start(WB[:, :, :], a["wqkv"].rearrange("(k p) n -> p k n", p=P)).then_inc(b_w, 16)
            eng.dma_start(WO1[:, :, :], a["wo1"].rearrange("(k p) n -> p k n", p=P)).then_inc(b_w, 16)

        def b_pool(eng):
            with eng.Fori(0, NB) as b:
                eng.wait_ge(b_ln, b * 2 * TT + 2 * TT)
                eng.sem_inc(s_alone, 1)
                eng.tensor_scalar(VEPS[:, :], MV[:, :, 1], 1e-5, 1.0, ALU.add, ALU.mult).then_inc(b_lp, 1)
                eng.wait_ge(b_lp, b + 1)
                eng.tensor_tensor(RSTD[:, :], VEPS[:, :], NHALF[:, 0:TT], ALU.pow).then_inc(b_rstd, 1)
                for t in range(TT):
                    n = b * TT + t
                    eng.wait_ge(b_rot, n * 4 + 4)
                    if t >= 2:
                        eng.wait_ge(b_tp, n - 1)
                    else:
                        eng.wait_ge(b_tp, n - t)
                    eng.tensor_tensor(QE[:, t % 2, :], RA[:, 0:D], RB[:, 0:D], ALU.add).then_inc(b_qk, 1)
                    for r in range(2):
                        eng.tensor_tensor(KE[:, t % 2, :].rearrange("p (h r d) -> p h r d", r=2, d=HD)[:, :, r, :],
                                          RA[:, D:].rearrange("p (h d) -> p h d", d=HD),
                                          RB[:, D:].rearrange("p (h d) -> p h d", d=HD), ALU.add).then_inc(b_qk, 1)

        def b_dve(eng):
            eng.memset(VB[:, :, :, HD:HD + 1], 1.0).then_inc(b_ones, 1)
            eng.wait_ge(b_w, 32)
            with eng.Fori(0, NB) as b:
                for t in range(TT):
                    eng.bn_stats(STAT[:, t, :], hrow(b * TT + t)).then_inc(b_ln, 1)
                eng.wait_ge(b_ln, b * 2 * TT + TT)
                eng.sem_inc(s_alone, 1)
                for t in range(TT):
                    eng.bn_aggr(MV[:, t, :], STAT[:, t:t + 1, :]).then_inc(b_ln, 1)
                eng.wait_ge(b_rstd, b + 1)

                def norm(t):
                    n = b * TT + t
                    if t >= 2:
                        eng.wait_ge(b_xtp, n - 1)
                    eng.tensor_scalar(BXN[:, t % 2, :], hrow(n), MV[:, t, 0:1], RSTD[:, t:t + 1],
                                      ALU.subtract, ALU.mult).then_inc(b_xn, 1)

                def rotate(t):
                    n = b * TT + t
                    eng.wait_ge(b_pr, n + 1)
                    eng.wait_ge(b_qk, 3 * n)
                    c0 = C_ROPE1 + t * 2 * HD
                    for o, nh, src in ((0, NH, PS[:, 1, :]), (D, KVH, PS[:, 2, 0:D // 2])):
                        cos = CST[:, c0:c0 + HD].unsqueeze(1).to_broadcast([P, nh, HD])
                        eng.tensor_tensor(RA[:, o:o + nh * HD].rearrange("p (h d) -> p h d", d=HD),
                                          src.rearrange("p (h d) -> p h d", d=HD), cos, ALU.mult).then_inc(b_rot, 1)
                        x = src.rearrange("p (h d e) -> p h d e", d=HD // 2, e=2)
                        y = RB[:, o:o + nh * HD].rearrange("p (h d e) -> p h d e", d=HD // 2, e=2)
                        sn = CST[:, c0 + HD:c0 + 2 * HD].rearrange("p (d e) -> p d e", e=2)
                        for e in range(2):
                            ins = eng.tensor_tensor(y[:, :, :, e], x[:, :, :, 1 - e],
                                                    sn[:, :, e].unsqueeze(1).to_broadcast([P, nh, HD // 2]), ALU.mult)
                        ins.then_inc(b_rot, 1)

                norm(0)
                norm(1)
                for t in range(TT):
                    rotate(t)
                    if t + 2 < TT:
                        norm(t + 2)
                    n = b * TT + t
                    eng.wait_ge(b_tp, n + 1)
                    eng.tensor_copy(KT1[:, :, t * P:(t + 1) * P], PS[:, 4, :].rearrange("p (g q) -> p g q", q=P))\
                       .then_inc(b_kt, 1)

                U = units()

                def top(m):
                    k = b * UN + m
                    eng.wait_ge(b_s, k + 1)
                    eng.wait_ge(b_e, 2 * k - 2) if m >= 2 else None
                    eng.tensor_reduce(NM1[:, m % 2, :], PS[:, 2 * (m % 2):2 * (m % 2) + 2, :], AX, ALU.max, negate=True)\
                       .then_inc(b_mx, 1)

                def turned(m):
                    eng.wait_ge(b_ptp, b * UN + m + 1)
                    eng.tensor_copy(PT1[:, m % 2, 0, :], PS[:, 4, :]).then_inc(b_pt0, 1)

                def norm_out(m):
                    g, t, jj = U[m]
                    k = b * UN + m
                    eng.wait_ge(b_o, k + 1)
                    o = PS[:, 6 + m % 2, 0:2 * (HD + 1)].rearrange("p (r d) -> p r d", d=HD + 1)
                    eng.reciprocal(RS1[:, m % 2, :], o[:, :, HD]).then_inc(b_rs, 1)
                    eng.wait_ge(b_rs, k + 1)
                    c = (4 * g + 2 * jj) * HD
                    eng.tensor_tensor(AO[:, t, c:c + 2 * HD].rearrange("p (r d) -> p r d", d=HD), o[:, :, 0:HD],
                                      RS1[:, m % 2, :].unsqueeze(2).to_broadcast([P, 2, HD]), ALU.mult).then_inc(b_ao, 1)

                top(0)
                for m in range(UN):
                    if m + 1 < UN:
                        top(m + 1)
                    turned(m)
                    if m >= 1:
                        norm_out(m - 1)
                norm_out(UN - 1)
                for t in range(TT):
                    n = b * TT + t
                    eng.wait_ge(b_out, n + 1)
                    eng.tensor_tensor(hrow(n), PS[:, 2 + t % 2, :], hrow(n), ALU.add).then_inc(b_res, 1)
                eng.wait_ge(b_res, b * TT + TT)

        def b_act(eng):
            with eng.Fori(0, NB) as b:
                for t in range(TT):
                    n = b * TT + t
                    eng.wait_ge(b_xtp, n + 1)
                    if t >= 1:
                        eng.wait_ge(b_pr, n)
                    eng.activation(flat(BXT[:, :, :]), PS[:, 0, :], ACT.Copy).then_inc(b_xt, 1)
                    eng.wait_ge(b_pr, n + 1)
                    eng.wait_ge(b_rot, n * 4 + 4)
                    eng.activation(VB[:, t, :, 0:HD], PS[:, 2, D // 2:].rearrange("p (h d) -> p h d", d=HD), ACT.Copy)\
                       .then_inc(b_v, 1)
                    eng.wait_ge(b_tp, n + 1)
                    eng.activation(QT1[:, :, t * P:(t + 1) * P], PS[:, 3, :].rearrange("p (g q) -> p g q", q=P), ACT.Copy,
                                   scale=SCALE1).then_inc(b_qt, 1)

                def exps(m):
                    k = b * UN + m
                    eng.wait_ge(b_mx, k + 1)
                    if m >= 2:
                        eng.wait_ge(b_ptp, k - 1)
                    else:
                        eng.wait_ge(b_ptp, k - m)
                    for r in range(2):
                        eng.activation(PE1[:, m % 2, r, :], PS[:, 2 * (m % 2) + r, :], ACT.Exp,
                                       bias=NM1[:, m % 2, r:r + 1]).then_inc(b_e, 1)

                def turned(m):
                    eng.wait_ge(b_ptp, b * UN + m + 1)
                    eng.activation(PT1[:, m % 2, 1, :], PS[:, 5, :], ACT.Copy).then_inc(b_pt1, 1)

                exps(0)
                for m in range(UN):
                    if m + 1 < UN:
                        exps(m + 1)
                    turned(m)
                for t in range(TT):
                    n = b * TT + t
                    eng.wait_ge(b_aop, n + 1)
                    eng.activation(flat(AOT[:, t % 2, :, :]), PS[:, t % 2, :], ACT.Copy).then_inc(b_aot, 1)

        def b_pe(eng):
            eng.wait_ge(b_w, 32)
            eng.wait_ge(b_ones, 1)
            with eng.Fori(0, NB) as b:
                eng.wait_ge(b_res, b * TT)
                for t in range(TT):
                    n = b * TT + t
                    eng.wait_ge(b_xn, n + 1)
                    eng.wait_ge(b_xt, n)
                    for k in range(KT):
                        mm = eng.transpose(PS[:, 0, k * P:(k + 1) * P], BXN[:, t % 2, k * P:(k + 1) * P], ident)
                    mm.then_inc(b_xtp, 1)
                    eng.wait_ge(b_xt, n + 1)
                    eng.wait_ge(b_v, n)
                    for k in range(KT):
                        eng.matmul(PS[:, 1, :], BXT[:, k, :], WB[:, k, 0:D], start=(k == 0), stop=(k == KT - 1))
                        mm = eng.matmul(PS[:, 2, :], BXT[:, k, :], WB[:, k, D:], start=(k == 0), stop=(k == KT - 1))
                    mm.then_inc(b_pr, 1)
                    eng.wait_ge(b_qk, 3 * n + 3)
                    eng.wait_ge(b_qt, n)
                    eng.wait_ge(b_kt, n)
                    for k in range(GR):
                        eng.transpose(PS[:, 3, k * P:(k + 1) * P], QE[:, t % 2, k * P:(k + 1) * P], ident)
                        mm = eng.transpose(PS[:, 4, k * P:(k + 1) * P], KE[:, t % 2, k * P:(k + 1) * P], ident)
                    mm.then_inc(b_tp, 1)
                eng.wait_ge(b_qt, b * TT + TT)
                eng.wait_ge(b_kt, b * TT + TT)
                eng.wait_ge(b_v, b * TT + TT)
                U = units()

                def scores(m):
                    g, t, jj = U[m]
                    k = b * UN + m
                    if m >= 2:
                        eng.wait_ge(b_e, 2 * k - 2)
                    for r in range(2):
                        p = 32 * (2 * jj + r)
                        mm = eng.matmul(PS[:, 2 * (m % 2) + r, :], QT1[p:p + 32, g, t * P:(t + 1) * P],
                                        KT1[p:p + 32, g, :], start=True, stop=True)
                    mm.then_inc(b_s, 1)

                def turn(m):
                    k = b * UN + m
                    eng.wait_ge(b_e, 2 * k + 2)
                    eng.wait_ge(b_pt0, k)
                    eng.wait_ge(b_pt1, k)
                    for r in range(2):
                        for c in range(TT):
                            mm = eng.transpose(PS[:, 4 + r, c * P:(c + 1) * P], PE1[:, m % 2, r, c * P:(c + 1) * P], ident)
                    mm.then_inc(b_ptp, 1)

                def values(m):
                    g, t, jj = U[m]
                    k = b * UN + m
                    eng.wait_ge(b_pt0, k + 1)
                    eng.wait_ge(b_pt1, k + 1)
                    if m >= 2:
                        eng.wait_ge(b_ao, k - 1)
                    for r in range(2):
                        for c in range(TT):
                            mm = eng.matmul(PS[:, 6 + m % 2, r * (HD + 1):(r + 1) * (HD + 1)],
                                            PT1[:, m % 2, r, c * P:(c + 1) * P], VB[:, c, 2 * g + jj, :],
                                            start=(c == 0), stop=(c == TT - 1))
                    mm.then_inc(b_o, 1)

                scores(0)
                for m in range(UN):
                    if m + 1 < UN:
                        scores(m + 1)
                    turn(m)
                    if m >= 1:
                        values(m - 1)
                values(UN - 1)
                eng.wait_ge(b_ao, b * UN + UN)
                for t in range(TT):
                    n = b * TT + t
                    if t >= 2:
                        eng.wait_ge(b_aot, n - 1)
                    for k in range(KT):
                        mm = eng.transpose(PS[:, t % 2, k * P:(k + 1) * P], AO[:, t, k * P:(k + 1) * P], ident)
                    mm.then_inc(b_aop, 1)
                    eng.wait_ge(b_aot, n + 1)
                    if t >= 2:
                        eng.wait_ge(b_res, n - 1)
                    for k in range(KT):
                        mm = eng.matmul(PS[:, 2 + t % 2, :], AOT[:, t % 2, k, :], WO1[:, k, :], start=(k == 0), stop=(k == KT - 1))
                    mm.then_inc(b_out, 1)

        FK = FF // P
        with Arena() as ar:
            CFQ = sb("CFQ", [P, KT, FF], F32R, ar)
            CPQ = sb("CPQ", [P, FK, D], BF16, ar)
            ONES = sb("ONES", [P, P], F32, ar)
            ABS = sb("ABS", [P, 2], F32, ar)
            WSC = sb("WSC", [P, 4], F32, ar)
            with Arena() as tmp:
                CF = sb("CF", [P, KT * FF], F32, tmp)
                CP = sb("CP", [P, FK * D], F32, tmp)
            GXN = sb("GXN", [P, 2, D], F32, ar)
            GXH = sb("GXH", [P, 2, D], F32R, ar)
            GXL = sb("GXL", [P, 2, D], F32R, ar)
            GV = sb("GV", [P, 2, 8], F32, ar)
            GST = sb("GST", [P, 2, 8], F32, ar)
            GR1 = sb("GR1", [P, 2, FF], F32, ar)
            GY = sb("GY", [P, FF], F32, ar)
            GQ = sb("GQ", [P, 2, FF], BF16, ar)
            GT = sb("GT", [P, 2, FK, P], BF16, ar)

        g_w = sem("g_w"); g_abs = sem("g_abs"); g_sum = sem("g_sum"); g_sc = sem("g_sc"); g_t = sem("g_t"); g_one = sem("g_one")
        g_st = sem("g_st"); g_pv = sem("g_pv"); g_rstd = sem("g_rstd"); g_xn = sem("g_xn"); g_xtp = sem("g_xtp"); g_hi = sem("g_hi")
        g_lo = sem("g_lo"); g_mm = sem("g_mm"); g_r = sem("g_r"); g_mx = sem("g_mx"); g_c = sem("g_c"); g_y = sem("g_y"); g_q = sem("g_q")
        g_tp = sem("g_tp"); g_ta = sem("g_ta"); g_tb = sem("g_tb"); g_op = sem("g_op"); g_res = sem("g_res"); g_p1 = sem("g_p1")
        G_C, G_ST = 4, 5

        def gw_sync(eng):
            eng.dma_start(CF[:, :].rearrange("p (k n) -> p k n", k=KT), a["c_fc"].rearrange("(k p) n -> p k n", p=P))\
               .then_inc(g_w, 16)
            eng.dma_start(CP[:, :].rearrange("p (k n) -> p k n", k=FK), a["c_projT"].rearrange("(k p) n -> p k n", p=P))\
               .then_inc(g_w, 16)

        def gw_dve(eng):
            eng.memset(ONES[:, :], 1.0).then_inc(g_one, 1)
            eng.wait_ge(g_w, 32)
            for i, w in enumerate((CF, CP)):
                eng.tensor_reduce(ABS[:, i:i + 1], w[:, :], AX, ALU.add, apply_absolute_value=True).then_inc(g_abs, 1)
            eng.wait_ge(g_sum, 1)
            eng.tensor_scalar(WSC[:, 0:2], PS[:, 0, 0:2], 1.0 / (D * FF), 1e-5, ALU.mult, ALU.max).then_inc(g_sc, 1)
            eng.wait_ge(g_sc, 1)
            eng.reciprocal(WSC[:, 2:4], WSC[:, 0:2]).then_inc(g_sc, 1)
            eng.wait_ge(g_sc, 2)
            for i, (w, q) in enumerate(((CF, flat(CFQ[:, :, :])), (CP, flat(CPQ[:, :, :])))):
                eng.tensor_scalar(w[:, :], w[:, :], WSC[:, 2 + i:3 + i], MAGIC, ALU.mult, ALU.add).then_inc(g_t, 1)
                eng.wait_ge(g_t, 3 * i + 1)
                eng.tensor_scalar(w[:, :], w[:, :], MAGIC, -1.0, ALU.subtract, ALU.max).then_inc(g_t, 1)
                eng.wait_ge(g_t, 3 * i + 2)
                eng.tensor_scalar(q, w[:, :], 1.0, None, ALU.min).then_inc(g_t, 1)
            eng.wait_ge(g_t, 6)

        def gw_pe(eng):
            eng.wait_ge(g_abs, 2)
            eng.wait_ge(g_one, 1)
            eng.matmul(PS[:, 0, 0:2], ONES[:, :], ABS[:, :], start=True, stop=True).then_inc(g_sum, 1)

        def g_dve(eng):
            def front(n, u):
                eng.bn_stats(GST[:, u, 0:6], hrow(n)).then_inc(g_st, 1)
                eng.wait_ge(g_st, n * 2 + 1)
                eng.sem_inc(s_alone, 1)
                eng.bn_aggr(GV[:, u, V_MEAN:V_VAR + 1], GST[:, u:u + 1, 0:6]).then_inc(g_st, 1)
                eng.wait_ge(g_rstd, n + 1)
                eng.tensor_scalar(GXN[:, u, :], hrow(n), GV[:, u, V_MEAN:V_MEAN + 1], GV[:, u, V_RSTD:V_RSTD + 1],
                                  ALU.subtract, ALU.mult).then_inc(g_xn, 1)

            def low(n, u):
                eng.wait_ge(g_hi, n + 1)
                eng.tensor_tensor(GXL[:, u, :], PS[:, 0, :], GXH[:, u, :].bitcast(F32), ALU.subtract).then_inc(g_lo, 1)

            def peak(n, u):
                eng.wait_ge(g_r, 4 * n + 4)
                eng.tensor_reduce(GV[:, u, V_AM:V_AM + 1], GR1[:, u, :], AX, ALU.max).then_inc(g_mx, 1)

            def rounded(n, u):
                eng.wait_ge(g_y, n + 1)
                eng.tensor_scalar(GQ[:, u, :], GY[:, :], MAGIC, MAGIC, ALU.add, ALU.subtract).then_inc(g_q, 1)

            def turned(n, u):
                eng.wait_ge(g_tp, n + 1)
                eng.tensor_copy(flat(GT[:, u, 0:8, :]), PS[:, 5, :].bitcast(BF16)).then_inc(g_ta, 1)

            def fin(n, u):
                eng.wait_ge(g_op, n + 1)
                eng.scalar_tensor_tensor(hrow(n), PS[:, 7, :], GV[:, u, G_ST:G_ST + 1], hrow(n), ALU.mult, ALU.add)\
                   .then_inc(g_res, 1)

            front(0, 0)
            low(0, 0)
            two_by_two(eng,
                       lambda n, u: (front(n + 1, 1 - u), peak(n, u), low(n + 1, 1 - u), rounded(n, u)),
                       lambda n, u: (front(n + 1, 1 - u), turned(n - 1, 1 - u), peak(n, u), low(n + 1, 1 - u),
                                     fin(n - 1, 1 - u), rounded(n, u)),
                       lambda n, u: (turned(n - 1, 1 - u), peak(n, u), fin(n - 1, 1 - u), rounded(n, u)))
            turned(NT - 1, 1)
            fin(NT - 1, 1)

        def g_pool(eng):
            def rstd(n, u):
                eng.wait_ge(g_st, n * 2 + 2)
                eng.sem_inc(s_alone, 1)
                eng.tensor_scalar(GV[:, u, V_RSTD:V_RSTD + 1], GV[:, u, V_VAR:V_VAR + 1], 1e-5, 1.0, ALU.add, ALU.mult)\
                   .then_inc(g_pv, 1)
                eng.wait_ge(g_pv, n + 1)
                eng.tensor_tensor(GV[:, u, V_RSTD:V_RSTD + 1], GV[:, u, V_RSTD:V_RSTD + 1], NHALF[:, 0:1], ALU.pow)\
                   .then_inc(g_rstd, 1)

            def token_scales(n, u):
                v = GV[:, u, :]
                eng.wait_ge(g_mx, n + 1)
                eng.tensor_tensor(v[:, V_AM:V_AM + 1], v[:, V_AM:V_AM + 1], v[:, V_AM:V_AM + 1], ALU.mult).then_inc(g_p1, 1)
                eng.wait_ge(g_p1, n * 4 + 1)
                eng.sem_inc(s_alone, 1)
                eng.tensor_scalar(v[:, V_AM:V_AM + 1], v[:, V_AM:V_AM + 1], 1e-5, None, ALU.max).then_inc(g_p1, 1)
                eng.wait_ge(g_p1, n * 4 + 2)
                eng.sem_inc(s_alone, 1)
                eng.tensor_scalar(v[:, V_AM:V_AM + 1], v[:, V_AM:V_AM + 1], 1.0 / 255.0, 1.0, ALU.mult, ALU.mult)\
                   .then_inc(g_p1, 1)
                eng.wait_ge(g_p1, n * 4 + 3)
                eng.tensor_tensor(v[:, G_ST:G_ST + 1], v[:, V_AM:V_AM + 1], WSC[:, 1:2], ALU.mult).then_inc(g_p1, 1)
                eng.tensor_tensor(v[:, G_C:G_C + 1], v[:, V_AM:V_AM + 1], NHALF[:, 0:1], ALU.pow).then_inc(g_c, 1)

            rstd(0, 0)
            two_by_two(eng,
                       lambda n, u: (rstd(n + 1, 1 - u), token_scales(n, u)),
                       lambda n, u: (rstd(n + 1, 1 - u), token_scales(n, u)),
                       lambda n, u: (token_scales(n, u),))

        def g_act(eng):
            def high(n, u):
                eng.wait_ge(g_xtp, n + 1)
                eng.activation(GXH[:, u, :], PS[:, 0, :], ACT.Copy).then_inc(g_hi, 1)

            def relu(n, u):
                for c in range(4):
                    eng.wait_ge(g_mm, 4 * n + c + 1)
                    eng.activation(GR1[:, u, c * 512:(c + 1) * 512], PS[:, 1 + c, :], ACT.Relu, scale=WSC[:, 0:1])\
                       .then_inc(g_r, 1)

            def squared(n, u):
                eng.wait_ge(g_c, n + 1)
                eng.wait_ge(g_q, n)
                eng.activation(GY[:, :], GR1[:, u, :], ACT.Square, scale=GV[:, u, G_C:G_C + 1]).then_inc(g_y, 1)

            def turned(n, u):
                eng.wait_ge(g_tp, n + 1)
                eng.activation(flat(GT[:, u, 8:16, :]), PS[:, 6, :].bitcast(BF16), ACT.Copy).then_inc(g_tb, 1)

            high(0, 0)
            two_by_two(eng,
                       lambda n, u: (relu(n, u), high(n + 1, 1 - u), squared(n, u)),
                       lambda n, u: (relu(n, u), turned(n - 1, 1 - u), high(n + 1, 1 - u), squared(n, u)),
                       lambda n, u: (relu(n, u), turned(n - 1, 1 - u), squared(n, u)))
            turned(NT - 1, 1)

        def g_pe(eng):
            def xt(n, u):
                eng.wait_ge(g_xn, n + 1)
                eng.wait_ge(g_lo, n)
                for k in range(KT):
                    mm = eng.transpose(PS[:, 0, k * P:(k + 1) * P], GXN[:, u, k * P:(k + 1) * P], ident)
                mm.then_inc(g_xtp, 1)

            def up(n, u):
                eng.wait_ge(g_lo, n + 1)
                for c in range(4):
                    if not (isinstance(n, int) and n == 0):
                        eng.wait_ge(g_r, 4 * n - 3 + c)
                    for k in range(KT):
                        for x in (GXH, GXL):
                            mm = eng.matmul(PS[:, 1 + c, :], x[:, u, k * P:(k + 1) * P], CFQ[:, k, c * 512:(c + 1) * 512],
                                            start=(k == 0 and x is GXH), stop=(k == KT - 1 and x is GXL))
                    mm.then_inc(g_mm, 1)

            def down(n, u):
                eng.wait_ge(g_q, n + 1)
                eng.wait_ge(g_ta, n)
                eng.wait_ge(g_tb, n)
                for k in range(FK):
                    mm = eng.transpose(PS[:, 5 + k // 8, (k % 8) * 64:(k % 8 + 1) * 64].bitcast(BF16),
                                       GQ[:, u, k * P:(k + 1) * P], IDB[:, :])
                mm.then_inc(g_tp, 1)

            def proj(n, u):
                eng.wait_ge(g_ta, n + 1)
                eng.wait_ge(g_tb, n + 1)
                eng.wait_ge(g_res, n)
                for k in range(FK):
                    mm = eng.matmul(PS[:, 7, :], GT[:, u, k, :], CPQ[:, k, :], start=(k == 0), stop=(k == FK - 1))
                mm.then_inc(g_op, 1)

            eng.wait_ge(g_t, 6)
            xt(0, 0)
            two_by_two(eng,
                       lambda n, u: (up(n, u), xt(n + 1, 1 - u)),
                       lambda n, u: (down(n - 1, 1 - u), up(n, u), xt(n + 1, 1 - u), proj(n - 1, 1 - u)),
                       lambda n, u: (down(n - 1, 1 - u), up(n, u), proj(n - 1, 1 - u)))
            down(NT - 1, 1)
            proj(NT - 1, 1)

        block = ctx.enter_context(nc.Block())

        @block.sync
        def _(eng):
            sync_eng[0] = eng
            e_sync(eng)
            w_sync(eng)
            barrier(eng, clears=True)
            a_sync(eng)
            barrier(eng)
            if "F" in stages:
                fw_sync(eng)
                barrier(eng)
                barrier(eng)
            if "B" in stages:
                b_sync(eng)
                barrier(eng)
            if "G" in stages:
                gw_sync(eng)
                barrier(eng)
                barrier(eng)
            eng.dma_start(out.rearrange("b (t p) n -> p (b t) n", p=P), H[:, :, :]).then_inc(s_ids, 16)
            eng.wait_ge(s_ids, 48)

        @block.gpsimd
        def _(eng):
            e_pool(eng)
            barrier(eng)
            a_pool(eng)
            barrier(eng)
            if "F" in stages:
                barrier(eng)
                f_pool(eng)
                barrier(eng)
            if "B" in stages:
                b_pool(eng)
                barrier(eng)
            if "G" in stages:
                barrier(eng)
                g_pool(eng)
                barrier(eng)

        @block.scalar
        def _(eng):
            e_act(eng)
            w_act(eng)
            barrier(eng)
            a_act(eng)
            barrier(eng)
            if "F" in stages:
                barrier(eng)
                f_act(eng)
                barrier(eng)
            if "B" in stages:
                b_act(eng)
                barrier(eng)
            if "G" in stages:
                barrier(eng)
                g_act(eng)
                barrier(eng)

        @block.vector
        def _(eng):
            e_dve(eng)
            w_dve(eng)
            barrier(eng)
            a_dve(eng)
            barrier(eng)
            if "F" in stages:
                fw_dve(eng)
                barrier(eng)
                f_dve(eng)
                barrier(eng)
            if "B" in stages:
                b_dve(eng)
                barrier(eng)
            if "G" in stages:
                gw_dve(eng)
                barrier(eng)
                g_dve(eng)
                barrier(eng)

        @block.tensor
        def _(eng):
            e_pe(eng)
            w_pe(eng)
            barrier(eng)
            a_pe(eng)
            barrier(eng)
            if "F" in stages:
                barrier(eng)
                f_pe(eng)
                barrier(eng)
            if "B" in stages:
                b_pe(eng)
                barrier(eng)
            if "G" in stages:
                gw_pe(eng)
                barrier(eng)
                g_pe(eng)
                barrier(eng)


NAMES = {"L0_tok_ts_w": "ts_w", "L0_tok_pos_w": "pos_w", "L0_attn_q_norm_w": "q_norm_w", "L0_attn_wq_b": "wq_b",
         "L0_attn_kv_norm_w": "kv_norm_w", "L0_attn_wkv_b": "wkv_b",
         "L0_ffn_w_gate_up": "w_gate_up", "L0_ffn_w_down": "w_down", "L1_attn_wo": "wo1", "L1_ffn_c_fc": "c_fc"}


def layouts(inputs):
    g = {v: np.ascontiguousarray(inputs[k]) for k, v in NAMES.items()}
    x = np.asarray(inputs["x"])
    g["x"] = np.ascontiguousarray(x)
    nxt = np.concatenate([x[:, 1:], x[:, -1:]], 1).reshape(NT * 4, 32).T
    g["ext"] = np.ascontiguousarray(np.concatenate([nxt] * 4, 0))
    g["woT"] = np.ascontiguousarray(np.asarray(inputs["L0_attn_wo"]).T)
    g["waT"] = np.ascontiguousarray(np.concatenate([inputs["L0_attn_wq_a"], inputs["L0_attn_wkv_a"]], 0).T)
    wpe = np.asarray(inputs["L0_attn_wq_b"]).reshape(NH, LORA + ROPE, QLORA)[:, LORA:].transpose(0, 2, 1)
    g["wpe"] = np.ascontiguousarray(np.concatenate([wpe, wpe[:, :, ROPE // 2:], wpe[:, :, :ROPE // 2]], 2))
    g["w_gate_upT"] = np.ascontiguousarray(np.asarray(inputs["L0_ffn_w_gate_up"]).T)
    g["w_downT"] = np.ascontiguousarray(np.asarray(inputs["L0_ffn_w_down"]).T)
    g["wqkv"] = np.ascontiguousarray(np.concatenate([inputs["L1_attn_wq"], inputs["L1_attn_wk"], inputs["L1_attn_wv"]], 1))
    g["c_projT"] = np.ascontiguousarray(np.asarray(inputs["L1_ffn_c_proj"]).T)
    g["consts"] = constants()
    return g


def kernel(**inputs):
    import concourse.bacc as bacc
    from concourse.bass_utils import run_bass_kernel_spmd

    nc = bacc.Bacc("TRN2", target_bir_lowering=False, num_devices=1)
    arrays, aps = {}, {}
    for name, v in layouts(inputs).items():
        arrays["in_" + name] = v
        aps[name] = nc.dram_tensor("in_" + name, v.shape, mybir.dt.from_np(v.dtype), kind="ExternalInput").ap()
    out = nc.dram_tensor("out_0", (NB, S, D), F32, kind="ExternalOutput").ap()
    tower_kernel(nc, aps, out)
    r = run_bass_kernel_spmd(nc, [arrays], core_ids=[0])
    return r.results[0]["out_0"]
```

```python
from contextlib import ExitStack

import numpy as np
import concourse.bass as bass
from concourse import mybir

F32 = mybir.dt.float32
F32R = mybir.dt.float32r
BF16 = mybir.dt.bfloat16
I32 = mybir.dt.int32
ALU = mybir.AluOpType
ACT = mybir.ActivationFunctionType
AX = mybir.AxisListType.X

P = 128
NB = 4
S = 512
D = 512
TT = S // P
NT = NB * TT
KT = D // P
NH = 16
LORA = 128
QLORA = 384
QK = QLORA // P
ROPE = 64
QKV0 = QLORA + LORA + ROPE
SCALE0 = float(LORA + ROPE) ** -0.5
INTER = 1408
FF = 2048
HD = 32
SCALE1 = float(HD) ** -0.5
BUCKETS = 32
BPP = 4
PASSES = BUCKETS // BPP
MAGIC = 12582912.0

C_ID, C_MASK, C_ROPEQ, C_ROPEK, C_RQ1, C_RK1, C_ID32, C_GRP, C_FLIP, C_N = 0, 128, 256, 768, 1280, 1536, 1792, 1824, 1825, 1953


def constants():
    c = np.zeros((P, C_N), np.float32)
    r = np.arange(P)
    c[:, C_ID:C_ID + P] = np.eye(P)
    c[:, C_MASK:C_MASK + P] = np.where(r[None, :] <= r[:, None], 0.0, -1e30)
    pos = np.arange(S, dtype=np.float32)
    inv = (1.0 / 10000.0 ** (np.arange(0, ROPE, 2, dtype=np.float32) / ROPE)).astype(np.float32)
    ang = (pos[:, None] * inv[None, :]).astype(np.float32)
    cos, sin = np.cos(ang), np.sin(ang)
    c[:, C_ROPEQ:C_ROPEQ + S] = np.concatenate([cos, cos, -sin, sin], 1).T
    k = np.concatenate([cos, cos, -sin, sin], 1).reshape(TT, P, 2 * ROPE)
    c[:, C_ROPEK:C_ROPEK + TT * 2 * ROPE] = k.transpose(1, 0, 2).reshape(P, -1)
    inv = (1.0 / 10000.0 ** (np.arange(0, HD, 2, dtype=np.float32) / HD)).astype(np.float32)
    ang = (pos[:, None] * inv[None, :]).astype(np.float32)
    cos, sin = np.cos(ang), np.sin(ang)
    t = np.concatenate([np.repeat(cos, 2, 1), np.stack([-sin, sin], -1).reshape(S, HD)], 1)
    t = t.reshape(TT, P, 2 * HD).transpose(1, 0, 2).reshape(P, -1)
    c[:, C_RK1:C_RK1 + TT * 2 * HD] = t
    c[:, C_RQ1:C_RQ1 + TT * 2 * HD] = t * SCALE1
    c[:, C_ID32:C_ID32 + 32] = (r[:, None] % 32 == np.arange(32)[None, :])
    c[:, C_GRP] = r // 32
    c[:, C_FLIP:C_FLIP + P] = np.eye(P)[::-1]
    return c


def tower_kernel(nc, a, out, stages="FBG"):
    ctx = ExitStack()
    with ctx:
        def sb(name, shape, dt=F32, c=ctx):
            return c.enter_context(nc.sbuf_tensor(name, shape, dt))

        first = []

        first_sems = ExitStack()

        def sem(name, c=ctx):
            return c.enter_context(nc.semaphore(name))

        def sem1(name):
            first.append(sem(name, first_sems))
            return first[-1]

        PS = ctx.enter_context(nc.psum_tensor("PS", [P, 8, 512], F32))
        H = sb("H", [P, NT, D])
        CST = sb("CST", [P, C_N])
        IDB = sb("IDB", [P, P], BF16)
        MASKB = sb("MASKB", [P, P], BF16)
        STAT = sb("STAT", [P, TT, 6])
        MV = sb("MV", [P, TT, 2])
        RSTD = sb("RSTD", [P, TT])
        VEPS = sb("VEPS", [P, TT])
        NHALF = sb("NHALF", [P, 2 * TT])
        ident = CST[:, C_ID:C_ID + P]

        QNS = sb("QNS", [P, QK], F32)

        s_const = sem("s_const")
        s_bar = sem("s_bar")
        s_open = sem("s_open")
        s_alone = sem("s_alone")
        s_pre = sem("s_pre")

        def flat(ap):
            return ap.rearrange("p a n -> p (a n)")

        bars, sync_eng = {}, [None]

        def barrier(eng, clears=False):
            k = bars.get(id(eng), 0) + 1
            bars[id(eng)] = k
            eng.drain().then_inc(s_bar, 1)
            if eng is sync_eng[0]:
                eng.wait_ge(s_bar, 5 * k)
                if clears:
                    for x in first:
                        eng.sem_clear(x)
                eng.sem_inc(s_open, 1)
            eng.wait_ge(s_open, k)

        wqk_scr = nc.dram_tensor("wqk_scr", [NH, P, QK, LORA], F32, kind="Internal").ap()

        class Arena:
            def __enter__(self):
                self.c = ExitStack()
                return self.c

            def __exit__(self, *x):
                self.c.close()

        arena_w = ExitStack()
        WVO = sb("WVO", [P, NH, D], c=arena_w)
        with Arena() as ar:
            XB = sb("XB", [P, NB, S], I32, ar)
            EXT = sb("EXT", [P, NT * 4], I32, ar)
            DIFF = sb("DIFF", [P, 2, 4 * S], I32, ar)
            MAG = sb("MAG", [P, 2, 4 * S], F32, ar)
            EXPO = sb("EXPO", [P, 2, 4 * S], I32, ar)
            EXB = sb("EXB", [P, 2, 4 * S], BF16, ar)
            MSK = sb("MSK", [P, 8, 4 * S], BF16, ar)
            POSB = sb("POSB", [P, TT, S], F32, ar)
            POSF = sb("POSF", [P, TT, S], F32, ar)
            TSC = sb("TSC", [P, PASSES], F32, ar)
            TSH = sb("TSH", [P, 3, PASSES], BF16, ar)
            TSF = sb("TSF", [P, 3, PASSES], F32, ar)
            TSR = sb("TSR", [P, 2, PASSES], F32, ar)
            TAB = sb("TAB", [P, 3, PASSES, 32], BF16, ar)
            WQN = sb("WQN", [P, 2, QLORA], F32, ar)
            WKV = sb("WKV", [P, 2, 2, LORA], F32, ar)
            WOT = sb("WOT", [P, 2, D], F32, ar)
            WQKE = sb("WQKE", [P, 2, QK, LORA], F32, ar)

        s_ids = sem("s_ids"); s_pos = sem1("s_pos"); s_ts = sem1("s_ts")
        s_tab = sem1("s_tab")
        diff_free = sem1("diff_free"); diff_ready = sem1("diff_ready"); mag_ready = sem1("mag_ready")
        expo_ready = sem1("expo_ready"); exb_ready = sem1("exb_ready"); mask_ready = sem1("mask_ready")
        mask_used = sem1("mask_used"); emb_ready = sem1("emb_ready"); h_ready = sem1("h_ready")
        exb_free = sem1("exb_free"); pos_ps = sem1("pos_ps"); pos_ready = sem1("pos_ready")
        w_loaded = [sem1("w_loaded0"), sem1("w_loaded1")]
        w_used = sem1("w_used"); wqk_ps = sem1("wqk_ps"); wqk_sb = sem1("wqk_sb"); wqk_out = sem1("wqk_out")
        wvo_ps = sem1("wvo_ps"); wvo_sb = sem1("wvo_sb")

        def e_sync(eng):
            eng.dma_start(CST[:, :], a["consts"]).then_inc(s_const, 16)
            eng.dma_start(XB[:, :, :].rearrange("p b n -> p (b n)"),
                          a["x"].rearrange("(o b) n -> o (b n)", o=1).to_broadcast([P, NB * S])).then_inc(s_ids, 16)
            eng.dma_start(EXT[:, :], a["ext"]).then_inc(s_ids, 16)
            for t in range(TT):
                src = bass.AP(a["pos_w"].tensor, S - P * (t + 1), [[1, P], [1, S]])
                eng.dma_start(POSF[:, t, :], src).then_inc(s_pos, 16)
            for g in range(4):
                src = bass.AP(a["ts_w"].tensor, g, [[0, 32], [BPP, PASSES]])
                with nc.allow_non_contiguous_dma(reason="32 table entries"):
                    eng.dma_start(TSC[32 * g:32 * g + 32, :], src).then_inc(s_ts, 16)

        def e_pool(eng):
            eng.memset(NHALF[:, :], -0.5).then_inc(s_pre, 1)
            eng.wait_ge(s_ids, 32)
            with eng.Fori(0, NB) as b:
                for t in range(TT):
                    n = b * TT + t
                    eng.wait_ge(diff_free, n + 1)
                    eng.tensor_tensor(
                        DIFF[:, t % 2, :].rearrange("p (q n) -> p q n", q=4),
                        EXT[:, bass.ds(n * 4, 4)].unsqueeze(2).to_broadcast([P, 4, S]),
                        XB[:, bass.ds(b, 1), :].to_broadcast([P, 4, S]), ALU.subtract).then_inc(diff_ready, 1)

        def e_act(eng):
            eng.sem_inc(diff_free, 2)
            eng.sem_inc(exb_free, 2)
            def magnitude(n, u):
                eng.wait_ge(diff_ready, n + 1)
                eng.wait_ge(expo_ready, n)
                eng.activation(MAG[:, u, :], DIFF[:, u, :], ACT.Abs).then_inc(diff_free, 1)

            def exponent(n, u):
                eng.wait_ge(expo_ready, n + 1)
                eng.wait_ge(exb_free, n + 1)
                eng.activation(EXB[:, u, :], EXPO[:, u, :], ACT.Relu, bias=-127.0).then_inc(exb_ready, 1)

            with eng.Fori(0, NB) as b:
                for t in range(TT):
                    magnitude(b * TT + t, t % 2)
                    exponent(b * TT + t, t % 2)

        def e_dve(eng):
            eng.wait_ge(s_const, 16)
            eng.tensor_copy(IDB[:, :], ident).then_inc(s_pre, 1)
            eng.tensor_copy(MASKB[:, :], CST[:, C_MASK:C_MASK + P]).then_inc(s_pre, 1)
            eng.wait_ge(s_ts, 64)
            k = 0
            for part in range(3):
                src = TSC[:, :] if part == 0 else TSR[:, part - 1, :]
                eng.tensor_copy(TSH[:, part, :], src).then_inc(s_tab, 1)
                eng.wait_ge(s_tab, k + 1)
                eng.tensor_copy(TSF[:, part, :], TSH[:, part, :]).then_inc(s_tab, 1)
                eng.wait_ge(s_tab, k + 2)
                k += 2
                if part < 2:
                    eng.tensor_tensor(TSR[:, part, :], src, TSF[:, part, :], ALU.subtract).then_inc(s_tab, 1)
                    k += 1
                    eng.wait_ge(s_tab, k)
            for part in range(3):
                for q in range(PASSES):
                    eng.tensor_scalar(TAB[:, part, q, :], CST[:, C_ID32:C_ID32 + 32], TSF[:, part, q:q + 1], None,
                                      ALU.mult).then_inc(s_tab, 1)
                    k += 1
            for t in range(TT):
                eng.wait_ge(pos_ps, t + 1)
                eng.tensor_copy(POSB[:, t, :], PS[:, 4 + t, :]).then_inc(pos_ready, 1)
            eng.wait_ge(pos_ready, TT)

            def expo(n, u):
                eng.wait_ge(diff_free, n + 3)
                eng.tensor_scalar(EXPO[:, u, :], MAG[:, u, :].bitcast(I32), 23, None,
                                  ALU.logical_shift_right).then_inc(expo_ready, 1)

            def masks(n, u):
                eng.wait_ge(exb_ready, n + 1)
                for q in range(PASSES):
                    eng.wait_ge(mask_used, n * PASSES + q + 1)
                    ins = eng.tensor_scalar(MSK[:, q, :], EXB[:, u, :], CST[:, C_GRP:C_GRP + 1], float(BPP * q),
                                            ALU.subtract, ALU.is_equal).then_inc(mask_ready, 1)
                eng.wait_ge(mask_ready, n * PASSES + PASSES)
                eng.sem_inc(exb_free, 1)

            def add_pos(n, t):
                eng.wait_ge(emb_ready, n + 1)
                eng.tensor_tensor(flat(H[:, bass.ds(n, 1), :]), PS[:, t % 2, :], POSB[:, t, :],
                                  ALU.add).then_inc(h_ready, 1)

            with eng.Fori(0, NB) as b:
                for t in range(TT):
                    expo(b * TT + t, t % 2)
                    masks(b * TT + t, t % 2)
                    add_pos(b * TT + t, t)

        def e_pe(eng):
            eng.sem_inc(mask_used, PASSES)
            eng.wait_ge(s_tab, 32)
            eng.wait_ge(s_pre, 3)
            eng.wait_ge(s_pos, 64)
            for t in range(TT):
                eng.matmul(PS[:, 4 + t, :], CST[:, C_FLIP:C_FLIP + P], POSF[:, t, :], start=True, stop=True)\
                   .then_inc(pos_ps, 1)
            eng.wait_ge(pos_ready, TT)
            with eng.Fori(0, NB) as b:
                for t in range(TT):
                    n = b * TT + t
                    for q in range(PASSES):
                        eng.wait_ge(mask_ready, n * PASSES + q + 1)
                        if q == 0 and t >= 2:
                            eng.wait_ge(h_ready, n - 1)
                        elif q == 0:
                            eng.wait_ge(h_ready, n - t)
                        for part in range(3):
                            for r in range(4):
                                mm = eng.matmul(PS[32 * r:32 * r + 32, t % 2, :], TAB[:, part, q, :],
                                                MSK[:, q, r * S:(r + 1) * S],
                                                start=(q == 0 and part == 0), stop=(q == PASSES - 1 and part == 2))
                        mm.then_inc(mask_used, 1)
                    eng.wait_ge(mask_used, (n + 2) * PASSES)
                    eng.sem_inc(emb_ready, 1)

        def w_sync(eng):
            wq = a["wq_b"].rearrange("(h d) k -> h d k", h=NH)
            wkv = a["wkv_b"].rearrange("(h u d) k -> h d u k", h=NH, u=2)
            wot = a["woT"].rearrange("(h d) n -> h d n", h=NH)
            with eng.Fori(0, NH // 2) as j:
                for u in range(2):
                    h = j * 2 + u
                    eng.wait_ge(w_used, h + 1)
                    eng.dma_start(WQN[:, u, :], wq[bass.ds(h, 1), 0:P, :].rearrange("a d k -> (a d) k"))\
                       .then_inc(w_loaded[u], 16)
                    eng.dma_start(WKV[:, u, :, :], wkv[bass.ds(h, 1)].rearrange("a d u k -> (a d) u k"))\
                       .then_inc(w_loaded[u], 16)
                    eng.dma_start(WOT[:, u, :], wot[bass.ds(h, 1)].rearrange("a d n -> (a d) n"))\
                       .then_inc(w_loaded[u], 16)
                    eng.wait_ge(wqk_sb, h + 1)
                    eng.dma_start(wqk_scr[bass.ds(h, 1)].rearrange("a p k c -> (a p) k c"), WQKE[:, u, :, :])\
                       .then_inc(wqk_out, 16)
            eng.wait_ge(wqk_out, 16 * NH)

        def w_pe(eng):
            eng.sem_inc(w_used, 2)
            with eng.Fori(0, NH // 2) as j:
                for u in range(2):
                    h = j * 2 + u
                    eng.wait_ge(w_loaded[u], j * 48 + 48)
                    if u == 0:
                        eng.wait_ge(wqk_sb, h)
                        eng.wait_ge(wvo_sb, h)
                    for k in range(QK):
                        mm = eng.matmul(PS[:, 2 + u, k * P:(k + 1) * P], WQN[:, u, k * P:(k + 1) * P],
                                        WKV[:, u, 0, :], start=True, stop=True)
                    mm.then_inc(wqk_ps, 1)
                    eng.matmul(PS[:, 4 + u, :], WKV[:, u, 1, :], WOT[:, u, :], start=True, stop=True)\
                       .then_inc(wvo_ps, 1)
                    eng.wait_ge(wvo_ps, h + 1)
                    eng.sem_inc(w_used, 1)

        def w_act(eng):
            with eng.Fori(0, NH // 2) as j:
                for u in range(2):
                    h = j * 2 + u
                    eng.wait_ge(wqk_ps, h + 1)
                    eng.wait_ge(wqk_out, j * 32)
                    eng.activation(WQKE[:, u, :, :].rearrange("p k c -> p (k c)"), PS[:, 2 + u, 0:QLORA],
                                   ACT.Copy).then_inc(wqk_sb, 1)

        def w_dve(eng):
            with eng.Fori(0, NH // 2) as j:
                for u in range(2):
                    h = j * 2 + u
                    eng.wait_ge(wvo_ps, h + 1)
                    eng.tensor_copy(flat(WVO[:, bass.ds(h, 1), :]), PS[:, 4 + u, :]).then_inc(wvo_sb, 1)

        with Arena() as ar:
            WA = sb("WA", [P, KT, QKV0], F32, ar)
            QNW = sb("QNW", [P, QK], F32, ar)
            KVW = sb("KVW", [P, 1], F32, ar)
            WQ = sb("WQ", [P, 2, QK, 2 * P], F32, ar)
            XN = sb("XN", [P, 2, D], F32, ar)
            XNT = sb("XNT", [P, KT, P], F32, ar)
            RAW = sb("RAW", [P, TT, QKV0], F32, ar)
            SQ = sb("SQ", [P, QLORA], F32, ar)
            SSQ = sb("SSQ", [P, 2 * TT], F32, ar)
            MSQ = sb("MSQ", [P, 2 * TT], F32, ar)
            RMS = sb("RMS", [P, 2 * TT], F32, ar)
            KR = sb("KR", [P, 2, ROPE], F32, ar)
            QL = sb("QL", [P, TT, QLORA], F32, ar)
            CN = sb("CN", [P, TT, LORA], F32, ar)
            KP = sb("KP", [P, TT, 2 * ROPE], F32, ar)
            QLT = sb("QLT", [P, QK, S], F32, ar)
            CT = sb("CT", [P, S], F32, ar)
            KPT = sb("KPT", [P, S], F32, ar)
            QN = sb("QN", [P, 2, S], F32, ar)
            QP = sb("QP", [P, 2, S], F32, ar)
            NMX = sb("NMX", [P, 2, TT], F32, ar)
            SUM = sb("SUM", [P, 2, TT], F32, ar)
            RSUM = sb("RSUM", [P, 2, TT], F32, ar)
            PR = sb("PR", [P, TT, S], F32, ar)
            PT = sb("PT", [P, TT, S], F32, ar)
            OT = sb("OT", [P, 2, S], F32, ar)
            ZB = sb("ZB", [P, S], BF16, ar)

        arena_w.close()

        s_wa = sem("s_wa"); ln_s = sem("ln_s"); ln_p = sem("ln_p"); ln_ready = sem("ln_ready"); xn_ready = sem("xn_ready")
        xt_ps = sem("xt_ps"); xt_ready = sem("xt_ready"); raw_ps = sem("raw_ps"); raw_ready = sem("raw_ready")
        ssq_ready = sem("ssq_ready"); msq_ready = sem("msq_ready"); rms_ready = sem("rms_ready")
        kr_done = sem("kr_done"); kv_ready = sem("kv_ready"); kt_ps = sem("kt_ps"); kt_ready = sem("kt_ready"); kc_ready = sem("kc_ready")
        wq_loaded = [sem("wq_loaded0"), sem("wq_loaded1")]
        qn_ps = sem("qn_ps"); qn_ready = sem("qn_ready"); qp_ps = sem("qp_ps"); qp_ready = sem("qp_ready")
        s_ps = sem("s_ps"); max_ready = sem("max_ready"); p_ready = sem("p_ready"); rs_ready = sem("rs_ready")
        pn_ready = sem("pn_ready"); pt_ps = sem("pt_ps"); pt_ready = sem("pt_ready"); ot_ps = sem("ot_ps")
        ot_ready = sem("ot_ready"); w_done = sem("w_done"); res_done = sem("res_done"); zb_ready = sem("zb_ready")
        sq_done = sem("sq_done")
        SB, PTB, QB = 4, 6, 7

        def tile_at(u, i):
            return (SB + 1 - u, 0) if i == 2 else (SB + u, P if i == 1 else 0)


        def a_sync(eng):
            eng.dma_start(WA[:, :, :], a["waT"].rearrange("(k p) n -> p k n", p=P)).then_inc(s_wa, 16)
            with nc.allow_non_contiguous_dma(reason="norm weights"):
                eng.dma_start(QNW[:, :], a["q_norm_w"].rearrange("(k p) -> p k", p=P)).then_inc(s_wa, 16)
                eng.dma_start(KVW[:, :], a["kv_norm_w"].rearrange("(p o) -> p o", o=1)).then_inc(s_wa, 16)
            wpe = a["wpe"].rearrange("h (k p) c -> h p k c", p=P)
            with eng.Fori(0, NB) as b:
                with eng.Fori(0, NH // 2) as j:
                    for u in range(2):
                        n = b * NH + j * 2 + u
                        eng.wait_ge(qp_ps, n + 1)
                        h = j * 2 + u
                        eng.dma_start(WQ[:, u, :, 0:P], wqk_scr[bass.ds(h, 1)].rearrange("a p k c -> (a p) k c"))\
                           .then_inc(wq_loaded[u], 16)
                        eng.dma_start(WQ[:, u, :, P:2 * P], wpe[bass.ds(h, 1)].rearrange("a p k c -> (a p) k c"))\
                           .then_inc(wq_loaded[u], 16)

        def layernorm_stats(eng, b, k0):
            for t in range(TT):
                eng.bn_stats(STAT[:, t, :], flat(H[:, bass.ds(b * TT + t, 1), :])).then_inc(ln_s, 1)
            eng.wait_ge(ln_s, k0 + b * 2 * TT + TT)
            eng.sem_inc(s_alone, 1)
            for t in range(TT):
                eng.bn_aggr(MV[:, t, :], STAT[:, t:t + 1, :]).then_inc(ln_s, 1)

        def layernorm_rstd(eng, b, k0, p0):
            eng.wait_ge(ln_s, k0 + b * 2 * TT + 2 * TT)
            eng.sem_inc(s_alone, 1)
            eng.tensor_scalar(VEPS[:, :], MV[:, :, 1], 1e-5, 1.0, ALU.add, ALU.mult).then_inc(ln_p, 1)
            eng.wait_ge(ln_p, p0 + b + 1)
            eng.tensor_tensor(RSTD[:, :], VEPS[:, :], NHALF[:, 0:TT], ALU.pow).then_inc(ln_ready, 1)

        def a_pool(eng):
            with eng.Fori(0, NB) as b:
                layernorm_rstd(eng, b, 0, 0)
                eng.wait_ge(ssq_ready, b * 2 * TT + 2 * TT)
                eng.sem_inc(s_alone, 1)
                eng.tensor_scalar(MSQ[:, 0:TT], SSQ[:, 0:TT], 1.0 / LORA, 1e-6, ALU.mult, ALU.add).then_inc(msq_ready, 1)
                eng.tensor_scalar(MSQ[:, TT:], SSQ[:, TT:], 1.0 / QLORA, 1e-6, ALU.mult, ALU.add).then_inc(msq_ready, 1)
                eng.wait_ge(msq_ready, b * 2 + 2)
                eng.tensor_tensor(RMS[:, :], MSQ[:, :], NHALF[:, :], ALU.pow).then_inc(rms_ready, 1)
                with eng.Fori(0, NH // 2) as j:
                    for u in range(2):
                        n = b * NH + j * 2 + u
                        for i in range(TT):
                            eng.wait_ge(rs_ready, n * TT + i + 1)
                            eng.sem_inc(s_alone, 1)
                            eng.tensor_scalar(PR[:, i, 0:(i + 1) * P], PR[:, i, 0:(i + 1) * P], RSUM[:, u, i:i + 1],
                                              1.0, ALU.mult, ALU.mult).then_inc(pn_ready, 1)

        def a_dve(eng):
            eng.sem_inc(pt_ready, 1)
            eng.sem_inc(ot_ready, 1)
            eng.memset(ZB[:, :], 0.0).then_inc(zb_ready, 1)
            eng.wait_ge(s_wa, 48)
            eng.tensor_scalar(QNS[:, :], QNW[:, :], SCALE0, None, ALU.mult).then_inc(zb_ready, 1)
            with eng.Fori(0, NB) as b:
                layernorm_stats(eng, b, 0)
                eng.wait_ge(ln_ready, b + 1)
                for t in range(TT):
                    if t >= 2:
                        eng.wait_ge(xt_ps, b * TT + t - 1)
                    eng.tensor_scalar(XN[:, t % 2, :], flat(H[:, bass.ds(b * TT + t, 1), :]), MV[:, t, 0:1],
                                      RSTD[:, t:t + 1], ALU.subtract, ALU.mult).then_inc(xn_ready, 1)
                eng.wait_ge(rms_ready, b + 1)
                for t in range(TT):
                    eng.tensor_scalar(QL[:, t, :], RAW[:, t, 0:QLORA], RMS[:, TT + t:TT + t + 1], None,
                                      ALU.mult).then_inc(kv_ready, 1)
                    eng.tensor_scalar(CN[:, t, :], RAW[:, t, QLORA:QLORA + LORA], RMS[:, t:t + 1], None,
                                      ALU.mult).then_inc(kv_ready, 1)
                    kk = RAW[:, t, QLORA + LORA:QKV0]
                    c0 = C_ROPEK + t * 2 * ROPE
                    if t >= 1:
                        eng.wait_ge(kv_ready, b * 4 * TT + 4 * t)
                    eng.tensor_tensor(KR[:, 0, :], kk, CST[:, c0:c0 + ROPE], ALU.mult).then_inc(kr_done, 1)
                    eng.tensor_tensor(KR[:, 1, 0:32], kk[:, 32:64], CST[:, c0 + ROPE:c0 + ROPE + 32],
                                      ALU.mult).then_inc(kr_done, 1)
                    eng.tensor_tensor(KR[:, 1, 32:64], kk[:, 0:32], CST[:, c0 + ROPE + 32:c0 + 2 * ROPE],
                                      ALU.mult).then_inc(kr_done, 1)
                    eng.wait_ge(kr_done, b * 3 * TT + 3 * t + 3)
                    for r in range(2):
                        eng.tensor_tensor(KP[:, t, r * ROPE:(r + 1) * ROPE], KR[:, 0, :], KR[:, 1, :],
                                          ALU.add).then_inc(kv_ready, 1)
                for t in range(TT):
                    eng.wait_ge(kt_ps, b * 2 * TT + 2 * t + 2)
                    eng.tensor_copy(CT[:, t * P:(t + 1) * P], PS[:, 6 + t % 2, 0:P]).then_inc(kc_ready, 1)
                    eng.tensor_copy(KPT[:, t * P:(t + 1) * P], PS[:, 6 + t % 2, P:2 * P]).then_inc(kc_ready, 1)

                def query_pe(n, u):
                    eng.wait_ge(qp_ps, n + 3)
                    eng.tensor_tensor(QP[:, u, :], PS[:, QB, :], CST[:, C_ROPEQ:C_ROPEQ + S], ALU.mult)\
                       .then_inc(qp_ready, 1)

                def tile_max(n, u, i):
                    bank, col = tile_at(u, i)
                    eng.wait_ge(s_ps, n * 3 + max(i, 1))
                    eng.tensor_reduce(NMX[:, u, i:i + 1], PS[:, bank, col:col + (i + 1) * P], AX, ALU.max, negate=True)\
                       .then_inc(max_ready, 1)

                def tile_recip(n, u, i):
                    eng.wait_ge(p_ready, n * TT + i + 3)
                    eng.reciprocal(RSUM[:, u, i:i + 1], SUM[:, u, i:i + 1]).then_inc(rs_ready, 1)

                def tiles_turned(n, u, i):
                    eng.wait_ge(pt_ps, n * 3 + i + 1)
                    if i == 1:
                        eng.tensor_copy(PT[:, 0, 0:P], PS[:, PTB, 0:P])
                    col = P if i == 1 else 0
                    eng.tensor_copy(PT[:, 0:i + 1, i * P:(i + 1) * P],
                                    PS[:, PTB, col:col + (i + 1) * P].rearrange("p (k q) -> p k q", q=P))\
                       .then_inc(pt_ready, 1)

                def head_out(n, u):
                    eng.wait_ge(ot_ps, n + 1)
                    eng.tensor_scalar(OT[:, u, :], PS[:, QB, :], KVW[:, 0:1], None, ALU.mult).then_inc(ot_ready, 1)

                def head(n, u, first=False, last=False):
                    tile_max(n, u, 2)
                    tile_recip(n, u, 0)
                    tile_recip(n, u, 1)
                    tile_recip(n, u, 2)
                    if not first:
                        head_out(n - 1, 1 - u)
                    tile_max(n, u, 3)
                    tile_recip(n, u, 3)
                    tiles_turned(n, u, 1)
                    if not last:
                        query_pe(n + 1, 1 - u)
                    tiles_turned(n, u, 2)
                    tiles_turned(n, u, 3)
                    if not last:
                        tile_max(n + 1, 1 - u, 0)
                        tile_max(n + 1, 1 - u, 1)

                n0 = b * NH
                query_pe(n0, 0)
                tile_max(n0, 0, 0)
                tile_max(n0, 0, 1)
                head(n0, 0, first=True)
                with eng.Fori(0, NH // 2 - 1) as j:
                    head(n0 + j * 2 + 1, 1)
                    head(n0 + j * 2 + 2, 0)
                head(n0 + NH - 1, 1, last=True)
                head_out(n0 + NH - 1, 1)
                for t in range(TT):
                    eng.wait_ge(w_done, b * TT + t + 1)
                    h = flat(H[:, bass.ds(b * TT + t, 1), :])
                    eng.tensor_tensor(h, PS[:, t, :], h, ALU.add).then_inc(res_done, 1)
                eng.wait_ge(res_done, b * TT + TT)

        def a_act(eng):
            eng.sem_inc(p_ready, 2)
            eng.wait_ge(s_wa, 48)
            eng.wait_ge(zb_ready, 2)
            with eng.Fori(0, NB) as b:
                for t in range(TT):
                    eng.wait_ge(xt_ps, b * TT + t + 1)
                    if t >= 1:
                        eng.wait_ge(raw_ps, b * TT + t)
                    eng.activation(flat(XNT[:, :, :]), PS[:, 4, :], ACT.Copy).then_inc(xt_ready, 1)
                    eng.wait_ge(raw_ps, b * TT + t + 1)
                    eng.activation(RAW[:, t, 0:QLORA], PS[:, 5, 0:QLORA], ACT.Copy).then_inc(raw_ready, 1)
                    eng.activation(RAW[:, t, QLORA:], PS[:, 6, 0:LORA + ROPE], ACT.Copy).then_inc(raw_ready, 1)
                    eng.wait_ge(raw_ready, b * 2 * TT + 2 * t + 2)
                    eng.activation(SQ[:, 0:LORA], RAW[:, t, QLORA:QLORA + LORA], ACT.Square,
                                   accum_out=SSQ[:, t:t + 1]).then_inc(ssq_ready, 1)
                    eng.wait_ge(ssq_ready, b * 2 * TT + 2 * t + 1)
                    eng.activation(SQ[:, :], RAW[:, t, 0:QLORA], ACT.Square,
                                   accum_out=SSQ[:, TT + t:TT + t + 1]).then_inc(ssq_ready, 1)
                    eng.wait_ge(ssq_ready, b * 2 * TT + 2 * t + 2)
                for t in range(TT):
                    eng.wait_ge(kt_ps, b * 2 * TT + 2 * t + 1)
                    for k in range(QK):
                        ins = eng.activation(QLT[:, k, t * P:(t + 1) * P], PS[:, 4 + t % 2, k * P:(k + 1) * P],
                                             ACT.Copy, scale=QNS[:, k:k + 1])
                    ins.then_inc(kt_ready, 1)

                def query_latent(n, u):
                    eng.wait_ge(qn_ps, n + 1)
                    eng.activation(QN[:, u, :], PS[:, QB, :], ACT.Copy, scale=KVW[:, 0:1]).then_inc(qn_ready, 1)

                def tile_exp(n, u, i):
                    bank, col = tile_at(u, i)
                    if i == 0:
                        eng.wait_ge(pt_ps, n * 3 + 1)
                    eng.wait_ge(max_ready, n * TT + max(i, 1) + 1)
                    eng.activation(PR[:, i, 0:(i + 1) * P], PS[:, bank, col:col + (i + 1) * P], ACT.Exp,
                                   bias=NMX[:, u, i:i + 1], accum_out=SUM[:, u, i:i + 1]).then_inc(p_ready, 1)

                def head(n, u, last=False):
                    for i in range(TT):
                        tile_exp(n, u, i)
                    if not last:
                        query_latent(n + 1, 1 - u)

                n0 = b * NH
                query_latent(n0, 0)
                head(n0, 0)
                with eng.Fori(0, NH // 2 - 1) as j:
                    head(n0 + j * 2 + 1, 1)
                    head(n0 + j * 2 + 2, 0)
                head(n0 + NH - 1, 1, last=True)

        def a_pe(eng):
            eng.sem_inc(qp_ps, 2)
            eng.sem_inc(pt_ps, 1)
            eng.wait_ge(s_wa, 48)
            eng.wait_ge(zb_ready, 1)
            with eng.Fori(0, NB) as b:
                for t in range(TT):
                    n = b * TT + t
                    eng.wait_ge(xn_ready, n + 1)
                    if t >= 1:
                        eng.wait_ge(xt_ready, n)
                    for k in range(KT):
                        mm = eng.transpose(PS[:, 4, k * P:(k + 1) * P], XN[:, t % 2, k * P:(k + 1) * P], ident)
                    mm.then_inc(xt_ps, 1)
                    eng.wait_ge(xt_ready, n + 1)
                    if t >= 1:
                        eng.wait_ge(raw_ready, 2 * n)
                    for k in range(KT):
                        eng.matmul(PS[:, 5, 0:QLORA], XNT[:, k, :], WA[:, k, 0:QLORA], start=(k == 0), stop=(k == KT - 1))
                        mm = eng.matmul(PS[:, 6, 0:LORA + ROPE], XNT[:, k, :], WA[:, k, QLORA:],
                                        start=(k == 0), stop=(k == KT - 1))
                    mm.then_inc(raw_ps, 1)
                eng.wait_ge(raw_ready, b * 2 * TT + 2 * TT)
                for t in range(TT):
                    eng.wait_ge(kv_ready, b * 4 * TT + 4 * t + 4)
                    if t >= 2:
                        eng.wait_ge(kt_ready, b * TT + t - 1)
                        eng.wait_ge(kc_ready, b * 2 * TT + 2 * (t - 1))
                    for k in range(QK):
                        mm = eng.transpose(PS[:, 4 + t % 2, k * P:(k + 1) * P], QL[:, t, k * P:(k + 1) * P], ident)
                    mm.then_inc(kt_ps, 1)
                    eng.transpose(PS[:, 6 + t % 2, 0:P], CN[:, t, :], ident)
                    eng.transpose(PS[:, 6 + t % 2, P:2 * P], KP[:, t, :], ident).then_inc(kt_ps, 1)
                eng.wait_ge(kt_ready, b * TT + TT)
                eng.wait_ge(kc_ready, b * 2 * TT + 2 * TT)

                def query_latent(n, u, j):
                    eng.wait_ge(wq_loaded[u], j * 32 + 32)
                    for k in range(QK):
                        mm = eng.matmul(PS[:, QB, :], WQ[:, u, k, 0:P], QLT[:, k, :], start=(k == 0), stop=(k == QK - 1))
                    mm.then_inc(qn_ps, 1)

                def query_pe(n, u):
                    eng.wait_ge(qn_ready, n + 1)
                    for k in range(QK):
                        mm = eng.matmul(PS[:, QB, :], WQ[:, u, k, P:2 * P], QLT[:, k, :], start=(k == 0), stop=(k == QK - 1))
                    mm.then_inc(qp_ps, 1)

                def scores(n, u, i):
                    if i == 1:
                        eng.wait_ge(p_ready, n * TT + 1)
                        eng.wait_ge(qn_ready, n + 1)
                        eng.wait_ge(qp_ready, n + 1)
                    elif i == 2:
                        eng.wait_ge(p_ready, n * TT + 2)
                    else:
                        eng.wait_ge(p_ready, n * TT + 4)
                    for r in ((0, 1) if i == 1 else (i,)):
                        w = (r + 1) * P
                        bank, col = tile_at(u, r)
                        o = PS[:, bank, :]
                        eng.matmul(o[:, col:col + w], QN[:, u, r * P:w], CT[:, 0:w], start=True, stop=False)
                        eng.matmul(o[:, col:col + w], QP[:, u, r * P:w], KPT[:, 0:w], start=False, stop=False)
                        mm = eng.matmul(o[:, col + r * P:col + w], IDB[:, :], MASKB[:, :], start=False, stop=True)
                    mm.then_inc(s_ps, 1)

                def turn(n, u, i):
                    eng.wait_ge(pn_ready, n * TT + i + 1)
                    eng.wait_ge(pt_ready, n * 3 + i)
                    if i == 1:
                        eng.transpose(PS[:, PTB, 0:P], PR[:, 0, 0:P], ident)
                    col = P if i == 1 else 0
                    for k in range(i + 1):
                        mm = eng.transpose(PS[:, PTB, col + k * P:col + (k + 1) * P], PR[:, i, k * P:(k + 1) * P], ident)
                    mm.then_inc(pt_ps, 1)

                def values(n):
                    eng.wait_ge(pt_ready, n * 3 + 4)
                    for k in range(TT):
                        mm = eng.matmul(PS[:, QB, k * P:], CN[:, k, :], PT[:, k, k * P:], start=(k == 0), stop=(k == TT - 1))
                    mm.then_inc(ot_ps, 1)

                def project(n, u, h, tiles, last=False):
                    eng.wait_ge(ot_ready, n + 2)
                    for t in tiles:
                        mm = eng.matmul(PS[:, t, :], OT[:, u, t * P:(t + 1) * P], flat(WVO[:, bass.ds(h, 1), :]),
                                        start=False, stop=last, skip_group_check=True)
                        if last:
                            mm.then_inc(w_done, 1)

                def head(n, u, j, h, first=False, last=False):
                    scores(n, u, 2)
                    if not first:
                        values(n - 1)
                    scores(n, u, 3)
                    if not last:
                        eng.wait_ge(ot_ready, n + 1)
                        query_latent(n + 1, 1 - u, j)
                    turn(n, u, 1)
                    if not first:
                        project(n - 1, 1 - u, h - 1, (0, 1))
                    if not last:
                        query_pe(n + 1, 1 - u)
                    turn(n, u, 2)
                    if not first:
                        project(n - 1, 1 - u, h - 1, (2, 3))
                    turn(n, u, 3)
                    if not last:
                        scores(n + 1, 1 - u, 1)

                n0 = b * NH
                j0 = b * (NH // 2)
                eng.wait_ge(res_done, b * TT)
                for t in range(TT):
                    eng.matmul(PS[:, t, :], IDB[:, :], ZB[:, :], start=True, stop=False, skip_group_check=True)
                eng.wait_ge(ot_ready, n0 + 1)
                query_latent(n0, 0, j0)
                query_pe(n0, 0)
                scores(n0, 0, 1)
                head(n0, 0, j0, 0, first=True)
                with eng.Fori(0, NH // 2 - 1) as j:
                    head(n0 + j * 2 + 1, 1, j0 + j + 1, j * 2 + 1)
                    head(n0 + j * 2 + 2, 0, j0 + j + 1, j * 2 + 2)
                head(n0 + NH - 1, 1, None, NH - 1, last=True)
                values(n0 + NH - 1)
                project(n0 + NH - 1, 1, NH - 1, range(TT), last=True)

        CH = [(0, 512), (512, 512), (1024, 384)]
        IT = INTER // P
        RT1, RT2 = 2 * INTER // P, D // P
        ROWS = (RT1 + RT2) * P
        scale_scr = nc.dram_tensor("scale_scr", [2, ROWS], F32, kind="Internal").ap()
        with Arena() as ar:
            W1Q = sb("W1Q", [P, KT, 2 * INTER], BF16, ar)
            W2Q = sb("W2Q", [P, IT, D], BF16, ar)
            SW = sb("SW", [P, ROWS], F32, ar)
            with Arena() as tmp:
                RW = sb("RW", [P, ROWS], F32, tmp)
                W1T = sb("W1T", [P, 2, 2 * INTER], F32, tmp)
                W2T = sb("W2T", [P, IT, D], F32, tmp)
                WN1 = sb("WN1", [P, 2, D], F32, tmp)
                WN2 = sb("WN2", [P, 2, INTER], F32, tmp)
                AMW = sb("AMW", [P, 2, RT1 + RT2], F32, tmp)
            FXN = sb("FXN", [P, 2, D], F32, ar)
            FXM = sb("FXM", [P, 2, D], F32, ar)
            FXQ = sb("FXQ", [P, 2, D], BF16, ar)
            FXT = sb("FXT", [P, 2, KT, P], BF16, ar)
            FS = sb("FS", [P, 2, 8], F32, ar)
            FST = sb("FST", [P, 2, 8], F32, ar)
            GS = sb("GS", [P, 2, 512], F32, ar)
            GA = sb("GA", [P, 2, 512], F32, ar)
            US = sb("US", [P, 2, 512], F32, ar)
            HM = sb("HM", [P, 2, INTER], F32, ar)
            HR = sb("HR", [P, INTER], F32, ar)
            HQ = sb("HQ", [P, 2, INTER], BF16, ar)
            HT = sb("HT", [P, 2, IT, P], BF16, ar)
            FO = sb("FO", [P, 2, D], F32, ar)

        V_MEAN, V_VAR, V_RSTD, V_SX, V_RX, V_SH, V_RH, V_AM = range(8)
        fw_load = [sem("fw_load0"), sem("fw_load1")]; fw_max = sem("fw_max"); fw_s = sem("fw_s"); fw_scr = sem("fw_scr")
        fw_b = sem("fw_b"); fw_t = [sem("fw_t0"), sem("fw_t1")]; fw_t2 = sem("fw_t2"); fw_q = sem("fw_q"); fw_m = sem("fw_m")
        f_st = sem("f_st"); f_v = sem("f_v"); f_rstd = sem("f_rstd"); f_am = sem("f_am"); f_xm = sem("f_xm"); f_xq = sem("f_xq")
        f_xtp = sem("f_xtp"); f_xt = sem("f_xt"); f_mm = sem("f_mm"); f_g = sem("f_g"); f_ga = sem("f_ga"); f_u = sem("f_u")
        f_hm = sem("f_hm"); f_hr = sem("f_hr"); f_hq = sem("f_hq"); f_htp = sem("f_htp"); f_ht = sem("f_ht")
        f_op = sem("f_op"); f_o = sem("f_o"); f_res = sem("f_res"); f_hs = sem("f_hs"); f_h1 = sem("f_h1"); f_xn = sem("f_xn")

        def fw_tiles():
            return [(0, i) for i in range(RT1)] + [(1, i) for i in range(RT2)]

        def fw_sync(eng):
            w1 = a["w_gate_up"].rearrange("(t p) k -> t p k", p=P)
            with eng.Fori(0, RT1 // 2) as j:
                for u in range(2):
                    eng.wait_ge(fw_free, j * 2 + u + 1)
                    eng.dma_start(WN1[:, u:u + 1, :], w1[bass.ds(j * 2 + u, 1)].rearrange("a p k -> p a k"))\
                       .then_inc(fw_load[u], 16)
            w2 = a["w_down"].rearrange("(t p) k -> t p k", p=P)
            for i in range(RT2):
                if i >= 2:
                    eng.wait_ge(fw_max, RT1 + i - 1)
                eng.dma_start(WN2[:, i % 2, :], w2[i]).then_inc(fw_load2[i % 2], 16)
            eng.dma_start(W2T[:, :, :], a["w_downT"].rearrange("(k p) n -> p k n", p=P)).then_inc(fw_t2, 16)
            w1t = a["w_gate_upT"].rearrange("(k p) n -> k p n", p=P)
            for k in range(KT):
                if k == 2:
                    eng.wait_ge(fw_s, 4)
                    with nc.allow_non_contiguous_dma(reason="one scale a partition"):
                        for i in range(2):
                            eng.dma_start(scale_scr[i].rearrange("(t p) -> p t", p=P), AMW[:, i, :]).then_inc(fw_scr, 16)
                    eng.wait_ge(fw_scr, 32)
                    eng.dma_start(SW[:, :], scale_scr[0:1].to_broadcast([P, ROWS])).then_inc(fw_b, 16)
                    eng.dma_start(RW[:, :], scale_scr[1:2].to_broadcast([P, ROWS])).then_inc(fw_b, 16)
                if k >= 2:
                    eng.wait_ge(fw_q, k - 1)
                eng.dma_start(W1T[:, k % 2, :], w1t[k]).then_inc(fw_t[k % 2], 16)

        fw_free = sem("fw_free"); fw_load2 = [sem("fw_load20"), sem("fw_load21")]

        def fw_dve(eng):
            eng.sem_inc(fw_free, 2)
            with eng.Fori(0, RT1 // 2) as j:
                for u in range(2):
                    eng.wait_ge(fw_load[u], j * 16 + 16)
                    eng.tensor_reduce(AMW[:, 0, bass.ds(j * 2 + u, 1)], WN1[:, u, :], AX, ALU.max,
                                      apply_absolute_value=True).then_inc(fw_max, 1)
                    eng.wait_ge(fw_max, j * 2 + u + 1)
                    eng.sem_inc(fw_free, 1)
            for i in range(RT2):
                eng.wait_ge(fw_load2[i % 2], 16 * (i // 2) + 16)
                eng.tensor_reduce(AMW[:, 0, RT1 + i:RT1 + i + 1], WN2[:, i % 2, :], AX, ALU.max,
                                  apply_absolute_value=True).then_inc(fw_max, 1)
            eng.wait_ge(fw_max, RT1 + RT2)
            eng.tensor_scalar(AMW[:, 0, :], AMW[:, 0, :], 1.0 / 127.0, 1e-8, ALU.mult, ALU.max).then_inc(fw_s, 2)
            eng.wait_ge(fw_s, 2)
            eng.reciprocal(AMW[:, 1, :], AMW[:, 0, :]).then_inc(fw_s, 2)
            eng.wait_ge(fw_b, 32)
            for k in range(KT):
                eng.wait_ge(fw_t[k % 2], 16 * (k // 2) + 16)
                eng.tensor_tensor(W1T[:, k % 2, :], W1T[:, k % 2, :], RW[:, 0:RT1 * P], ALU.mult).then_inc(fw_m, 1)
                eng.wait_ge(fw_m, k + 1)
                eng.tensor_scalar(W1Q[:, k, :], W1T[:, k % 2, :], MAGIC, MAGIC, ALU.add, ALU.subtract).then_inc(fw_q, 1)
            eng.wait_ge(fw_t2, 16)
            eng.tensor_tensor(W2T[:, :, :], W2T[:, :, :], RW[:, RT1 * P:].unsqueeze(1).to_broadcast([P, IT, D]),
                              ALU.mult).then_inc(fw_m, 1)
            eng.wait_ge(fw_m, KT + 1)
            eng.tensor_scalar(W2Q[:, :, :], W2T[:, :, :], MAGIC, MAGIC, ALU.add, ALU.subtract).then_inc(fw_q, 1)
            eng.wait_ge(fw_q, KT + 1)

        def hrow(n):
            return flat(H[:, bass.ds(n, 1), :])

        def two_by_two(eng, first, steady, last):
            first(0, 0)
            with eng.Fori(0, NT // 2 - 1) as j:
                steady(j * 2 + 1, 1)
                steady(j * 2 + 2, 0)
            last(NT - 1, 1)

        def quant_scale(eng, v, src, dst, rdst, base, count):
            pass

        def f_dve(eng):
            def front(n, u):
                eng.bn_stats(FST[:, u, 0:6], hrow(n)).then_inc(f_st, 1)
                eng.wait_ge(f_st, n * 2 + 1)
                eng.sem_inc(s_alone, 1)
                eng.bn_aggr(FS[:, u, V_MEAN:V_VAR + 1], FST[:, u:u + 1, 0:6]).then_inc(f_st, 1)
                eng.wait_ge(f_rstd, n + 1)
                eng.tensor_scalar(FXN[:, u, :], hrow(n), FS[:, u, V_MEAN:V_MEAN + 1], FS[:, u, V_RSTD:V_RSTD + 1],
                                  ALU.subtract, ALU.mult).then_inc(f_xn, 1)
                eng.wait_ge(f_xn, n + 1)
                eng.tensor_reduce(FS[:, u, V_AM:V_AM + 1], FXN[:, u, :], AX, ALU.max, apply_absolute_value=True)\
                   .then_inc(f_am, 1)
                eng.wait_ge(f_am, n * 3 + 1)
                eng.tensor_scalar(FS[:, u, V_SX:V_SX + 1], FS[:, u, V_AM:V_AM + 1], 1.0 / 127.0, 1e-8,
                                  ALU.mult, ALU.max).then_inc(f_am, 1)
                eng.wait_ge(f_am, n * 3 + 2)
                eng.reciprocal(FS[:, u, V_RX:V_RX + 1], FS[:, u, V_SX:V_SX + 1]).then_inc(f_am, 1)
                eng.wait_ge(f_am, n * 3 + 3)
                eng.tensor_scalar(FXM[:, u, :], FXN[:, u, :], FS[:, u, V_RX:V_RX + 1], MAGIC, ALU.mult, ALU.add)\
                   .then_inc(f_xm, 1)
                eng.wait_ge(f_xm, n + 1)
                eng.tensor_scalar(FXQ[:, u, :], FXM[:, u, :], MAGIC, None, ALU.subtract).then_inc(f_xq, 1)

            def mid(n, u):
                for c, (c0, w) in enumerate(CH):
                    eng.wait_ge(f_mm, n * 3 + c + 1)
                    g = (c % 2) * 2
                    k = n * 3 + c
                    eng.wait_ge(f_gfree, k + 1)
                    eng.scalar_tensor_tensor(GS[:, c % 2, 0:w], PS[:, 1 + g, 0:w], FS[:, u, V_SX:V_SX + 1],
                                             SW[:, c0:c0 + w], ALU.mult, ALU.mult).then_inc(f_g, 1)
                    eng.wait_ge(f_ufree, k + 1)
                    eng.scalar_tensor_tensor(US[:, c % 2, 0:w], PS[:, 2 + g, 0:w], FS[:, u, V_SX:V_SX + 1],
                                             SW[:, INTER + c0:INTER + c0 + w], ALU.mult, ALU.mult).then_inc(f_u, 1)

            def back(n, u):
                eng.wait_ge(f_hm, n * 3 + 3)
                eng.tensor_reduce(FS[:, u, V_AM:V_AM + 1], HM[:, u, :], AX, ALU.max, apply_absolute_value=True)\
                   .then_inc(f_hs, 1)
                eng.wait_ge(f_hs, n * 3 + 1)
                eng.tensor_scalar(FS[:, u, V_SH:V_SH + 1], FS[:, u, V_AM:V_AM + 1], 1.0 / 127.0, 1e-8,
                                  ALU.mult, ALU.max).then_inc(f_hs, 1)
                eng.wait_ge(f_hs, n * 3 + 2)
                eng.reciprocal(FS[:, u, V_RH:V_RH + 1], FS[:, u, V_SH:V_SH + 1]).then_inc(f_hs, 1)
                eng.wait_ge(f_hs, n * 3 + 3)
                eng.tensor_scalar(HR[:, :], HM[:, u, :], FS[:, u, V_RH:V_RH + 1], MAGIC, ALU.mult, ALU.add)\
                   .then_inc(f_hr, 1)
                eng.wait_ge(f_hr, n + 1)
                eng.tensor_scalar(HQ[:, u, :], HR[:, :], MAGIC, None, ALU.subtract).then_inc(f_hq, 1)

            def fin(n, u):
                eng.wait_ge(f_op, n + 1)
                eng.scalar_tensor_tensor(FO[:, u, :], PS[:, 7, :], FS[:, u, V_SH:V_SH + 1], SW[:, RT1 * P:],
                                         ALU.mult, ALU.mult).then_inc(f_o, 1)

            front(0, 0)
            two_by_two(eng,
                       lambda n, u: (mid(n, u), front(n + 1, 1 - u), back(n, u)),
                       lambda n, u: (mid(n, u), fin(n - 1, 1 - u), front(n + 1, 1 - u), back(n, u)),
                       lambda n, u: (mid(n, u), fin(n - 1, 1 - u), back(n, u)))
            fin(NT - 1, 1)

        f_gfree = sem("f_gfree"); f_ufree = sem("f_ufree"); f_pv = sem("f_pv")

        def f_pool(eng):
            def rstd(n, u):
                eng.wait_ge(f_st, n * 2 + 2)
                eng.sem_inc(s_alone, 1)
                eng.tensor_scalar(FS[:, u, V_RSTD:V_RSTD + 1], FS[:, u, V_VAR:V_VAR + 1], 1e-5, 1.0, ALU.add, ALU.mult)\
                   .then_inc(f_pv, 1)
                eng.wait_ge(f_pv, n + 1)
                eng.tensor_tensor(FS[:, u, V_RSTD:V_RSTD + 1], FS[:, u, V_RSTD:V_RSTD + 1], NHALF[:, 0:1], ALU.pow)\
                   .then_inc(f_rstd, 1)

            def gate(n, u):
                for c, (c0, w) in enumerate(CH):
                    eng.wait_ge(f_ga, n * 3 + c + 1)
                    eng.wait_ge(f_u, n * 3 + c + 1)
                    eng.tensor_tensor(HM[:, u, c0:c0 + w], GA[:, c % 2, 0:w], US[:, c % 2, 0:w], ALU.mult)\
                       .then_inc(f_hm, 1)
                    eng.wait_ge(f_hm, n * 3 + c + 1)
                    eng.sem_inc(f_ufree, 1)

            def residual(n, u):
                eng.wait_ge(f_o, n + 1)
                eng.tensor_tensor(hrow(n), hrow(n), FO[:, u, :], ALU.add).then_inc(f_res, 1)

            eng.sem_inc(f_ufree, 2)
            rstd(0, 0)
            two_by_two(eng,
                       lambda n, u: (gate(n, u), rstd(n + 1, 1 - u)),
                       lambda n, u: (gate(n, u), rstd(n + 1, 1 - u), residual(n - 1, 1 - u)),
                       lambda n, u: (gate(n, u), residual(n - 1, 1 - u)))
            residual(NT - 1, 1)

        def f_act(eng):
            def xt(n, u):
                eng.wait_ge(f_xtp, n + 1)
                eng.activation(flat(FXT[:, u, :, :]), PS[:, 0, 0:256].bitcast(BF16), ACT.Copy).then_inc(f_xt, 1)

            def silu(n, u):
                for c, (c0, w) in enumerate(CH):
                    eng.wait_ge(f_g, n * 3 + c + 1)
                    eng.wait_ge(f_ufree, n * 3 + c + 1)
                    eng.activation(GA[:, c % 2, 0:w], GS[:, c % 2, 0:w], ACT.Silu).then_inc(f_ga, 1)
                    eng.wait_ge(f_ga, n * 3 + c + 1)
                    eng.sem_inc(f_gfree, 1)

            def ht(n, u):
                eng.wait_ge(f_htp, n + 1)
                eng.activation(flat(HT[:, u, 0:8, :]), PS[:, 5, :].bitcast(BF16), ACT.Copy)
                eng.activation(flat(HT[:, u, 8:IT, :]), PS[:, 6, 0:192].bitcast(BF16), ACT.Copy).then_inc(f_ht, 1)

            eng.sem_inc(f_gfree, 2)
            two_by_two(eng,
                       lambda n, u: (xt(n, u), silu(n, u)),
                       lambda n, u: (xt(n, u), silu(n, u), ht(n - 1, 1 - u)),
                       lambda n, u: (xt(n, u), silu(n, u), ht(n - 1, 1 - u)))
            ht(NT - 1, 1)

        def f_pe(eng):
            def xt(n, u):
                eng.wait_ge(f_xq, n + 1)
                eng.wait_ge(f_xt, n)
                for k in range(KT):
                    mm = eng.transpose(PS[:, 0, k * 64:(k + 1) * 64].bitcast(BF16), FXQ[:, u, k * P:(k + 1) * P], IDB[:, :])
                mm.then_inc(f_xtp, 1)

            def up(n, u):
                eng.wait_ge(f_xt, n + 1)
                for c, (c0, w) in enumerate(CH):
                    if not (isinstance(n, int) and n * 3 + c < 2):
                        eng.wait_ge(f_u, n * 3 + c - 1)
                    g = (c % 2) * 2
                    for k in range(KT):
                        eng.matmul(PS[:, 1 + g, 0:w], FXT[:, u, k, :], W1Q[:, k, c0:c0 + w], start=(k == 0), stop=(k == KT - 1))
                        mm = eng.matmul(PS[:, 2 + g, 0:w], FXT[:, u, k, :], W1Q[:, k, INTER + c0:INTER + c0 + w],
                                        start=(k == 0), stop=(k == KT - 1))
                    mm.then_inc(f_mm, 1)

            def down(n, u):
                eng.wait_ge(f_hq, n + 1)
                eng.wait_ge(f_ht, n)
                for k in range(IT):
                    mm = eng.transpose(PS[:, 5 + k // 8, (k % 8) * 64:(k % 8 + 1) * 64].bitcast(BF16),
                                       HQ[:, u, k * P:(k + 1) * P], IDB[:, :])
                mm.then_inc(f_htp, 1)
                eng.wait_ge(f_ht, n + 1)
                eng.wait_ge(f_o, n)
                for k in range(IT):
                    mm = eng.matmul(PS[:, 7, :], HT[:, u, k, :], W2Q[:, k, :], start=(k == 0), stop=(k == IT - 1))
                mm.then_inc(f_op, 1)

            two_by_two(eng,
                       lambda n, u: (xt(n, u), up(n, u)),
                       lambda n, u: (xt(n, u), up(n, u), down(n - 1, 1 - u)),
                       lambda n, u: (xt(n, u), up(n, u), down(n - 1, 1 - u)))
            down(NT - 1, 1)

        first_sems.close()

        KVH = NH // 2
        QKC = (NH + KVH) * HD
        with Arena() as ar:
            WB = sb("WB", [P, KT, 2 * D], F32, ar)
            WO1 = sb("WO1", [P, KT, D], F32, ar)
            BXN = sb("BXN", [P, 2, D], F32, ar)
            BXT = sb("BXT", [P, 2, KT, P], F32, ar)
            RA = sb("RA", [P, QKC], F32, ar)
            RB = sb("RB", [P, QKC], F32, ar)
            RS = sb("RS", [P, QKC], F32, ar)
            STK = sb("STK", [P, NH + KVH, 4, HD], F32R, ar)
            VB = sb("VB", [P, TT, KVH, HD + 1], F32, ar)
            QT1 = sb("QT1", [P, NH, S], F32R, ar)
            KT1 = sb("KT1", [P, KVH, S], F32R, ar)
            NM1 = sb("NM1", [P, 3, 2], F32, ar)
            PE1 = sb("PE1", [P, 3, 2, S], F32, ar)
            PT1 = sb("PT1", [P, 3, 2, S], F32, ar)
            RS1 = sb("RS1", [P, 2, 2], F32, ar)
            AO = sb("AO", [P, TT, D], F32, ar)
            AOT = sb("AOT", [P, 2, KT, P], F32, ar)

        b_w = sem("b_w"); b_ones = sem("b_ones"); b_ln = sem("b_ln"); b_lp = sem("b_lp"); b_rstd = sem("b_rstd"); b_xn = sem("b_xn")
        b_xtp = sem("b_xtp"); b_xt = sem("b_xt"); b_pr = sem("b_pr"); b_v = sem("b_v"); b_rot = sem("b_rot"); b_sum = sem("b_sum")
        b_hi = sem("b_hi"); b_lo = sem("b_lo")
        b_tp = sem("b_tp"); b_qt = sem("b_qt"); b_s = sem("b_s"); b_mx = sem("b_mx"); b_e = sem("b_e")
        b_ptp = sem("b_ptp"); b_pt0 = sem("b_pt0"); b_pt1 = sem("b_pt1"); b_o = sem("b_o"); b_rs = sem("b_rs"); b_ao = sem("b_ao")
        b_aop = sem("b_aop"); b_aot = sem("b_aot"); b_out = sem("b_out"); b_res = sem("b_res")
        UN = NH // 2 * TT
        LT, LV = 2, 4
        NSK = (NH + KVH) // 4

        def b_sync(eng):
            eng.dma_start(WB[:, :, :], a["wqkv"].rearrange("(k p) n -> p k n", p=P)).then_inc(b_w, 16)
            eng.dma_start(WO1[:, :, :], a["wo1"].rearrange("(k p) n -> p k n", p=P)).then_inc(b_w, 16)

        def b_pool(eng):
            with eng.Fori(0, NB) as b:
                eng.wait_ge(b_ln, b * 2 * TT + 2 * TT)
                eng.sem_inc(s_alone, 1)
                eng.tensor_scalar(VEPS[:, :], MV[:, :, 1], 1e-5, 1.0, ALU.add, ALU.mult).then_inc(b_lp, 1)
                eng.wait_ge(b_lp, b + 1)
                eng.tensor_tensor(RSTD[:, :], VEPS[:, :], NHALF[:, 0:TT], ALU.pow).then_inc(b_rstd, 1)
                for t in range(TT):
                    n = b * TT + t
                    eng.wait_ge(b_rot, n * 4 + 4)
                    eng.wait_ge(b_lo, n)
                    eng.tensor_tensor(RS[:, :], RA[:, :], RB[:, :], ALU.add).then_inc(b_sum, 1)

        def b_dve(eng):
            eng.memset(VB[:, :, :, HD:HD + 1], 1.0).then_inc(b_ones, 1)
            eng.wait_ge(b_w, 32)
            with eng.Fori(0, NB) as b:
                for t in range(TT):
                    eng.bn_stats(STAT[:, t, :], hrow(b * TT + t)).then_inc(b_ln, 1)
                eng.wait_ge(b_ln, b * 2 * TT + TT)
                eng.sem_inc(s_alone, 1)
                for t in range(TT):
                    eng.bn_aggr(MV[:, t, :], STAT[:, t:t + 1, :]).then_inc(b_ln, 1)
                eng.wait_ge(b_rstd, b + 1)

                def norm(t):
                    n = b * TT + t
                    if t >= 2:
                        eng.wait_ge(b_xtp, n - 1)
                    eng.tensor_scalar(BXN[:, t % 2, :], hrow(n), MV[:, t, 0:1], RSTD[:, t:t + 1],
                                      ALU.subtract, ALU.mult).then_inc(b_xn, 1)

                def rotate(t):
                    n = b * TT + t
                    eng.wait_ge(b_pr, n + 1)
                    eng.wait_ge(b_sum, n)
                    for o, nh, src, tab in ((0, NH, PS[:, 1 + 2 * (t % 2), :], C_RQ1),
                                            (D, KVH, PS[:, 2 + 2 * (t % 2), 0:D // 2], C_RK1)):
                        c0 = tab + t * 2 * HD
                        cos = CST[:, c0:c0 + HD].unsqueeze(1).to_broadcast([P, nh, HD])
                        eng.tensor_tensor(RA[:, o:o + nh * HD].rearrange("p (h d) -> p h d", d=HD),
                                          src.rearrange("p (h d) -> p h d", d=HD), cos, ALU.mult).then_inc(b_rot, 1)
                        x = src.rearrange("p (h d e) -> p h d e", d=HD // 2, e=2)
                        y = RB[:, o:o + nh * HD].rearrange("p (h d e) -> p h d e", d=HD // 2, e=2)
                        sn = CST[:, c0 + HD:c0 + 2 * HD].rearrange("p (d e) -> p d e", e=2)
                        for e in range(2):
                            ins = eng.tensor_tensor(y[:, :, :, e], x[:, :, :, 1 - e],
                                                    sn[:, :, e].unsqueeze(1).to_broadcast([P, nh, HD // 2]), ALU.mult)
                        ins.then_inc(b_rot, 1)

                def low(t):
                    n = b * TT + t
                    eng.wait_ge(b_hi, 2 * n + 2)
                    r = RS[:, :].rearrange("p (h d) -> p h d", d=HD)
                    eng.tensor_tensor(STK[:, 0:NH, 2:4, :], r[:, 0:NH, :].unsqueeze(2).to_broadcast([P, NH, 2, HD]),
                                      STK[:, 0:NH, 0:2, :].bitcast(F32), ALU.subtract)
                    k = STK[:, NH:, :, :].rearrange("p h (x y) d -> p h x y d", y=2)
                    for x in range(2):
                        ins = eng.tensor_tensor(k[:, :, x, 1, :], r[:, NH:, :], k[:, :, x, 0, :].bitcast(F32), ALU.subtract)
                    ins.then_inc(b_lo, 1)

                norm(0)
                norm(1)
                for t in range(TT):
                    n = b * TT + t
                    rotate(t)
                    if t + 2 < TT:
                        norm(t + 2)
                    low(t)
                def top(m):
                    k = b * UN + m
                    eng.wait_ge(b_s, k + 1)
                    eng.tensor_reduce(NM1[:, m % 3, :], PS[:, 2 * (m % 2):2 * (m % 2) + 2, :], AX, ALU.max, negate=True)\
                       .then_inc(b_mx, 1)

                def turned(m):
                    eng.wait_ge(b_ptp, b * UN + m + 1)
                    if m >= 3:
                        eng.wait_ge(b_o, b * UN + m - 2)
                    eng.tensor_copy(PT1[:, m % 3, 0, :], PS[:, 4, :]).then_inc(b_pt0, 1)

                def norm_out(m):
                    hp, t = divmod(m, TT)
                    k = b * UN + m
                    eng.wait_ge(b_o, k + 1)
                    o = PS[:, 6 + m % 2, 0:2 * (HD + 1)].rearrange("p (r d) -> p r d", d=HD + 1)
                    eng.reciprocal(RS1[:, m % 2, :], o[:, :, HD]).then_inc(b_rs, 1)
                    eng.wait_ge(b_rs, k + 1)
                    c = 2 * hp * HD
                    eng.tensor_tensor(AO[:, t, c:c + 2 * HD].rearrange("p (r d) -> p r d", d=HD), o[:, :, 0:HD],
                                      RS1[:, m % 2, :].unsqueeze(2).to_broadcast([P, 2, HD]), ALU.mult).then_inc(b_ao, 1)

                for m in range(UN + LV):
                    if m < UN:
                        top(m)
                    if LT <= m < UN + LT:
                        turned(m - LT)
                    if m >= LV:
                        norm_out(m - LV)
                for t in range(TT):
                    n = b * TT + t
                    eng.wait_ge(b_out, n + 1)
                    eng.tensor_tensor(hrow(n), PS[:, 2 + t % 2, :], hrow(n), ALU.add).then_inc(b_res, 1)
                eng.wait_ge(b_res, b * TT + TT)

        def b_act(eng):
            eng.sem_inc(b_xt, 1)
            eng.sem_inc(b_qt, 3)
            with eng.Fori(0, NB) as b:
                def inputs(t):
                    n = b * TT + t
                    eng.wait_ge(b_xtp, n + 1)
                    if t >= 2:
                        eng.wait_ge(b_pr, n - 1)
                    eng.activation(flat(BXT[:, t % 2, :, :]), PS[:, 0, :], ACT.Copy).then_inc(b_xt, 1)

                def high(t):
                    n = b * TT + t
                    eng.wait_ge(b_rot, n * 4 + 4)
                    eng.activation(VB[:, t, :, 0:HD], PS[:, 2 + 2 * (t % 2), D // 2:].rearrange("p (h d) -> p h d", d=HD),
                                   ACT.Copy).then_inc(b_v, 1)
                    eng.wait_ge(b_sum, n + 1)
                    eng.wait_ge(b_tp, n * NSK + 1)
                    r = RS[:, :].rearrange("p (h d) -> p h d", d=HD)
                    eng.activation(STK[:, 0:NH, 0:2, :], r[:, 0:NH, :].unsqueeze(2).to_broadcast([P, NH, 2, HD]), ACT.Copy)\
                       .then_inc(b_hi, 1)
                    k = STK[:, NH:, :, :].rearrange("p h (x y) d -> p h x y d", y=2)
                    eng.activation(k[:, :, :, 0, :], r[:, NH:, :].unsqueeze(2).to_broadcast([P, KVH, 2, HD]), ACT.Copy)\
                       .then_inc(b_hi, 1)

                def stacks(t):
                    n = b * TT + t
                    for c in range(NSK):
                        eng.wait_ge(b_tp, n * NSK + c + 2)
                        dst = QT1[:, 4 * c:4 * c + 4, :] if c < 4 else KT1[:, 4 * c - NH:4 * c - NH + 4, :]
                        eng.activation(dst[:, :, t * P:(t + 1) * P], PS[:, 5 + c % 3, :].rearrange("p (g q) -> p g q", q=P),
                                       ACT.Copy).then_inc(b_qt, 1)

                inputs(0)
                inputs(1)
                for t in range(TT):
                    if t + 2 < TT:
                        inputs(t + 2)
                    high(t)
                    stacks(t)

                def exps(m):
                    k = b * UN + m
                    eng.wait_ge(b_mx, k + 1)
                    if m >= 3:
                        eng.wait_ge(b_ptp, k - 2)
                    for r in range(2):
                        eng.activation(PE1[:, m % 3, r, :], PS[:, 2 * (m % 2) + r, :], ACT.Exp,
                                       bias=NM1[:, m % 3, r:r + 1]).then_inc(b_e, 1)

                def turned(m):
                    eng.wait_ge(b_ptp, b * UN + m + 1)
                    if m >= 3:
                        eng.wait_ge(b_o, b * UN + m - 2)
                    eng.activation(PT1[:, m % 3, 1, :], PS[:, 5, :], ACT.Copy).then_inc(b_pt1, 1)

                for m in range(UN + LT):
                    if m >= LT:
                        turned(m - LT)
                    if m < UN:
                        exps(m)
                for t in range(TT):
                    n = b * TT + t
                    eng.wait_ge(b_aop, n + 1)
                    eng.activation(flat(AOT[:, t % 2, :, :]), PS[:, t % 2, :], ACT.Copy).then_inc(b_aot, 1)

        def b_pe(eng):
            eng.sem_inc(b_tp, 1)
            eng.wait_ge(b_w, 32)
            eng.wait_ge(b_ones, 1)
            with eng.Fori(0, NB) as b:
                eng.wait_ge(b_res, b * TT)
                def inputs(t):
                    n = b * TT + t
                    eng.wait_ge(b_xn, n + 1)
                    eng.wait_ge(b_xt, n + 1)
                    for k in range(KT):
                        mm = eng.transpose(PS[:, 0, k * P:(k + 1) * P], BXN[:, t % 2, k * P:(k + 1) * P], ident)
                    mm.then_inc(b_xtp, 1)

                def products(t):
                    n = b * TT + t
                    eng.wait_ge(b_xt, n + 2)
                    if t >= 2:
                        eng.wait_ge(b_v, n - 1)
                    for k in range(KT):
                        eng.matmul(PS[:, 1 + 2 * (t % 2), :], BXT[:, t % 2, k, :], WB[:, k, 0:D],
                                   start=(k == 0), stop=(k == KT - 1))
                        mm = eng.matmul(PS[:, 2 + 2 * (t % 2), :], BXT[:, t % 2, k, :], WB[:, k, D:],
                                        start=(k == 0), stop=(k == KT - 1))
                    mm.then_inc(b_pr, 1)

                def stacks(t):
                    n = b * TT + t
                    eng.wait_ge(b_lo, n + 1)
                    for c in range(NSK):
                        eng.wait_ge(b_qt, n * NSK + c + 1)
                        for k in range(4):
                            mm = eng.transpose(PS[:, 5 + c % 3, k * P:(k + 1) * P],
                                               STK[:, 4 * c + k, :, :].rearrange("p x d -> p (x d)").bitcast(F32), ident)
                        mm.then_inc(b_tp, 1)

                inputs(0)
                inputs(1)
                products(0)
                for t in range(TT):
                    if t + 2 < TT:
                        inputs(t + 2)
                    if t + 1 < TT:
                        products(t + 1)
                    stacks(t)
                eng.wait_ge(b_qt, (b * TT + TT) * NSK + 3)
                eng.wait_ge(b_v, b * TT + TT)

                def scores(m):
                    hp, t = divmod(m, TT)
                    k = b * UN + m
                    if m >= 2:
                        eng.wait_ge(b_e, 2 * k - 2)
                    for r in range(2):
                        mm = eng.matmul(PS[:, 2 * (m % 2) + r, :], QT1[:, 2 * hp + r, t * P:(t + 1) * P],
                                        KT1[:, hp, :], start=True, stop=True)
                    mm.then_inc(b_s, 1)

                def turn(m):
                    k = b * UN + m
                    eng.wait_ge(b_e, 2 * k + 2)
                    if m >= 1:
                        eng.wait_ge(b_pt0, k)
                        eng.wait_ge(b_pt1, k)
                    for r in range(2):
                        for c in range(TT):
                            mm = eng.transpose(PS[:, 4 + r, c * P:(c + 1) * P], PE1[:, m % 3, r, c * P:(c + 1) * P], ident)
                    mm.then_inc(b_ptp, 1)

                def values(m):
                    hp, t = divmod(m, TT)
                    k = b * UN + m
                    eng.wait_ge(b_pt0, k + 1)
                    eng.wait_ge(b_pt1, k + 1)
                    if m >= 2:
                        eng.wait_ge(b_ao, k - 1)
                    for r in range(2):
                        for c in range(TT):
                            mm = eng.matmul(PS[:, 6 + m % 2, r * (HD + 1):(r + 1) * (HD + 1)],
                                            PT1[:, m % 3, r, c * P:(c + 1) * P], VB[:, c, hp, :],
                                            start=(c == 0), stop=(c == TT - 1))
                    mm.then_inc(b_o, 1)

                for m in range(UN + LV):
                    if m < UN:
                        scores(m)
                    if LT <= m < UN + LT:
                        turn(m - LT)
                    if m >= LV:
                        values(m - LV)
                eng.wait_ge(b_ao, b * UN + UN)
                for t in range(TT):
                    n = b * TT + t
                    if t >= 2:
                        eng.wait_ge(b_aot, n - 1)
                    for k in range(KT):
                        mm = eng.transpose(PS[:, t % 2, k * P:(k + 1) * P], AO[:, t, k * P:(k + 1) * P], ident)
                    mm.then_inc(b_aop, 1)
                    eng.wait_ge(b_aot, n + 1)
                    if t >= 2:
                        eng.wait_ge(b_res, n - 1)
                    for k in range(KT):
                        mm = eng.matmul(PS[:, 2 + t % 2, :], AOT[:, t % 2, k, :], WO1[:, k, :], start=(k == 0), stop=(k == KT - 1))
                    mm.then_inc(b_out, 1)

        FK = FF // P
        with Arena() as ar:
            CFQ = sb("CFQ", [P, KT, FF], F32R, ar)
            CPQ = sb("CPQ", [P, FK, D], BF16, ar)
            ONES = sb("ONES", [P, P], F32, ar)
            ABS = sb("ABS", [P, 2], F32, ar)
            WSC = sb("WSC", [P, 4], F32, ar)
            with Arena() as tmp:
                CF = sb("CF", [P, KT * FF], F32, tmp)
                CP = sb("CP", [P, FK * D], F32, tmp)
            GXN = sb("GXN", [P, 2, D], F32, ar)
            GXH = sb("GXH", [P, 2, D], F32R, ar)
            GXL = sb("GXL", [P, 2, D], F32R, ar)
            GV = sb("GV", [P, 2, 8], F32, ar)
            GST = sb("GST", [P, 2, 8], F32, ar)
            GR1 = sb("GR1", [P, 2, FF], F32, ar)
            GY = sb("GY", [P, FF], F32, ar)
            GQ = sb("GQ", [P, 2, FF], BF16, ar)
            GT = sb("GT", [P, 2, FK, P], BF16, ar)

        g_w = sem("g_w"); g_abs = sem("g_abs"); g_sum = sem("g_sum"); g_sc = sem("g_sc"); g_t = sem("g_t"); g_one = sem("g_one")
        g_st = sem("g_st"); g_pv = sem("g_pv"); g_rstd = sem("g_rstd"); g_xn = sem("g_xn"); g_xtp = sem("g_xtp"); g_hi = sem("g_hi")
        g_lo = sem("g_lo"); g_mm = sem("g_mm"); g_r = sem("g_r"); g_mx = sem("g_mx"); g_c = sem("g_c"); g_y = sem("g_y"); g_q = sem("g_q")
        g_tp = sem("g_tp"); g_ta = sem("g_ta"); g_tb = sem("g_tb"); g_op = sem("g_op"); g_res = sem("g_res"); g_p1 = sem("g_p1")
        G_C, G_ST = 4, 5

        def gw_sync(eng):
            eng.dma_start(CF[:, :].rearrange("p (k n) -> p k n", k=KT), a["c_fc"].rearrange("(k p) n -> p k n", p=P))\
               .then_inc(g_w, 16)
            eng.dma_start(CP[:, :].rearrange("p (k n) -> p k n", k=FK), a["c_projT"].rearrange("(k p) n -> p k n", p=P))\
               .then_inc(g_w, 16)

        def gw_dve(eng):
            eng.memset(ONES[:, :], 1.0).then_inc(g_one, 1)
            eng.wait_ge(g_w, 32)
            for i, w in enumerate((CF, CP)):
                eng.tensor_reduce(ABS[:, i:i + 1], w[:, :], AX, ALU.add, apply_absolute_value=True).then_inc(g_abs, 1)
            eng.wait_ge(g_sum, 1)
            eng.tensor_scalar(WSC[:, 0:2], PS[:, 0, 0:2], 1.0 / (D * FF), 1e-5, ALU.mult, ALU.max).then_inc(g_sc, 1)
            eng.wait_ge(g_sc, 1)
            eng.reciprocal(WSC[:, 2:4], WSC[:, 0:2]).then_inc(g_sc, 1)
            eng.wait_ge(g_sc, 2)
            for i, (w, q) in enumerate(((CF, flat(CFQ[:, :, :])), (CP, flat(CPQ[:, :, :])))):
                eng.tensor_scalar(w[:, :], w[:, :], WSC[:, 2 + i:3 + i], MAGIC, ALU.mult, ALU.add).then_inc(g_t, 1)
                eng.wait_ge(g_t, 3 * i + 1)
                eng.tensor_scalar(w[:, :], w[:, :], MAGIC, -1.0, ALU.subtract, ALU.max).then_inc(g_t, 1)
                eng.wait_ge(g_t, 3 * i + 2)
                eng.tensor_scalar(q, w[:, :], 1.0, None, ALU.min).then_inc(g_t, 1)
            eng.wait_ge(g_t, 6)

        def gw_pe(eng):
            eng.wait_ge(g_abs, 2)
            eng.wait_ge(g_one, 1)
            eng.matmul(PS[:, 0, 0:2], ONES[:, :], ABS[:, :], start=True, stop=True).then_inc(g_sum, 1)

        def g_dve(eng):
            def front(n, u):
                eng.bn_stats(GST[:, u, 0:6], hrow(n)).then_inc(g_st, 1)
                eng.wait_ge(g_st, n * 2 + 1)
                eng.sem_inc(s_alone, 1)
                eng.bn_aggr(GV[:, u, V_MEAN:V_VAR + 1], GST[:, u:u + 1, 0:6]).then_inc(g_st, 1)
                eng.wait_ge(g_rstd, n + 1)
                eng.tensor_scalar(GXN[:, u, :], hrow(n), GV[:, u, V_MEAN:V_MEAN + 1], GV[:, u, V_RSTD:V_RSTD + 1],
                                  ALU.subtract, ALU.mult).then_inc(g_xn, 1)

            def low(n, u):
                eng.wait_ge(g_hi, n + 1)
                eng.tensor_tensor(GXL[:, u, :], PS[:, 0, :], GXH[:, u, :].bitcast(F32), ALU.subtract).then_inc(g_lo, 1)

            def peak(n, u):
                eng.wait_ge(g_r, 4 * n + 4)
                eng.tensor_reduce(GV[:, u, V_AM:V_AM + 1], GR1[:, u, :], AX, ALU.max).then_inc(g_mx, 1)

            def rounded(n, u):
                eng.wait_ge(g_y, n + 1)
                eng.tensor_scalar(GQ[:, u, :], GY[:, :], MAGIC, MAGIC, ALU.add, ALU.subtract).then_inc(g_q, 1)

            def turned(n, u):
                eng.wait_ge(g_tp, n + 1)
                eng.tensor_copy(flat(GT[:, u, 0:8, :]), PS[:, 5, :].bitcast(BF16)).then_inc(g_ta, 1)

            def fin(n, u):
                eng.wait_ge(g_op, n + 1)
                eng.scalar_tensor_tensor(hrow(n), PS[:, 7, :], GV[:, u, G_ST:G_ST + 1], hrow(n), ALU.mult, ALU.add)\
                   .then_inc(g_res, 1)

            front(0, 0)
            low(0, 0)
            two_by_two(eng,
                       lambda n, u: (front(n + 1, 1 - u), peak(n, u), low(n + 1, 1 - u), rounded(n, u)),
                       lambda n, u: (front(n + 1, 1 - u), turned(n - 1, 1 - u), peak(n, u), low(n + 1, 1 - u),
                                     fin(n - 1, 1 - u), rounded(n, u)),
                       lambda n, u: (turned(n - 1, 1 - u), peak(n, u), fin(n - 1, 1 - u), rounded(n, u)))
            turned(NT - 1, 1)
            fin(NT - 1, 1)

        def g_pool(eng):
            def rstd(n, u):
                eng.wait_ge(g_st, n * 2 + 2)
                eng.sem_inc(s_alone, 1)
                eng.tensor_scalar(GV[:, u, V_RSTD:V_RSTD + 1], GV[:, u, V_VAR:V_VAR + 1], 1e-5, 1.0, ALU.add, ALU.mult)\
                   .then_inc(g_pv, 1)
                eng.wait_ge(g_pv, n + 1)
                eng.tensor_tensor(GV[:, u, V_RSTD:V_RSTD + 1], GV[:, u, V_RSTD:V_RSTD + 1], NHALF[:, 0:1], ALU.pow)\
                   .then_inc(g_rstd, 1)

            def token_scales(n, u):
                v = GV[:, u, :]
                eng.wait_ge(g_mx, n + 1)
                eng.tensor_tensor(v[:, V_AM:V_AM + 1], v[:, V_AM:V_AM + 1], v[:, V_AM:V_AM + 1], ALU.mult).then_inc(g_p1, 1)
                eng.wait_ge(g_p1, n * 4 + 1)
                eng.sem_inc(s_alone, 1)
                eng.tensor_scalar(v[:, V_AM:V_AM + 1], v[:, V_AM:V_AM + 1], 1e-5, None, ALU.max).then_inc(g_p1, 1)
                eng.wait_ge(g_p1, n * 4 + 2)
                eng.sem_inc(s_alone, 1)
                eng.tensor_scalar(v[:, V_AM:V_AM + 1], v[:, V_AM:V_AM + 1], 1.0 / 255.0, 1.0, ALU.mult, ALU.mult)\
                   .then_inc(g_p1, 1)
                eng.wait_ge(g_p1, n * 4 + 3)
                eng.tensor_tensor(v[:, G_ST:G_ST + 1], v[:, V_AM:V_AM + 1], WSC[:, 1:2], ALU.mult).then_inc(g_p1, 1)
                eng.tensor_tensor(v[:, G_C:G_C + 1], v[:, V_AM:V_AM + 1], NHALF[:, 0:1], ALU.pow).then_inc(g_c, 1)

            rstd(0, 0)
            two_by_two(eng,
                       lambda n, u: (rstd(n + 1, 1 - u), token_scales(n, u)),
                       lambda n, u: (rstd(n + 1, 1 - u), token_scales(n, u)),
                       lambda n, u: (token_scales(n, u),))

        def g_act(eng):
            def high(n, u):
                eng.wait_ge(g_xtp, n + 1)
                eng.activation(GXH[:, u, :], PS[:, 0, :], ACT.Copy).then_inc(g_hi, 1)

            def relu(n, u):
                for c in range(4):
                    eng.wait_ge(g_mm, 4 * n + c + 1)
                    eng.activation(GR1[:, u, c * 512:(c + 1) * 512], PS[:, 1 + c, :], ACT.Relu, scale=WSC[:, 0:1])\
                       .then_inc(g_r, 1)

            def squared(n, u):
                eng.wait_ge(g_c, n + 1)
                eng.wait_ge(g_q, n)
                eng.activation(GY[:, :], GR1[:, u, :], ACT.Square, scale=GV[:, u, G_C:G_C + 1]).then_inc(g_y, 1)

            def turned(n, u):
                eng.wait_ge(g_tp, n + 1)
                eng.activation(flat(GT[:, u, 8:16, :]), PS[:, 6, :].bitcast(BF16), ACT.Copy).then_inc(g_tb, 1)

            high(0, 0)
            two_by_two(eng,
                       lambda n, u: (relu(n, u), high(n + 1, 1 - u), squared(n, u)),
                       lambda n, u: (relu(n, u), turned(n - 1, 1 - u), high(n + 1, 1 - u), squared(n, u)),
                       lambda n, u: (relu(n, u), turned(n - 1, 1 - u), squared(n, u)))
            turned(NT - 1, 1)

        def g_pe(eng):
            def xt(n, u):
                eng.wait_ge(g_xn, n + 1)
                eng.wait_ge(g_lo, n)
                for k in range(KT):
                    mm = eng.transpose(PS[:, 0, k * P:(k + 1) * P], GXN[:, u, k * P:(k + 1) * P], ident)
                mm.then_inc(g_xtp, 1)

            def up(n, u):
                eng.wait_ge(g_lo, n + 1)
                for c in range(4):
                    if not (isinstance(n, int) and n == 0):
                        eng.wait_ge(g_r, 4 * n - 3 + c)
                    for k in range(KT):
                        for x in (GXH, GXL):
                            mm = eng.matmul(PS[:, 1 + c, :], x[:, u, k * P:(k + 1) * P], CFQ[:, k, c * 512:(c + 1) * 512],
                                            start=(k == 0 and x is GXH), stop=(k == KT - 1 and x is GXL))
                    mm.then_inc(g_mm, 1)

            def down(n, u):
                eng.wait_ge(g_q, n + 1)
                eng.wait_ge(g_ta, n)
                eng.wait_ge(g_tb, n)
                for k in range(FK):
                    mm = eng.transpose(PS[:, 5 + k // 8, (k % 8) * 64:(k % 8 + 1) * 64].bitcast(BF16),
                                       GQ[:, u, k * P:(k + 1) * P], IDB[:, :])
                mm.then_inc(g_tp, 1)

            def proj(n, u):
                eng.wait_ge(g_ta, n + 1)
                eng.wait_ge(g_tb, n + 1)
                eng.wait_ge(g_res, n)
                for k in range(FK):
                    mm = eng.matmul(PS[:, 7, :], GT[:, u, k, :], CPQ[:, k, :], start=(k == 0), stop=(k == FK - 1))
                mm.then_inc(g_op, 1)

            eng.wait_ge(g_t, 6)
            xt(0, 0)
            two_by_two(eng,
                       lambda n, u: (up(n, u), xt(n + 1, 1 - u)),
                       lambda n, u: (down(n - 1, 1 - u), up(n, u), xt(n + 1, 1 - u), proj(n - 1, 1 - u)),
                       lambda n, u: (down(n - 1, 1 - u), up(n, u), proj(n - 1, 1 - u)))
            down(NT - 1, 1)
            proj(NT - 1, 1)

        block = ctx.enter_context(nc.Block())

        @block.sync
        def _(eng):
            sync_eng[0] = eng
            e_sync(eng)
            w_sync(eng)
            barrier(eng, clears=True)
            a_sync(eng)
            barrier(eng)
            if "F" in stages:
                fw_sync(eng)
                barrier(eng)
                barrier(eng)
            if "B" in stages:
                b_sync(eng)
                barrier(eng)
            if "G" in stages:
                gw_sync(eng)
                barrier(eng)
                barrier(eng)
            eng.dma_start(out.rearrange("b (t p) n -> p (b t) n", p=P), H[:, :, :]).then_inc(s_ids, 16)
            eng.wait_ge(s_ids, 48)

        @block.gpsimd
        def _(eng):
            e_pool(eng)
            barrier(eng)
            a_pool(eng)
            barrier(eng)
            if "F" in stages:
                barrier(eng)
                f_pool(eng)
                barrier(eng)
            if "B" in stages:
                b_pool(eng)
                barrier(eng)
            if "G" in stages:
                barrier(eng)
                g_pool(eng)
                barrier(eng)

        @block.scalar
        def _(eng):
            e_act(eng)
            w_act(eng)
            barrier(eng)
            a_act(eng)
            barrier(eng)
            if "F" in stages:
                barrier(eng)
                f_act(eng)
                barrier(eng)
            if "B" in stages:
                b_act(eng)
                barrier(eng)
            if "G" in stages:
                barrier(eng)
                g_act(eng)
                barrier(eng)

        @block.vector
        def _(eng):
            e_dve(eng)
            w_dve(eng)
            barrier(eng)
            a_dve(eng)
            barrier(eng)
            if "F" in stages:
                fw_dve(eng)
                barrier(eng)
                f_dve(eng)
                barrier(eng)
            if "B" in stages:
                b_dve(eng)
                barrier(eng)
            if "G" in stages:
                gw_dve(eng)
                barrier(eng)
                g_dve(eng)
                barrier(eng)

        @block.tensor
        def _(eng):
            e_pe(eng)
            w_pe(eng)
            barrier(eng)
            a_pe(eng)
            barrier(eng)
            if "F" in stages:
                barrier(eng)
                f_pe(eng)
                barrier(eng)
            if "B" in stages:
                b_pe(eng)
                barrier(eng)
            if "G" in stages:
                gw_pe(eng)
                barrier(eng)
                g_pe(eng)
                barrier(eng)


NAMES = {"L0_tok_ts_w": "ts_w", "L0_tok_pos_w": "pos_w", "L0_attn_q_norm_w": "q_norm_w", "L0_attn_wq_b": "wq_b",
         "L0_attn_kv_norm_w": "kv_norm_w", "L0_attn_wkv_b": "wkv_b",
         "L0_ffn_w_gate_up": "w_gate_up", "L0_ffn_w_down": "w_down", "L1_attn_wo": "wo1", "L1_ffn_c_fc": "c_fc"}


def layouts(inputs):
    g = {v: np.ascontiguousarray(inputs[k]) for k, v in NAMES.items()}
    x = np.asarray(inputs["x"])
    g["x"] = np.ascontiguousarray(x)
    nxt = np.concatenate([x[:, 1:], x[:, -1:]], 1).reshape(NT * 4, 32).T
    g["ext"] = np.ascontiguousarray(np.concatenate([nxt] * 4, 0))
    g["woT"] = np.ascontiguousarray(np.asarray(inputs["L0_attn_wo"]).T)
    g["waT"] = np.ascontiguousarray(np.concatenate([inputs["L0_attn_wq_a"], inputs["L0_attn_wkv_a"]], 0).T)
    wpe = np.asarray(inputs["L0_attn_wq_b"]).reshape(NH, LORA + ROPE, QLORA)[:, LORA:].transpose(0, 2, 1)
    g["wpe"] = np.ascontiguousarray(np.concatenate([wpe, wpe[:, :, ROPE // 2:], wpe[:, :, :ROPE // 2]], 2))
    g["w_gate_upT"] = np.ascontiguousarray(np.asarray(inputs["L0_ffn_w_gate_up"]).T)
    g["w_downT"] = np.ascontiguousarray(np.asarray(inputs["L0_ffn_w_down"]).T)
    g["wqkv"] = np.ascontiguousarray(np.concatenate([inputs["L1_attn_wq"], inputs["L1_attn_wk"], inputs["L1_attn_wv"]], 1))
    g["c_projT"] = np.ascontiguousarray(np.asarray(inputs["L1_ffn_c_proj"]).T)
    g["consts"] = constants()
    return g


def kernel(**inputs):
    import concourse.bacc as bacc
    from concourse.bass_utils import run_bass_kernel_spmd

    nc = bacc.Bacc("TRN2", target_bir_lowering=False, num_devices=1)
    arrays, aps = {}, {}
    for name, v in layouts(inputs).items():
        arrays["in_" + name] = v
        aps[name] = nc.dram_tensor("in_" + name, v.shape, mybir.dt.from_np(v.dtype), kind="ExternalInput").ap()
    out = nc.dram_tensor("out_0", (NB, S, D), F32, kind="ExternalOutput").ap()
    tower_kernel(nc, aps, out)
    r = run_bass_kernel_spmd(nc, [arrays], core_ids=[0])
    return r.results[0]["out_0"]
```

```python
from contextlib import ExitStack

import numpy as np
import concourse.bass as bass
from concourse import mybir

F32 = mybir.dt.float32
F32R = mybir.dt.float32r
BF16 = mybir.dt.bfloat16
I32 = mybir.dt.int32
ALU = mybir.AluOpType
ACT = mybir.ActivationFunctionType
AX = mybir.AxisListType.X

P = 128
NB = 4
S = 512
D = 512
TT = S // P
NT = NB * TT
KT = D // P
NH = 16
LORA = 128
QLORA = 384
QK = QLORA // P
ROPE = 64
QKV0 = QLORA + LORA + ROPE
SCALE0 = float(LORA + ROPE) ** -0.5
INTER = 1408
FF = 2048
HD = 32
SCALE1 = float(HD) ** -0.5
BUCKETS = 32
BPP = 4
PASSES = BUCKETS // BPP
MAGIC = 12582912.0

C_ID, C_MASK, C_ROPEQ, C_ROPEK, C_RQ1, C_RK1, C_ID32, C_GRP, C_FLIP, C_N = 0, 128, 256, 768, 1280, 1536, 1792, 1824, 1825, 1953


def constants():
    c = np.zeros((P, C_N), np.float32)
    r = np.arange(P)
    c[:, C_ID:C_ID + P] = np.eye(P)
    c[:, C_MASK:C_MASK + P] = np.where(r[None, :] <= r[:, None], 0.0, -1e30)
    pos = np.arange(S, dtype=np.float32)
    inv = (1.0 / 10000.0 ** (np.arange(0, ROPE, 2, dtype=np.float32) / ROPE)).astype(np.float32)
    ang = (pos[:, None] * inv[None, :]).astype(np.float32)
    cos, sin = np.cos(ang), np.sin(ang)
    c[:, C_ROPEQ:C_ROPEQ + S] = np.concatenate([cos, cos, -sin, sin], 1).T
    k = np.concatenate([cos, cos, -sin, sin], 1).reshape(TT, P, 2 * ROPE)
    c[:, C_ROPEK:C_ROPEK + TT * 2 * ROPE] = k.transpose(1, 0, 2).reshape(P, -1)
    inv = (1.0 / 10000.0 ** (np.arange(0, HD, 2, dtype=np.float32) / HD)).astype(np.float32)
    ang = (pos[:, None] * inv[None, :]).astype(np.float32)
    cos, sin = np.cos(ang), np.sin(ang)
    t = np.concatenate([np.repeat(cos, 2, 1), np.stack([-sin, sin], -1).reshape(S, HD)], 1)
    t = t.reshape(TT, P, 2 * HD).transpose(1, 0, 2).reshape(P, -1)
    c[:, C_RK1:C_RK1 + TT * 2 * HD] = t
    c[:, C_RQ1:C_RQ1 + TT * 2 * HD] = t * SCALE1
    c[:, C_ID32:C_ID32 + 32] = (r[:, None] % 32 == np.arange(32)[None, :])
    c[:, C_GRP] = r // 32
    c[:, C_FLIP:C_FLIP + P] = np.eye(P)[::-1]
    return c


def tower_kernel(nc, a, out, stages="FBG"):
    ctx = ExitStack()
    with ctx:
        def sb(name, shape, dt=F32, c=ctx):
            return c.enter_context(nc.sbuf_tensor(name, shape, dt))

        first = []

        first_sems = ExitStack()

        def sem(name, c=ctx):
            return c.enter_context(nc.semaphore(name))

        def sem1(name):
            first.append(sem(name, first_sems))
            return first[-1]

        PS = ctx.enter_context(nc.psum_tensor("PS", [P, 8, 512], F32))
        H = sb("H", [P, NT, D])
        CST = sb("CST", [P, C_N])
        IDB = sb("IDB", [P, P], BF16)
        MASKB = sb("MASKB", [P, P], BF16)
        STAT = sb("STAT", [P, TT, 6])
        MV = sb("MV", [P, TT, 2])
        RSTD = sb("RSTD", [P, TT])
        VEPS = sb("VEPS", [P, TT])
        NHALF = sb("NHALF", [P, 2 * TT])
        LNS = sb("LNS", [P, 8, NT])
        ident = CST[:, C_ID:C_ID + P]

        QNW = sb("QNW", [P, QK])
        KVW = sb("KVW", [P, 1])
        QNS = sb("QNS", [P, QK], F32)

        s_const = sem("s_const")
        s_bar = sem("s_bar")
        s_open = sem("s_open")
        s_alone = sem("s_alone")
        s_pre = sem("s_pre")

        def flat(ap):
            return ap.rearrange("p a n -> p (a n)")

        bars, sync_eng = {}, [None]

        def barrier(eng, clears=False):
            k = bars.get(id(eng), 0) + 1
            bars[id(eng)] = k
            eng.drain().then_inc(s_bar, 1)
            if eng is sync_eng[0]:
                eng.wait_ge(s_bar, 5 * k)
                if clears:
                    for x in first:
                        eng.sem_clear(x)
                eng.sem_inc(s_open, 1)
            eng.wait_ge(s_open, k)

        wqk_scr = nc.dram_tensor("wqk_scr", [NH, P, QK, LORA], F32, kind="Internal").ap()

        class Arena:
            def __enter__(self):
                self.c = ExitStack()
                return self.c

            def __exit__(self, *x):
                self.c.close()

        arena_w = ExitStack()
        WVO = sb("WVO", [P, NH, D], c=arena_w)
        with Arena() as ar:
            XB = sb("XB", [P, NB, S], I32, ar)
            EXT = sb("EXT", [P, NT * 4], I32, ar)
            DIFF = sb("DIFF", [P, 2, 4 * S], I32, ar)
            MAG = sb("MAG", [P, 2, 4 * S], F32, ar)
            EXPO = sb("EXPO", [P, 2, 4 * S], I32, ar)
            EXB = sb("EXB", [P, 2, 4 * S], BF16, ar)
            MSK = sb("MSK", [P, 8, 4 * S], BF16, ar)
            POSB = sb("POSB", [P, TT, S], F32, ar)
            POSF = sb("POSF", [P, TT, S], F32, ar)
            TSC = sb("TSC", [P, PASSES], F32, ar)
            TSH = sb("TSH", [P, 3, PASSES], BF16, ar)
            TSF = sb("TSF", [P, 3, PASSES], F32, ar)
            TSR = sb("TSR", [P, 2, PASSES], F32, ar)
            TAB = sb("TAB", [P, 3, PASSES, 32], BF16, ar)
            WQN = sb("WQN", [P, 2, QLORA], F32, ar)
            WKV = sb("WKV", [P, 2, 2, LORA], F32, ar)
            WOT = sb("WOT", [P, 2, D], F32, ar)
            WQKE = sb("WQKE", [P, 2, QK, LORA], F32, ar)

        s_ids = sem("s_ids"); s_norm = sem1("s_norm"); s_pos = sem1("s_pos"); s_ts = sem1("s_ts")
        s_tab = sem1("s_tab")
        diff_ready = sem1("diff_ready"); mag_ready = sem1("mag_ready")
        expo_ready = sem1("expo_ready"); exb_ready = sem1("exb_ready"); mask_ready = sem1("mask_ready")
        mask_used = sem1("mask_used"); h_ready = sem1("h_ready")
        pos_ps = sem1("pos_ps"); pos_ready = sem1("pos_ready")
        w_loaded = [sem1("w_loaded0"), sem1("w_loaded1")]
        wqk_ps = sem1("wqk_ps"); wqk_sb = sem1("wqk_sb"); wqk_out = [sem1("wqk_out0"), sem1("wqk_out1")]
        wvo_ps = sem1("wvo_ps"); wvo_sb = sem1("wvo_sb")

        def e_tables(eng):
            for t in range(TT):
                src = bass.AP(a["pos_w"].tensor, S - P * (t + 1), [[1, P], [1, S]])
                eng.dma_start(POSF[:, t, :], src).then_inc(s_pos, 16)
            for g in range(4):
                src = bass.AP(a["ts_w"].tensor, g, [[0, 32], [BPP, PASSES]])
                with nc.allow_non_contiguous_dma(reason="32 table entries"):
                    eng.dma_start(TSC[32 * g:32 * g + 32, :], src).then_inc(s_ts, 16)
            with nc.allow_non_contiguous_dma(reason="norm weights"):
                eng.dma_start(QNW[:, :], a["q_norm_w"].rearrange("(k p) -> p k", p=P)).then_inc(s_norm, 16)
                eng.dma_start(KVW[:, :], a["kv_norm_w"].rearrange("(p o) -> p o", o=1)).then_inc(s_norm, 16)

        def e_sync(eng):
            for u in range(2):
                eng.sem_inc(wqk_out[u], 16)
            eng.dma_start(CST[:, :], a["consts"]).then_inc(s_const, 16)
            eng.dma_start(XB[:, :, :].rearrange("p b n -> p (b n)"),
                          a["x"].rearrange("(o b) n -> o (b n)", o=1).to_broadcast([P, NB * S])).then_inc(s_ids, 16)
            eng.dma_start(EXT[:, :], a["ext"]).then_inc(s_ids, 16)

        def e_pool(eng):
            eng.memset(NHALF[:, :], -0.5).then_inc(s_pre, 1)
            eng.wait_ge(s_ids, 32)
            with eng.Fori(0, NB) as b:
                for t in range(TT):
                    n = b * TT + t
                    eng.wait_ge(mag_ready, n + 1)
                    eng.tensor_tensor(
                        DIFF[:, t % 2, :].rearrange("p (q n) -> p q n", q=4),
                        EXT[:, bass.ds(n * 4, 4)].unsqueeze(2).to_broadcast([P, 4, S]),
                        XB[:, bass.ds(b, 1), :].to_broadcast([P, 4, S]), ALU.subtract).then_inc(diff_ready, 1)

        def batches(body):
            def of(eng):
                with eng.Fori(0, NB - 1) as b:
                    for t in range(TT):
                        body(b * TT + t, t, b, None)
                for t in range(TT):
                    body((NB - 1) * TT + t, t, NB - 1, (NB - 1) * TT + t)
            return of

        def e_act(eng):
            e_tables(eng)
            eng.sem_inc(mag_ready, 2)
            eng.sem_inc(wqk_sb, 2)
            eng.sem_inc(wvo_sb, 2)

            def magnitude(n, u):
                eng.wait_ge(diff_ready, n + 1)
                eng.wait_ge(expo_ready, n + 1)
                eng.activation(MAG[:, u, :], DIFF[:, u, :], ACT.Abs).then_inc(mag_ready, 1)

            def exponent(n, u):
                eng.wait_ge(expo_ready, n + 3)
                eng.wait_ge(mask_ready, (n + 1) * PASSES)
                eng.activation(EXB[:, u, :], EXPO[:, u, :], ACT.Relu, bias=-127.0).then_inc(exb_ready, 1)

            def w0_head(h, u, j):
                eng.wait_ge(wqk_ps, h + 1)
                eng.wait_ge(wqk_out[u], j * 16 + 16)
                eng.activation(WQKE[:, u, :, :].rearrange("p k c -> p (k c)"), PS[:, 2 + u, 0:QLORA],
                               ACT.Copy).then_inc(wqk_sb, 1)
                eng.wait_ge(wvo_ps, h + 3)
                eng.activation(flat(WVO[:, bass.ds(h, 1), :]), PS[:, 4 + u, :], ACT.Copy, scale=KVW[:, 0:1]).then_inc(wvo_sb, 1)

            magnitude(0, 0)
            magnitude(1, 1)
            exponent(0, 0)
            eng.wait_ge(s_norm, 32)

            def step(n, t, b, last):
                if last is None or last + 2 < NT:
                    magnitude(n + 2, t % 2)
                if last is None or last + 1 < NT:
                    exponent(n + 1, 1 - t % 2)
                w0_head(n, t % 2, b * (TT // 2) + t // 2)
            batches(step)(eng)

        def e_dve(eng):
            eng.sem_inc(expo_ready, 2)
            eng.sem_inc(mask_ready, 2 * PASSES)
            eng.sem_inc(h_ready, 2)
            eng.wait_ge(s_const, 16)
            eng.tensor_copy(IDB[:, :], ident).then_inc(s_pre, 1)
            eng.tensor_copy(MASKB[:, :], CST[:, C_MASK:C_MASK + P]).then_inc(s_pre, 1)
            for t in range(TT):
                eng.wait_ge(pos_ps, t + 1)
                eng.tensor_copy(POSB[:, t, :], PS[:, 4 + t, :]).then_inc(pos_ready, 1)
            eng.wait_ge(pos_ready, TT)
            def expo(n, u):
                eng.wait_ge(mag_ready, n + 3)
                eng.tensor_scalar(EXPO[:, u, :], MAG[:, u, :].bitcast(I32), 23, None,
                                  ALU.logical_shift_right).then_inc(expo_ready, 1)

            expo(0, 0)
            eng.wait_ge(s_ts, 64)
            k = 0
            for part in range(3):
                src = TSC[:, :] if part == 0 else TSR[:, part - 1, :]
                eng.tensor_copy(TSH[:, part, :], src).then_inc(s_tab, 1)
                eng.wait_ge(s_tab, k + 1)
                eng.tensor_copy(TSF[:, part, :], TSH[:, part, :]).then_inc(s_tab, 1)
                eng.wait_ge(s_tab, k + 2)
                k += 2
                if part < 2:
                    eng.tensor_tensor(TSR[:, part, :], src, TSF[:, part, :], ALU.subtract).then_inc(s_tab, 1)
                    k += 1
                    eng.wait_ge(s_tab, k)
            for part in range(3):
                eng.tensor_tensor(TAB[:, part, :, :], CST[:, C_ID32:C_ID32 + 32].unsqueeze(1).to_broadcast([P, PASSES, 32]),
                                  TSF[:, part, :].unsqueeze(2).to_broadcast([P, PASSES, 32]), ALU.mult).then_inc(s_tab, 1)

            def masks(n, u, passes):
                for q in passes:
                    if q == 0:
                        eng.wait_ge(exb_ready, n + 1)
                    eng.wait_ge(mask_used, n * PASSES + q + 1)
                    eng.tensor_scalar(MSK[:, q, :], EXB[:, u, :], CST[:, C_GRP:C_GRP + 1], float(BPP * q),
                                      ALU.subtract, ALU.is_equal).then_inc(mask_ready, 1)

            def add_pos(n, t):
                eng.wait_ge(mask_used, n * PASSES + 2 * PASSES)
                eng.tensor_tensor(flat(H[:, bass.ds(n, 1), :]), PS[:, t % 2, :], POSB[:, t, :],
                                  ALU.add).then_inc(h_ready, 1)

            early = PASSES // 4
            masks(0, 0, range(early))

            def step(n, t, b, last):
                more = last is None or last + 1 < NT
                if more:
                    expo(n + 1, 1 - t % 2)
                masks(n, t % 2, range(early, PASSES))
                if more:
                    masks(n + 1, 1 - t % 2, range(early))
                add_pos(n, t)
            batches(step)(eng)

        def e_pe(eng):
            eng.sem_inc(mask_used, PASSES)
            eng.sem_inc(wvo_ps, 2)
            eng.wait_ge(s_const, 16)
            eng.wait_ge(s_pos, 64)
            for t in range(TT):
                eng.matmul(PS[:, 4 + t, :], CST[:, C_FLIP:C_FLIP + P], POSF[:, t, :], start=True, stop=True)\
                   .then_inc(pos_ps, 1)
            eng.wait_ge(pos_ready, TT)
            eng.wait_ge(s_tab, 11)
            eng.wait_ge(s_pre, 3)

            def w0_head(h, u, j):
                eng.wait_ge(w_loaded[u], j * 48 + 48)
                eng.wait_ge(wqk_sb, h + 1)
                eng.wait_ge(wvo_sb, h + 1)
                for k in range(QK):
                    mm = eng.matmul(PS[:, 2 + u, k * P:(k + 1) * P], WQN[:, u, k * P:(k + 1) * P],
                                    WKV[:, u, 0, :], start=True, stop=True)
                mm.then_inc(wqk_ps, 1)
                eng.matmul(PS[:, 4 + u, :], WKV[:, u, 1, :], WOT[:, u, :], start=True, stop=True)\
                   .then_inc(wvo_ps, 1)

            def step(n, t, b, last):
                for q in range(PASSES):
                    eng.wait_ge(mask_ready, n * PASSES + q + 1 + 2 * PASSES)
                    if q == 0:
                        eng.wait_ge(h_ready, n + 1)
                    for part in range(3):
                        for r in range(4):
                            mm = eng.matmul(PS[32 * r:32 * r + 32, t % 2, :], TAB[:, part, q, :],
                                            MSK[:, q, r * S:(r + 1) * S],
                                            start=(q == 0 and part == 0), stop=(q == PASSES - 1 and part == 2))
                    mm.then_inc(mask_used, 1)
                w0_head(n, t % 2, b * (TT // 2) + t // 2)
            batches(step)(eng)

        def w_sync(eng):
            wq = a["wq_b"].rearrange("(h d) k -> h d k", h=NH)
            wkv = a["wkv_b"].rearrange("(h u d) k -> h d u k", h=NH, u=2)
            wot = a["woT"].rearrange("(h d) n -> h d n", h=NH)

            def load(h, u):
                eng.wait_ge(wvo_ps, h + 1)
                eng.dma_start(WQN[:, u, :], wq[bass.ds(h, 1), 0:P, :].rearrange("a d k -> (a d) k"))\
                   .then_inc(w_loaded[u], 16)
                eng.dma_start(WKV[:, u, :, :], wkv[bass.ds(h, 1)].rearrange("a d u k -> (a d) u k"))\
                   .then_inc(w_loaded[u], 16)
                eng.dma_start(WOT[:, u, :], wot[bass.ds(h, 1)].rearrange("a d n -> (a d) n"))\
                   .then_inc(w_loaded[u], 16)

            def store(h, u):
                eng.wait_ge(wqk_sb, h + 3)
                eng.dma_start(wqk_scr[bass.ds(h, 1)].rearrange("a p k c -> (a p) k c"), WQKE[:, u, :, :])\
                   .then_inc(wqk_out[u], 16)

            load(0, 0)
            with eng.Fori(0, NH // 2 - 1) as j:
                load(j * 2 + 1, 1)
                store(j * 2, 0)
                load(j * 2 + 2, 0)
                store(j * 2 + 1, 1)
            load(NH - 1, 1)
            store(NH - 2, 0)
            store(NH - 1, 1)
            for u in range(2):
                eng.wait_ge(wqk_out[u], 16 * (NH // 2 + 1))

        def hrow(n):
            return flat(H[:, bass.ds(n, 1), :])

        def pipeline(eng, step, lag, turn=2):
            def at(k):
                step(k, k % turn, lambda d: 0 <= k + d < NT)
            start = (lag + turn - 1) // turn * turn
            turns = (NT - 2 - start) // turn
            for k in range(start):
                at(k)
            with eng.Fori(0, turns) as j:
                for v in range(turn):
                    step(j * turn + start + v, v, lambda d: True)
            for k in range(start + turn * turns, NT + lag):
                at(k)

        QH, QLO, CH_, CLO, KH, KLO, VH, VLO, NOP = 0, 3, 6, 7, 8, 9, 10, 11, 12
        ops_scr = nc.dram_tensor("ops_scr", [NT, P, NOP, P], F32, kind="Internal").ap()
        arena_h = ExitStack()
        OPS = sb("OPS", [P, 2, NOP, S], F32R, arena_h)
        WQ = sb("WQ", [P, 2, QK, 2 * P], F32, arena_h)
        WH = sb("WH", [P, 2, QK, 2 * P], F32R, arena_h)
        WL = sb("WL", [P, 2, QK, 2 * P], F32R, arena_h)
        with Arena() as ar:
            WA = sb("WA", [P, KT, QKV0], F32, ar)
            STL = sb("STL", [P, 2, 6], F32, ar)
            MVL = sb("MVL", [P, 2, 2], F32, ar)
            RSL = sb("RSL", [P, 2, 2], F32, ar)
            XN = sb("XN", [P, 2, D], F32, ar)
            XNT = sb("XNT", [P, 2, KT, P], F32, ar)
            RAW = sb("RAW", [P, 2, QKV0], F32, ar)
            SQ = sb("SQ", [P, 2, QLORA], F32, ar)
            SSQ = sb("SSQ", [P, 2, 2], F32, ar)
            MSQ = sb("MSQ", [P, 2, 2], F32, ar)
            RMS = sb("RMS", [P, 2, 2], F32, ar)
            KR = sb("KR", [P, 2, 2, ROPE], F32, ar)
            QL = sb("QL", [P, 2, QLORA], F32, ar)
            CN = sb("CN", [P, 2, LORA], F32, ar)
            KP = sb("KP", [P, 2, 2 * ROPE], F32, ar)
            FR = sb("FR", [P, 2, NOP, P], F32R, ar)

        ops_in = [sem("ops_in0"), sem("ops_in1")]; wq_loaded = [sem("wq_loaded0"), sem("wq_loaded1")]
        wh_ready = sem("wh_ready"); wl_ready = sem("wl_ready"); qp_ps = sem("qp_ps")
        s_wa = sem1("s_wa"); ln_s = sem1("ln_s"); ln_p = sem1("ln_p"); ln_ready = sem1("ln_ready"); xn_ready = sem1("xn_ready")
        xt_ps = sem1("xt_ps"); xt_ready = sem1("xt_ready"); raw_ps = sem1("raw_ps"); raw_ready = sem1("raw_ready")
        ssq_ready = sem1("ssq_ready"); msq_ready = sem1("msq_ready"); rms_ready = sem1("rms_ready"); qns_ready = sem1("qns_ready")
        kr_done = sem1("kr_done"); kv_ready = sem1("kv_ready"); kt_ps = sem1("kt_ps"); hi_ready = sem1("hi_ready")
        lo_ready = sem1("lo_ready"); ops_out = [sem1("ops_out0"), sem1("ops_out1")]
        LOS = QK + 3

        def operands(eng, b):
            if b >= 2:
                eng.wait_ge(ot_ps, (b - 1) * NH)
            for t in range(TT):
                eng.dma_start(OPS[:, b % 2, :, t * P:(t + 1) * P].bitcast(F32), ops_scr[b * TT + t])\
                   .then_inc(ops_in[b % 2], 16)

        def head_weights(eng, u, h):
            wpe = a["wpe"].rearrange("h (k p) c -> h p k c", p=P)
            eng.dma_start(WQ[:, u, :, 0:P], wqk_scr[bass.ds(h, 1)].rearrange("a p k c -> (a p) k c"))\
               .then_inc(wq_loaded[u], 16)
            eng.dma_start(WQ[:, u, :, P:2 * P], wpe[bass.ds(h, 1)].rearrange("a p k c -> (a p) k c"))\
               .then_inc(wq_loaded[u], 16)

        def split_weights(eng, n, u):
            eng.wait_ge(wq_loaded[u], n * 16 + (32 - 16 * u))
            if not (isinstance(n, int) and n < 2):
                eng.wait_ge(qp_ps, n - 1)
            eng.sem_inc(s_alone, 1)
            eng.tensor_scalar(WH[:, u, :, :], WQ[:, u, :, :], 1.0, 1.0, ALU.mult, ALU.mult).then_inc(wh_ready, 1)
            eng.wait_ge(wh_ready, n + 1)
            eng.tensor_tensor(WL[:, u, :, :], WQ[:, u, :, :], WH[:, u, :, :].bitcast(F32), ALU.subtract)\
               .then_inc(wl_ready, 1)

        def l_sync(eng):
            eng.dma_start(WA[:, :, :], a["waT"].rearrange("(k p) n -> p k n", p=P)).then_inc(s_wa, 16)
            for u in range(2):
                eng.sem_inc(ops_out[u], 16)
                head_weights(eng, u, u)

            def store(n, u):
                eng.wait_ge(lo_ready, n * LOS + LOS + 1)
                eng.dma_start(ops_scr[bass.ds(n, 1)].rearrange("a p c q -> (a p) c q"), FR[:, u, :, :].bitcast(F32))\
                   .then_inc(ops_out[u], 16)

            def stores(first, end):
                with eng.Fori(0, (end - first) // 2) as j:
                    store(j * 2 + first, 0)
                    store(j * 2 + (first + 1), 1)

            stores(0, TT + 2)
            for u in range(2):
                eng.wait_ge(ops_out[u], 16 * (TT // 2 + 1))
            operands(eng, 0)
            stores(TT + 2, 2 * TT + 2)
            for u in range(2):
                eng.wait_ge(ops_out[u], 16 * (TT + 1))
            operands(eng, 1)
            stores(2 * TT + 2, NT)
            for u in range(2):
                eng.wait_ge(ops_out[u], 16 * (NT // 2 + 1))

        def l_pool(eng):
            def rstd(n, u):
                eng.wait_ge(ln_s, n * 2 + 2)
                eng.sem_inc(s_alone, 1)
                eng.tensor_scalar(RSL[:, u, 1:2], MVL[:, u, 1:2], 1e-5, 1.0, ALU.add, ALU.mult).then_inc(ln_p, 1)
                eng.wait_ge(ln_p, n + 1)
                eng.tensor_tensor(RSL[:, u, 0:1], RSL[:, u, 1:2], NHALF[:, 0:1], ALU.pow).then_inc(ln_ready, 1)

            def rms(n, u):
                eng.wait_ge(ssq_ready, 2 * n + 2)
                eng.sem_inc(s_alone, 1)
                eng.tensor_scalar(MSQ[:, u, 0:1], SSQ[:, u, 0:1], 1.0 / LORA, 1e-6, ALU.mult, ALU.add).then_inc(msq_ready, 1)
                eng.tensor_scalar(MSQ[:, u, 1:2], SSQ[:, u, 1:2], 1.0 / QLORA, 1e-6, ALU.mult, ALU.add).then_inc(msq_ready, 1)
                eng.wait_ge(msq_ready, n * 2 + 2)
                eng.tensor_tensor(RMS[:, u, :], MSQ[:, u, :], NHALF[:, 0:2], ALU.pow).then_inc(rms_ready, 1)

            eng.sem_inc(wl_ready, 2)
            rstd(0, 0)
            rstd(1, 1)
            for n in range(2):
                split_weights(eng, n, n)

            def step(n, u, on):
                if on(2):
                    rstd(n + 2, u)
                if on(-1):
                    rms(n - 1, 1 - u)
            pipeline(eng, step, 3)

        def l_dve(eng):
            def stats(n, u):
                eng.bn_stats(STL[:, u, :], hrow(n)).then_inc(ln_s, 1)
                eng.wait_ge(ln_s, 2 * n + 1)
                eng.sem_inc(s_alone, 1)
                eng.bn_aggr(MVL[:, u, :], STL[:, u:u + 1, :]).then_inc(ln_s, 1)

            def norm(n, u):
                eng.wait_ge(ln_ready, n + 1)
                eng.tensor_scalar(XN[:, u, :], hrow(n), MVL[:, u, 0:1], RSL[:, u, 0:1], ALU.subtract, ALU.mult)\
                   .then_inc(xn_ready, 1)

            def scaled(n, u, t):
                eng.wait_ge(rms_ready, n + 1)
                kk = RAW[:, u, QLORA + LORA:QKV0]
                ropek = CST[:, C_ROPEK + t * 2 * ROPE:C_ROPEK + (t + 1) * 2 * ROPE]
                eng.tensor_tensor(KR[:, u, 0, :], kk, ropek[:, 0:ROPE], ALU.mult).then_inc(kr_done, 1)
                eng.tensor_tensor(KR[:, u, 1, 0:32], kk[:, 32:64], ropek[:, ROPE:ROPE + 32], ALU.mult).then_inc(kr_done, 1)
                eng.tensor_tensor(KR[:, u, 1, 32:64], kk[:, 0:32], ropek[:, ROPE + 32:2 * ROPE], ALU.mult).then_inc(kr_done, 1)
                eng.tensor_scalar(QL[:, u, :], RAW[:, u, 0:QLORA], RMS[:, u, 1:2], None, ALU.mult).then_inc(kv_ready, 1)
                eng.tensor_scalar(CN[:, u, :], RAW[:, u, QLORA:QLORA + LORA], RMS[:, u, 0:1], None, ALU.mult)\
                   .then_inc(kv_ready, 1)
                eng.wait_ge(kr_done, n * 3 + 3)
                for r in range(2):
                    eng.tensor_tensor(KP[:, u, r * ROPE:(r + 1) * ROPE], KR[:, u, 0, :], KR[:, u, 1, :],
                                      ALU.add).then_inc(kv_ready, 1)

            def low(n, u):
                f = FR[:, u, :, :]
                eng.wait_ge(hi_ready, n * LOS + LOS)
                for k in range(QK):
                    eng.scalar_tensor_tensor(f[:, QLO + k, :], PS[:, 6, k * P:(k + 1) * P], QNS[:, k:k + 1],
                                             f[:, QH + k, :].bitcast(F32), ALU.mult, ALU.subtract).then_inc(lo_ready, 1)
                eng.scalar_tensor_tensor(f[:, CLO, :], PS[:, 7, 0:P], KVW[:, 0:1], f[:, CH_, :].bitcast(F32),
                                         ALU.mult, ALU.subtract).then_inc(lo_ready, 1)
                eng.tensor_tensor(f[:, KLO, :], PS[:, 7, P:2 * P], f[:, KH, :].bitcast(F32), ALU.subtract).then_inc(lo_ready, 1)
                eng.tensor_tensor(f[:, VLO, :], CN[:, u, :], f[:, VH, :].bitcast(F32), ALU.subtract).then_inc(lo_ready, 1)

            eng.sem_inc(lo_ready, 1)
            eng.tensor_scalar(QNS[:, :], QNW[:, :], SCALE0, None, ALU.mult).then_inc(qns_ready, 1)
            eng.wait_ge(qns_ready, 1)
            for n in range(2):
                stats(n, n)
            for n in range(2):
                norm(n, n)

            def step(n, v, on):
                u = v % 2
                if on(2):
                    stats(n + 2, u)
                if on(-3):
                    low(n - 3, 1 - u)
                if on(2):
                    eng.wait_ge(xt_ps, n + 1)
                    norm(n + 2, u)
                if on(-1):
                    if on(-3):
                        eng.wait_ge(lo_ready, (n - 2) * LOS + 1)
                    scaled(n - 1, 1 - u, (v - 1) % TT)
            pipeline(eng, step, 3, turn=TT)

        def l_act(eng):
            def xnt(n, u):
                eng.wait_ge(xt_ps, n + 1)
                eng.activation(flat(XNT[:, u, :, :]), PS[:, u, :], ACT.Copy).then_inc(xt_ready, 1)

            def raw(n, u):
                eng.wait_ge(raw_ps, n + 1)
                if not (isinstance(n, int) and n < 2):
                    eng.wait_ge(kv_ready, 4 * n - 4)
                eng.activation(RAW[:, u, 0:QLORA], PS[:, 2 + 2 * u, 0:QLORA], ACT.Copy).then_inc(raw_ready, 1)
                eng.activation(RAW[:, u, QLORA:], PS[:, 3 + 2 * u, 0:LORA + ROPE], ACT.Copy).then_inc(raw_ready, 1)
                eng.wait_ge(raw_ready, 2 * n + 4)
                eng.activation(SQ[:, 0, 0:LORA], RAW[:, u, QLORA:QLORA + LORA], ACT.Square,
                               accum_out=SSQ[:, u, 0:1]).then_inc(ssq_ready, 1)
                eng.activation(SQ[:, 1, :], RAW[:, u, 0:QLORA], ACT.Square, accum_out=SSQ[:, u, 1:2]).then_inc(ssq_ready, 1)
                eng.wait_ge(ssq_ready, 2 * n + 2)

            def high(n, u):
                f = FR[:, u, :, :]
                eng.wait_ge(kt_ps, n + 1)
                eng.wait_ge(ops_out[u], n * 8 + (16 - 8 * u))
                for k in range(QK):
                    eng.activation(f[:, QH + k, :], PS[:, 6, k * P:(k + 1) * P], ACT.Copy, scale=QNS[:, k:k + 1])\
                       .then_inc(hi_ready, 1)
                eng.activation(f[:, CH_, :], PS[:, 7, 0:P], ACT.Copy, scale=KVW[:, 0:1]).then_inc(hi_ready, 1)
                eng.activation(f[:, KH, :], PS[:, 7, P:2 * P], ACT.Copy).then_inc(hi_ready, 1)
                eng.activation(f[:, VH, :], CN[:, u, :], ACT.Copy).then_inc(hi_ready, 1)

            eng.sem_inc(raw_ready, 2)
            eng.wait_ge(qns_ready, 1)
            xnt(0, 0)

            def step(n, u, on):
                if on(-3):
                    high(n - 3, 1 - u)
                if on(1):
                    xnt(n + 1, 1 - u)
                if on(0):
                    raw(n, u)
            pipeline(eng, step, 3)

        def l_pe(eng):
            eng.wait_ge(s_wa, 16)

            def xt(n, u):
                eng.wait_ge(xn_ready, n + 1)
                for k in range(KT):
                    mm = eng.transpose(PS[:, u, k * P:(k + 1) * P], XN[:, u, k * P:(k + 1) * P], ident)
                mm.then_inc(xt_ps, 1)

            def products(n, u):
                eng.wait_ge(xt_ready, n + 1)
                if not (isinstance(n, int) and n < 2):
                    eng.wait_ge(raw_ready, 2 * n)
                for k in range(KT):
                    eng.matmul(PS[:, 2 + 2 * u, 0:QLORA], XNT[:, u, k, :], WA[:, k, 0:QLORA], start=(k == 0), stop=(k == KT - 1))
                    mm = eng.matmul(PS[:, 3 + 2 * u, 0:LORA + ROPE], XNT[:, u, k, :], WA[:, k, QLORA:],
                                    start=(k == 0), stop=(k == KT - 1))
                mm.then_inc(raw_ps, 1)

            def turn(n, u):
                eng.wait_ge(kv_ready, n * 4 + 4)
                eng.wait_ge(lo_ready, n * LOS + 1)
                for k in range(QK):
                    eng.transpose(PS[:, 6, k * P:(k + 1) * P], QL[:, u, k * P:(k + 1) * P], ident)
                eng.transpose(PS[:, 7, 0:P], CN[:, u, :], ident)
                eng.transpose(PS[:, 7, P:2 * P], KP[:, u, :], ident).then_inc(kt_ps, 1)

            xt(0, 0)

            def step(n, u, on):
                if on(1):
                    xt(n + 1, 1 - u)
                if on(0):
                    products(n, u)
                if on(-2):
                    turn(n - 2, u)
            pipeline(eng, step, 3)

        with Arena() as ar:
            QNH = sb("QNH", [P, 2, S], F32R, ar)
            QNL = sb("QNL", [P, 2, S], F32R, ar)
            QPF = sb("QPF", [P, S], F32, ar)
            QPH = sb("QPH", [P, 2, S], F32R, ar)
            QPL = sb("QPL", [P, 2, S], F32R, ar)
            NMX = sb("NMX", [P, 2, TT], F32, ar)
            SUM = sb("SUM", [P, 2, TT], F32, ar)
            RSUM = sb("RSUM", [P, 2, TT], F32, ar)
            PR = sb("PR", [P, TT, S], F32, ar)
            PTH = sb("PTH", [P, TT, S], F32R, ar)
            PTL = sb("PTL", [P, TT, S], F32R, ar)
            OTH = sb("OTH", [P, 2, S], F32R, ar)
            OTL = sb("OTL", [P, 2, S], F32R, ar)
            VOH = sb("VOH", [P, 2, D], F32R, ar)
            VOL = sb("VOL", [P, 2, D], F32R, ar)

        arena_h.close()
        arena_w.close()

        qn_hi = sem("qn_hi"); qp_raw = sem("qp_raw"); qp_hi = sem("qp_hi")
        qn_ps = sem("qn_ps"); qn_ready = sem("qn_ready"); qp_ready = sem("qp_ready")
        s_ps = sem("s_ps"); max_ready = sem("max_ready"); p_ready = sem("p_ready"); rs_ready = sem("rs_ready")
        pn_ready = sem("pn_ready"); pt_ps = sem("pt_ps"); pt_hi = sem("pt_hi"); pt_ready = sem("pt_ready"); ot_ps = sem("ot_ps")
        ot_ready = sem("ot_ready"); ot_hi = sem("ot_hi"); vo_hi = sem("vo_hi"); vo_ready = sem("vo_ready"); w_done = sem("w_done"); res_done = sem("res_done")
        SB, PTB, QB = 4, 6, 7
        NN = NB * NH

        def tile_at(u, i):
            return (SB + 1 - u, 0) if i == 2 else (SB + u, P if i == 1 else 0)

        def heads(eng, step):
            for b in range(NB):
                step(b * NH, 0, b, 0)
                step(b * NH + 1, 1, b, 1)
                with eng.Fori(0, NH // 2 - 2) as j:
                    step(j * 2 + (b * NH + 2), 0, b, None)
                    step(j * 2 + (b * NH + 3), 1, b, None)
                step(b * NH + NH - 2, 0, b, NH - 2)
                step(b * NH + NH - 1, 1, b, NH - 1)

        def around(b, h):
            before = (b - 1 if b else None) if h == 0 else b
            after = (b + 1 if b + 1 < NB else None) if h == NH - 1 else b
            return before, after

        def a_sync(eng):
            def step(n, u, b, h):
                if b or h not in (0, 1):
                    eng.wait_ge(wl_ready, n + 1)
                    head_weights(eng, u, n - b * NH)
                if h == 1 and 1 <= b < NB - 1:
                    operands(eng, b + 1)
            heads(eng, step)

        def a_pool(eng):
            def normalise(n, u, i):
                eng.wait_ge(rs_ready, n * TT + i + 1)
                eng.sem_inc(s_alone, 1)
                eng.tensor_scalar(PR[:, i, 0:(i + 1) * P], PR[:, i, 0:(i + 1) * P], RSUM[:, u, i:i + 1],
                                  1.0, ALU.mult, ALU.mult).then_inc(pn_ready, 1)

            def step(n, u, b, h):
                for i in range(TT):
                    normalise(n, u, i)
                if not (b == NB - 1 and h in (NH - 2, NH - 1)):
                    split_weights(eng, n + 2, u)
            heads(eng, step)

        def a_dve(eng):
            eng.sem_inc(pt_ready, 1)
            eng.sem_inc(ot_ready, 1)

            def query_low(n, u):
                eng.wait_ge(qn_hi, n + 1)
                eng.tensor_tensor(QNL[:, u, :], PS[:, QB, :], QNH[:, u, :].bitcast(F32), ALU.subtract).then_inc(qn_ready, 1)

            def rope(n, u):
                eng.wait_ge(qp_ps, n + 1)
                for i in range(2):
                    q = slice(i * S // 2, (i + 1) * S // 2)
                    eng.tensor_tensor(QPF[:, q], PS[:, QB, q], CST[:, C_ROPEQ + q.start:C_ROPEQ + q.stop], ALU.mult)\
                       .then_inc(qp_raw, 1)

            def rope_low(n, u):
                for i in range(2):
                    q = slice(i * S // 2, (i + 1) * S // 2)
                    eng.wait_ge(qp_hi, n * 2 + i + 1)
                    eng.tensor_tensor(QPL[:, u, q], QPF[:, q], QPH[:, u, q].bitcast(F32), ALU.subtract).then_inc(qp_ready, 1)

            def tile_max(n, u, i):
                bank, col = tile_at(u, i)
                eng.wait_ge(s_ps, n * 3 + max(i, 1))
                eng.tensor_reduce(NMX[:, u, i:i + 1], PS[:, bank, col:col + (i + 1) * P], AX, ALU.max, negate=True)\
                   .then_inc(max_ready, 1)

            def tile_recip(n, u, i):
                eng.wait_ge(p_ready, n * TT + i + 3)
                eng.reciprocal(RSUM[:, u, i:i + 1], SUM[:, u, i:i + 1]).then_inc(rs_ready, 1)

            def turned_low(n, u, i):
                eng.wait_ge(pt_hi, n * 3 + i)
                if i == 1:
                    eng.tensor_tensor(PTL[:, 0, 0:P], PS[:, PTB, 0:P], PTH[:, 0, 0:P].bitcast(F32), ALU.subtract)
                col = P if i == 1 else 0
                eng.tensor_tensor(PTL[:, 0:i + 1, i * P:(i + 1) * P],
                                  PS[:, PTB, col:col + (i + 1) * P].rearrange("p (k q) -> p k q", q=P),
                                  PTH[:, 0:i + 1, i * P:(i + 1) * P].bitcast(F32), ALU.subtract).then_inc(pt_ready, 1)

            def head_out(n, u):
                eng.wait_ge(ot_hi, n + 1)
                eng.tensor_tensor(OTL[:, u, :], PS[:, QB, :], OTH[:, u, :].bitcast(F32), ALU.subtract).then_inc(ot_ready, 1)

            def weights_low(n, u, hh):
                eng.wait_ge(vo_hi, n + 1)
                eng.tensor_tensor(VOL[:, u, :], flat(WVO[:, bass.ds(hh, 1), :]), VOH[:, u, :].bitcast(F32), ALU.subtract)\
                   .then_inc(vo_ready, 1)

            def residual(b):
                for t in range(TT):
                    eng.wait_ge(w_done, b * TT + t + 1)
                    h = H[:, b * TT + t, :]
                    eng.tensor_tensor(h, PS[:, t, :], h, ALU.add).then_inc(res_done, 1)

            query_low(0, 0)
            rope(0, 0)
            rope_low(0, 0)
            tile_max(0, 0, 0)
            tile_max(0, 0, 1)

            def step(n, u, b, h):
                before, after = around(b, h)
                tile_max(n, u, 2)
                tile_recip(n, u, 0)
                tile_recip(n, u, 1)
                tile_recip(n, u, 2)
                if before is not None:
                    head_out(n - 1, 1 - u)
                tile_max(n, u, 3)
                tile_recip(n, u, 3)
                turned_low(n, u, 1)
                if after is not None:
                    query_low(n + 1, 1 - u)
                weights_low(n, u, n - b * NH)
                turned_low(n, u, 2)
                if after is not None:
                    rope(n + 1, 1 - u)
                    rope_low(n + 1, 1 - u)
                turned_low(n, u, 3)
                if after is not None:
                    tile_max(n + 1, 1 - u, 0)
                    tile_max(n + 1, 1 - u, 1)
                if h == 0 and b:
                    residual(b - 1)
            heads(eng, step)
            head_out(NN - 1, 1)
            residual(NB - 1)

        def a_act(eng):
            eng.sem_inc(p_ready, 2)

            def query_high(n, u):
                eng.wait_ge(qn_ps, n + 1)
                eng.activation(QNH[:, u, :], PS[:, QB, :], ACT.Copy).then_inc(qn_hi, 1)

            def rope_high(n, u):
                for i in range(2):
                    q = slice(i * S // 2, (i + 1) * S // 2)
                    eng.wait_ge(qp_raw, n * 2 + i + 1)
                    eng.activation(QPH[:, u, q], QPF[:, q], ACT.Copy).then_inc(qp_hi, 1)

            def turned_high(n, u, i):
                eng.wait_ge(pt_ps, n * 3 + i + 1)
                if i == 1:
                    eng.activation(PTH[:, 0, 0:P], PS[:, PTB, 0:P], ACT.Copy)
                col = P if i == 1 else 0
                eng.activation(PTH[:, 0:i + 1, i * P:(i + 1) * P],
                               PS[:, PTB, col:col + (i + 1) * P].rearrange("p (k q) -> p k q", q=P), ACT.Copy).then_inc(pt_hi, 1)

            def tile_exp(n, u, i):
                bank, col = tile_at(u, i)
                if i == 0:
                    eng.wait_ge(pt_ps, n * 3 + 1)
                eng.wait_ge(max_ready, n * TT + max(i, 1) + 1)
                eng.activation(PR[:, i, 0:(i + 1) * P], PS[:, bank, col:col + (i + 1) * P], ACT.Exp,
                               bias=NMX[:, u, i:i + 1], accum_out=SUM[:, u, i:i + 1]).then_inc(p_ready, 1)

            def weights_high(n, u, hh):
                eng.wait_ge(pt_ps, n * 3 + 1)
                eng.activation(VOH[:, u, :], flat(WVO[:, bass.ds(hh, 1), :]), ACT.Copy).then_inc(vo_hi, 1)

            def out_high(n, u):
                eng.wait_ge(ot_ps, n + 1)
                eng.activation(OTH[:, u, :], PS[:, QB, :], ACT.Copy).then_inc(ot_hi, 1)

            query_high(0, 0)
            rope_high(0, 0)

            def step(n, u, b, h):
                before, after = around(b, h)
                for i in range(TT - 1):
                    tile_exp(n, u, i)
                if before is not None:
                    out_high(n - 1, 1 - u)
                tile_exp(n, u, TT - 1)
                turned_high(n, u, 1)
                if after is not None:
                    query_high(n + 1, 1 - u)
                weights_high(n, u, n - b * NH)
                turned_high(n, u, 2)
                if after is not None:
                    rope_high(n + 1, 1 - u)
                turned_high(n, u, 3)
            heads(eng, step)
            out_high(NN - 1, 1)

        def a_pe(eng):
            eng.sem_inc(pt_ps, 1)

            def split_product(out, lhs, rhs, start, stop, skip=False):
                eng.matmul(out, lhs[0], rhs[0], start=start, stop=False, skip_group_check=skip)
                eng.matmul(out, lhs[0], rhs[1], start=False, stop=False, skip_group_check=skip)
                return eng.matmul(out, lhs[1], rhs[0], start=False, stop=stop, skip_group_check=skip)

            def queries(n, u, s, c):
                for k in range(QK):
                    mm = split_product(PS[:, QB, :], (WH[:, u, k, c:c + P], WL[:, u, k, c:c + P]),
                                       (OPS[:, s, QH + k, :], OPS[:, s, QLO + k, :]), k == 0, k == QK - 1)
                return mm

            def query_latent(n, u, s):
                eng.wait_ge(wl_ready, n + 3)
                queries(n, u, s, 0).then_inc(qn_ps, 1)

            def query_pe(n, u, s):
                eng.wait_ge(qn_ready, n + 1)
                queries(n, u, s, P).then_inc(qp_ps, 1)

            def scores(n, u, s, i):
                if i == 1:
                    eng.wait_ge(p_ready, n * TT + 1)
                    eng.wait_ge(qn_ready, n + 1)
                    eng.wait_ge(qp_ready, n * 2 + 1)
                elif i == 2:
                    eng.wait_ge(p_ready, n * TT + 2)
                    eng.wait_ge(qp_ready, n * 2 + 2)
                else:
                    eng.wait_ge(p_ready, n * TT + 4)
                for r in ((0, 1) if i == 1 else (i,)):
                    w = (r + 1) * P
                    bank, col = tile_at(u, r)
                    o = PS[:, bank, col:col + w]
                    split_product(o, (QNH[:, u, r * P:w], QNL[:, u, r * P:w]), (OPS[:, s, CH_, 0:w], OPS[:, s, CLO, 0:w]),
                                  True, False)
                    split_product(o, (QPH[:, u, r * P:w], QPL[:, u, r * P:w]), (OPS[:, s, KH, 0:w], OPS[:, s, KLO, 0:w]),
                                  False, False)
                    mm = eng.matmul(o[:, r * P:w], IDB[:, :], MASKB[:, :], start=False, stop=True)
                mm.then_inc(s_ps, 1)

            def turn(n, u, i):
                eng.wait_ge(pn_ready, n * TT + i + 1)
                eng.wait_ge(pt_ready, n * 3 + i)
                if i == 1:
                    eng.transpose(PS[:, PTB, 0:P], PR[:, 0, 0:P], ident)
                col = P if i == 1 else 0
                for k in range(i + 1):
                    mm = eng.transpose(PS[:, PTB, col + k * P:col + (k + 1) * P], PR[:, i, k * P:(k + 1) * P], ident)
                mm.then_inc(pt_ps, 1)

            def values(n, s):
                eng.wait_ge(pt_ready, n * 3 + 4)
                for k in range(TT):
                    mm = split_product(PS[:, QB, k * P:], (OPS[:, s, VH, k * P:(k + 1) * P], OPS[:, s, VLO, k * P:(k + 1) * P]),
                                       (PTH[:, k, k * P:], PTL[:, k, k * P:]), k == 0, k == TT - 1)
                mm.then_inc(ot_ps, 1)

            def project(n, u, b, h, tiles):
                eng.wait_ge(ot_ready, n + 2)
                eng.wait_ge(vo_ready, n + 1)
                for t in tiles:
                    if h == 0 and b:
                        eng.wait_ge(res_done, (b - 1) * TT + t + 1)
                    q = slice(t * P, (t + 1) * P)
                    mm = split_product(PS[:, t, :], (OTH[:, u, q], OTL[:, u, q]), (VOH[:, u, :], VOL[:, u, :]),
                                       h == 0, h == NH - 1, skip=True)
                    if h == NH - 1:
                        mm.then_inc(w_done, 1)

            eng.wait_ge(ops_in[0], 16 * TT)
            query_latent(0, 0, 0)
            query_pe(0, 0, 0)
            scores(0, 0, 0, 1)

            def step(n, u, b, h):
                before, after = around(b, h)
                last = None if h is None or h == 0 else h - 1
                if h == 0:
                    last = NH - 1
                if h == NH - 1 and after is not None:
                    eng.wait_ge(ops_in[after % 2], 16 * TT * (after // 2 + 1))
                scores(n, u, b % 2, 2)
                if before is not None:
                    values(n - 1, before % 2)
                scores(n, u, b % 2, 3)
                turn(n, u, 1)
                if after is not None:
                    eng.wait_ge(ot_ready, n + 1)
                    query_latent(n + 1, 1 - u, after % 2)
                if before is not None:
                    project(n - 1, 1 - u, before, last, (0, 1))
                turn(n, u, 2)
                if after is not None:
                    query_pe(n + 1, 1 - u, after % 2)
                if before is not None:
                    project(n - 1, 1 - u, before, last, (2, 3))
                turn(n, u, 3)
                if after is not None:
                    scores(n + 1, 1 - u, after % 2, 1)
            heads(eng, step)
            values(NN - 1, (NB - 1) % 2)
            project(NN - 1, 1, NB - 1, NH - 1, range(TT))

        CH = [(0, 512), (512, 512), (1024, 384)]
        IT = INTER // P
        RT1, RT2 = 2 * INTER // P, D // P
        ROWS = (RT1 + RT2) * P
        scale_scr = nc.dram_tensor("scale_scr", [1, ROWS], F32, kind="Internal").ap()
        with Arena() as ar:
            W1Q = sb("W1Q", [P, KT, 2 * INTER], BF16, ar)
            W2Q = sb("W2Q", [P, IT, D], BF16, ar)
            SW = sb("SW", [P, ROWS], F32, ar)
            FXT = sb("FXT", [P, NT, KT, P], BF16, ar)
            with Arena() as tmp:
                JUNK = sb("JUNK", [P, 2, D], F32, tmp)
                FXN = sb("FXN", [P, TT, D], F32, tmp)
                FXM = sb("FXM", [P, TT, D], F32, tmp)
                FXQ = sb("FXQ", [P, TT, D], BF16, tmp)
                WN1 = sb("WN1", [P, 3, 2, D], F32, tmp)
                WM1 = sb("WM1", [P, 2, 2, D], F32, tmp)
                WI1 = sb("WI1", [P, 2, 2, D], BF16, tmp)
                WN2 = sb("WN2", [P, 2, INTER], F32, tmp)
                WM2 = sb("WM2", [P, INTER], F32, tmp)
                WI2 = sb("WI2", [P, INTER], BF16, tmp)
                AMW = sb("AMW", [P, 3, RT1 + RT2], F32, tmp)
            FS = sb("FS", [P, 2, 12], F32, ar)
            GS = sb("GS", [P, 2, 512], F32, ar)
            GA = sb("GA", [P, 2, 512], F32, ar)
            US = sb("US", [P, 2, 512], F32, ar)
            HM = sb("HM", [P, 2, INTER], F32, ar)
            HR = sb("HR", [P, INTER], F32, ar)
            HQ = sb("HQ", [P, 2, INTER], BF16, ar)
            HT = sb("HT", [P, 2, IT, P], BF16, ar)
            FO = sb("FO", [P, 2, D], F32, ar)

        V_MEAN, V_VAR, V_RSTD, V_SX, V_RX, V_SH, V_RH, V_AM, V_AH = range(9)
        fw_load = [sem("fw_load%d" % i) for i in range(3)]; fw_load2 = [sem("fw_load20"), sem("fw_load21")]
        fw_max = sem("fw_max"); fw_s = sem("fw_s"); fw_scr = sem("fw_scr"); fw_b = sem("fw_b"); fw_m = sem("fw_m")
        fw_i = sem("fw_i"); fw_tp = sem("fw_tp"); fw_q = sem("fw_q")
        f_sum = sem("f_sum"); f_mean = sem("f_mean"); f_sq = sem("f_sq"); f_sx = sem("f_sx"); f_pv = sem("f_pv"); f_rstd = sem("f_rstd"); f_am = sem("f_am"); f_xm = sem("f_xm"); f_xq = sem("f_xq")
        f_xtp = sem("f_xtp"); f_xt = sem("f_xt"); f_mm = sem("f_mm"); f_g = sem("f_g"); f_ga = sem("f_ga"); f_u = sem("f_u")
        f_hm = sem("f_hm"); f_hr = sem("f_hr"); f_hq = sem("f_hq"); f_htp = sem("f_htp"); f_ht = sem("f_ht")
        f_op = sem("f_op"); f_o = sem("f_o"); f_res = sem("f_res"); f_hs = sem("f_hs"); f_xn = sem("f_xn")

        G1 = RT1 // 2

        def fw_sync(eng):
            w1 = a["w_gate_up"].rearrange("(g t p) k -> g p t k", p=P, t=2)
            w2 = a["w_down"].rearrange("(t p) k -> t p k", p=P)
            for g in range(G1):
                if g >= 3:
                    eng.wait_ge(fw_m, g - 2)
                eng.dma_start(WN1[:, g % 3, :, :], w1[g]).then_inc(fw_load[g % 3], 16)
            for i in range(RT2):
                if i >= 2:
                    eng.wait_ge(fw_m, G1 + i - 1)
                eng.dma_start(WN2[:, i % 2, :], w2[i]).then_inc(fw_load2[i % 2], 16)
            eng.wait_ge(fw_s, 2 * (G1 + RT2))
            with nc.allow_non_contiguous_dma(reason="one scale a partition"):
                eng.dma_start(scale_scr[0].rearrange("(t p) -> p t", p=P), AMW[:, 1, :]).then_inc(fw_scr, 16)
            eng.wait_ge(fw_scr, 16)
            eng.dma_start(SW[:, :], scale_scr[0:1].to_broadcast([P, ROWS])).then_inc(fw_b, 16)
            eng.wait_ge(fw_b, 16)

        def w_group(g):
            if g < G1:
                return WN1[:, g % 3, :, :], WM1[:, g % 2, :, :], WI1[:, g % 2, :, :], range(2 * g, 2 * g + 2)
            i = g - G1
            return (WN2[:, i % 2, :].unsqueeze(1), WM2[:, :].unsqueeze(1), WI2[:, :].unsqueeze(1), range(RT1 + i, RT1 + i + 1))

        def fw_dve(eng):
            def scale(g):
                src, mid, _, tiles = w_group(g)
                c0, c1 = tiles[0], tiles[-1] + 1
                if g < G1:
                    eng.wait_ge(fw_load[g % 3], 16 * (g // 3) + 16)
                else:
                    eng.wait_ge(fw_load2[(g - G1) % 2], 16 * ((g - G1) // 2) + 16)
                eng.tensor_reduce(AMW[:, 0, c0:c1], src, AX, ALU.max, apply_absolute_value=True).then_inc(fw_max, 1)
                eng.wait_ge(fw_max, g + 1)
                eng.tensor_scalar(AMW[:, 1, c0:c1], AMW[:, 0, c0:c1], 1.0 / 127.0, 1e-8, ALU.mult, ALU.max).then_inc(fw_s, 1)
                eng.wait_ge(fw_s, 2 * g + 1)
                eng.reciprocal(AMW[:, 2, c0:c1], AMW[:, 1, c0:c1]).then_inc(fw_s, 1)
                eng.wait_ge(fw_s, 2 * g + 2)
                if g < G1 and g >= 2:
                    eng.wait_ge(fw_i, g - 1)
                elif g >= G1:
                    eng.wait_ge(fw_i, g)
                for i, c in enumerate(tiles):
                    ins = eng.tensor_scalar(mid[:, i, :], src[:, i, :], AMW[:, 2, c:c + 1], MAGIC, ALU.mult, ALU.add)
                ins.then_inc(fw_m, 1)

            for g in range(G1):
                scale(g)
            for b in range(NB):
                fx_dve(eng, b)
                scale(G1 + b)

        def fw_pool(eng, groups):
            for g in groups:
                _, mid, out8, tiles = w_group(g)
                eng.wait_ge(fw_m, g + 1)
                if g >= 2 and g < G1:
                    eng.wait_ge(fw_tp, g - 1)
                elif g >= G1:
                    eng.wait_ge(fw_tp, g)
                eng.tensor_scalar(out8, mid, -MAGIC, 1.0, ALU.add, ALU.mult).then_inc(fw_i, 1)

        def fw_pe(eng, groups):
            for g in groups:
                out8, tiles = w_group(g)[2:]
                eng.wait_ge(fw_i, g + 1)
                if g < G1:
                    if g >= 2:
                        eng.wait_ge(fw_q, g - 1)
                    for k in range(KT):
                        for i in range(2):
                            c = (2 * k + i) * 64
                            mm = eng.transpose(PS[:, 2 + g % 2, c:c + 64].bitcast(BF16), out8[:, i, k * P:(k + 1) * P], IDB[:, :])
                else:
                    eng.wait_ge(fw_q, g)
                    for k in range(IT):
                        mm = eng.transpose(PS[:, 4 + k // 8, (k % 8) * 64:(k % 8 + 1) * 64].bitcast(BF16),
                                           out8[:, 0, k * P:(k + 1) * P], IDB[:, :])
                mm.then_inc(fw_tp, 1)

        def fw_act(eng, groups):
            for g in groups:
                eng.wait_ge(fw_tp, g + 1)
                if g < G1:
                    eng.activation(W1Q[:, :, 2 * g * P:(2 * g + 2) * P],
                                   PS[:, 2 + g % 2, :].bitcast(BF16).rearrange("p (k r) -> p k r", k=KT), ACT.Copy)\
                       .then_inc(fw_q, 1)
                else:
                    r0 = (g - G1) * P
                    eng.activation(W2Q[:, 0:8, r0:r0 + P], PS[:, 4, :].bitcast(BF16).rearrange("p (k r) -> p k r", r=P), ACT.Copy)
                    eng.activation(W2Q[:, 8:IT, r0:r0 + P], PS[:, 5, 0:192].bitcast(BF16).rearrange("p (k r) -> p k r", r=P),
                                   ACT.Copy).then_inc(fw_q, 1)

        LSUM, LMEAN, LSQ, LRSTD, LNM, LAX, LSX, LRX = range(8)

        def fx_pool(eng):
            fw_pool(eng, range(0, 2))
            mean_pool(eng, f_sum, f_mean)
            fw_pool(eng, range(2, 8))
            rstd_pool(eng, f_sq, f_pv, f_rstd)
            fw_pool(eng, range(8, G1))
            for b in range(NB):
                for n in range(b * TT, b * TT + TT):
                    eng.wait_ge(f_xm, n + 1)
                    if b:
                        eng.wait_ge(f_xtp, n - TT + 1)
                    eng.tensor_scalar(FXQ[:, n % TT, :], FXM[:, n % TT, :], -MAGIC, 1.0, ALU.add, ALU.mult)\
                       .then_inc(f_xq, 1)
                fw_pool(eng, [G1 + b])

        def stats_act(eng, junk, s_sum, s_mean, s_sq, between):
            for n in range(NT):
                eng.activation(junk[:, n % 2, :], H[:, n, :], ACT.Copy, accum_out=LNS[:, LSUM, n:n + 1]).then_inc(s_sum, 1)
                if n:
                    eng.wait_ge(s_sum, n)
            eng.wait_ge(s_mean, 1)
            eng.wait_ge(s_sum, NT)
            for n in range(NT):
                eng.activation(junk[:, n % 2, :], H[:, n, :], ACT.Square, bias=LNS[:, LMEAN, n:n + 1],
                               accum_out=LNS[:, LSQ, n:n + 1]).then_inc(s_sq, 1)
                if n:
                    eng.wait_ge(s_sq, n)
                between(n)

        def mean_pool(eng, s_sum, s_mean):
            eng.wait_ge(s_sum, NT)
            eng.tensor_scalar(LNS[:, LMEAN, :], LNS[:, LSUM, :], -1.0 / D, 1.0, ALU.mult, ALU.mult).then_inc(s_mean, 1)

        def rstd_pool(eng, s_sq, s_v, s_rstd):
            eng.wait_ge(s_sq, NT)
            eng.tensor_scalar(LNS[:, LSQ, :], LNS[:, LSQ, :], 1.0 / D, 1e-5, ALU.mult, ALU.add).then_inc(s_v, 1)
            eng.wait_ge(s_v, 1)
            eng.tensor_tensor(LNS[:, LRSTD, :], LNS[:, LSQ, :], NHALF[:, 0:1].to_broadcast([P, NT]), ALU.pow)\
               .then_inc(s_v, 1)
            eng.wait_ge(s_v, 2)
            eng.tensor_tensor(LNS[:, LNM, :], LNS[:, LMEAN, :], LNS[:, LRSTD, :], ALU.mult).then_inc(s_rstd, 1)

        def fx_act(eng):
            stats_act(eng, JUNK, f_sum, f_mean, f_sq, lambda n: fw_act(eng, [n // 2] if n % 2 == 0 else []))
            eng.wait_ge(f_rstd, 1)

            def norms(b):
                for n in range(b * TT, b * TT + TT):
                    if b:
                        eng.wait_ge(f_xm, n - TT + 1)
                    eng.activation(FXN[:, n % TT, :], H[:, n, :], ACT.Identity, bias=LNS[:, LNM, n:n + 1],
                                   scale=LNS[:, LRSTD, n:n + 1]).then_inc(f_xn, 1)

            def turned(b):
                for n in range(b * TT, b * TT + TT):
                    eng.wait_ge(f_xtp, n + 1)
                    eng.activation(flat(FXT[:, n, :, :]), PS[:, n % 2, 0:256].bitcast(BF16), ACT.Copy).then_inc(f_xt, 1)

            norms(0)
            fw_act(eng, range(NT // 2, G1))
            for b in range(NB):
                if b + 1 < NB:
                    norms(b + 1)
                turned(b)
                fw_act(eng, [G1 + b])

        def fx_dve(eng, b):
            rows = range(b * TT, b * TT + TT)
            c0, c1 = b * TT, b * TT + TT
            for n in rows:
                eng.wait_ge(f_xn, n + 1)
                eng.tensor_reduce(LNS[:, LAX, n:n + 1], FXN[:, n % TT, :], AX, ALU.max, apply_absolute_value=True)                   .then_inc(f_am, 1)
            eng.wait_ge(f_am, c1)
            eng.tensor_scalar(LNS[:, LSX, c0:c1], LNS[:, LAX, c0:c1], 1.0 / 127.0, 1e-8, ALU.mult, ALU.max).then_inc(f_sx, 1)
            eng.wait_ge(f_sx, 2 * b + 1)
            eng.reciprocal(LNS[:, LRX, c0:c1], LNS[:, LSX, c0:c1]).then_inc(f_sx, 1)
            eng.wait_ge(f_sx, 2 * b + 2)
            for n in rows:
                if b:
                    eng.wait_ge(f_xq, n - TT + 1)
                eng.tensor_scalar(FXM[:, n % TT, :], FXN[:, n % TT, :], LNS[:, LRX, n:n + 1], MAGIC, ALU.mult, ALU.add)                   .then_inc(f_xm, 1)
        def fx_pe(eng):
            fw_pe(eng, range(G1))
            for n in range(NT):
                eng.wait_ge(f_xq, n + 1)
                if n >= 2:
                    eng.wait_ge(f_xt, n - 1)
                for k in range(KT):
                    mm = eng.transpose(PS[:, n % 2, k * 64:(k + 1) * 64].bitcast(BF16), FXQ[:, n % TT, k * P:(k + 1) * P],
                                       IDB[:, :])
                mm.then_inc(f_xtp, 1)
                if n % TT == TT - 1:
                    fw_pe(eng, [G1 + n // TT])

        def f_dve(eng):
            eng.sem_inc(f_o, 1)
            def scaled(n, u, c):
                c0, w = CH[c]
                s = (u + c) % 2
                k = n * 3 + c
                eng.wait_ge(f_mm, k + 1)
                eng.wait_ge(f_ga, k + 1)
                eng.scalar_tensor_tensor(GS[:, s, 0:w], PS[:, 1 + 2 * s, 0:w], LNS[:, LSX, bass.ds(n, 1)],
                                         SW[:, c0:c0 + w], ALU.mult, ALU.mult).then_inc(f_g, 1)
                eng.wait_ge(f_hm, k + 1)
                eng.scalar_tensor_tensor(US[:, s, 0:w], PS[:, 2 + 2 * s, 0:w], LNS[:, LSX, bass.ds(n, 1)],
                                         SW[:, INTER + c0:INTER + c0 + w], ALU.mult, ALU.mult).then_inc(f_u, 1)

            def hidden_max(n, u):
                eng.wait_ge(f_hm, n * 3 + 3 + 2)
                eng.tensor_reduce(FS[:, u, V_AH:V_AH + 1], HM[:, u, :], AX, ALU.max, apply_absolute_value=True)\
                   .then_inc(f_hs, 1)

            def hidden_scale(n, u):
                eng.wait_ge(f_hs, n * 3 + 1)
                eng.tensor_scalar(FS[:, u, V_SH:V_SH + 1], FS[:, u, V_AH:V_AH + 1], 1.0 / 127.0, 1e-8,
                                  ALU.mult, ALU.max).then_inc(f_hs, 1)

            def hidden_recip(n, u):
                eng.wait_ge(f_hs, n * 3 + 2)
                eng.reciprocal(FS[:, u, V_RH:V_RH + 1], FS[:, u, V_SH:V_SH + 1]).then_inc(f_hs, 1)

            def hidden_round(n, u):
                eng.wait_ge(f_hs, n * 3 + 3)
                eng.tensor_scalar(HR[:, :], HM[:, u, :], FS[:, u, V_RH:V_RH + 1], MAGIC, ALU.mult, ALU.add)\
                   .then_inc(f_hr, 1)
                eng.wait_ge(f_hr, n + 1)
                eng.tensor_scalar(HQ[:, u, :], HR[:, :], MAGIC, None, ALU.subtract).then_inc(f_hq, 1)

            def out_scaled(n, u):
                eng.wait_ge(f_op, n + 1)
                eng.wait_ge(f_res, n + 1)
                eng.scalar_tensor_tensor(FO[:, u, :], PS[:, 7, :], FS[:, u, V_SH:V_SH + 1], SW[:, RT1 * P:],
                                         ALU.mult, ALU.mult).then_inc(f_o, 1)

            def step(n, u, on):
                if on(0):
                    scaled(n, u, 0)
                    scaled(n, u, 1)
                if on(-1):
                    hidden_max(n - 1, 1 - u)
                    hidden_scale(n - 1, 1 - u)
                    hidden_recip(n - 1, 1 - u)
                    hidden_round(n - 1, 1 - u)
                if on(0):
                    scaled(n, u, 2)
                if on(-2):
                    out_scaled(n - 2, u)
            pipeline(eng, step, 2)

        def f_pool(eng):
            eng.sem_inc(f_hm, 2)
            eng.sem_inc(f_res, 2)

            def gate(n, u, c):
                c0, w = CH[c]
                s = (u + c) % 2
                eng.wait_ge(f_ga, n * 3 + c + 3)
                eng.wait_ge(f_u, n * 3 + c + 1)
                eng.tensor_tensor(HM[:, u, c0:c0 + w], GA[:, s, 0:w], US[:, s, 0:w], ALU.mult).then_inc(f_hm, 1)

            def residual(n, u):
                eng.wait_ge(f_o, n + 2)
                eng.tensor_tensor(hrow(n), hrow(n), FO[:, u, :], ALU.add).then_inc(f_res, 1)

            def step(n, u, on):
                for c in range(3):
                    if on(0):
                        gate(n, u, c)
                if on(-2):
                    residual(n - 2, u)
            pipeline(eng, step, 2)

        def f_act(eng):
            eng.sem_inc(f_ht, 1)
            eng.sem_inc(f_ga, 2)

            def silu(n, u, c):
                w = CH[c][1]
                s = (u + c) % 2
                eng.wait_ge(f_g, n * 3 + c + 1)
                eng.wait_ge(f_hm, n * 3 + c + 1)
                eng.activation(GA[:, s, 0:w], GS[:, s, 0:w], ACT.Silu).then_inc(f_ga, 1)

            def ht(n, u):
                eng.wait_ge(f_htp, n + 1)
                eng.activation(flat(HT[:, u, 0:8, :]), PS[:, 5, :].bitcast(BF16), ACT.Copy)
                eng.activation(flat(HT[:, u, 8:IT, :]), PS[:, 6, 0:192].bitcast(BF16), ACT.Copy).then_inc(f_ht, 1)

            def step(n, u, on):
                for c in range(3):
                    if on(0):
                        silu(n, u, c)
                    if c == 1 and on(-2):
                        ht(n - 2, u)
            pipeline(eng, step, 2)

        def f_pe(eng):
            def up(n, u, c):
                c0, w = CH[c]
                s = (u + c) % 2
                if not (isinstance(n, int) and n * 3 + c < 2):
                    eng.wait_ge(f_u, n * 3 + c - 1)
                for k in range(KT):
                    eng.matmul(PS[:, 1 + 2 * s, 0:w], flat(FXT[:, bass.ds(n, 1), k, :]), W1Q[:, k, c0:c0 + w], start=(k == 0), stop=(k == KT - 1))
                    mm = eng.matmul(PS[:, 2 + 2 * s, 0:w], flat(FXT[:, bass.ds(n, 1), k, :]), W1Q[:, k, INTER + c0:INTER + c0 + w],
                                    start=(k == 0), stop=(k == KT - 1))
                mm.then_inc(f_mm, 1)

            def turn(n, u):
                eng.wait_ge(f_hq, n + 1)
                eng.wait_ge(f_ht, n + 1)
                for k in range(IT):
                    mm = eng.transpose(PS[:, 5 + k // 8, (k % 8) * 64:(k % 8 + 1) * 64].bitcast(BF16),
                                       HQ[:, u, k * P:(k + 1) * P], IDB[:, :])
                mm.then_inc(f_htp, 1)

            def down(n, u):
                eng.wait_ge(f_ht, n + 2)
                eng.wait_ge(f_o, n + 1)
                for k in range(IT):
                    mm = eng.matmul(PS[:, 7, :], HT[:, u, k, :], W2Q[:, k, :], start=(k == 0), stop=(k == IT - 1))
                mm.then_inc(f_op, 1)

            def step(n, u, on):
                if on(0):
                    up(n, u, 0)
                    up(n, u, 1)
                if on(-2):
                    turn(n - 2, u)
                if on(0):
                    up(n, u, 2)
                if on(-2):
                    down(n - 2, u)
            pipeline(eng, step, 2)

        first_sems.close()

        KVH = NH // 2
        QKC = (NH + KVH) * HD
        with Arena() as ar:
            WB = sb("WB", [P, KT, 2 * D], F32, ar)
            WO1 = sb("WO1", [P, KT, D], F32, ar)
            BXN = sb("BXN", [P, 2, D], F32, ar)
            BXT = sb("BXT", [P, 2, KT, P], F32, ar)
            RA = sb("RA", [P, QKC], F32, ar)
            RB = sb("RB", [P, QKC], F32, ar)
            RS = sb("RS", [P, QKC], F32, ar)
            STK = sb("STK", [P, NH + KVH, 4, HD], F32R, ar)
            VB = sb("VB", [P, TT, KVH, HD + 1], F32, ar)
            QT1 = sb("QT1", [P, NH, S], F32R, ar)
            KT1 = sb("KT1", [P, KVH, S], F32R, ar)
            NM1 = sb("NM1", [P, 3, 2], F32, ar)
            PE1 = sb("PE1", [P, 3, 2, S], F32, ar)
            PT1 = sb("PT1", [P, 3, 2, S], F32, ar)
            RS1 = sb("RS1", [P, 2, 2], F32, ar)
            AO = sb("AO", [P, TT, D], F32, ar)
            AOT = sb("AOT", [P, 2, KT, P], F32, ar)

        b_w = sem("b_w"); b_wo = sem("b_wo"); b_ones = sem("b_ones"); b_ln = sem("b_ln"); b_lp = sem("b_lp"); b_rstd = sem("b_rstd"); b_xn = sem("b_xn")
        b_xtp = sem("b_xtp"); b_xt = sem("b_xt"); b_pr = sem("b_pr"); b_v = sem("b_v"); b_rot = sem("b_rot"); b_sum = sem("b_sum")
        b_hi = sem("b_hi"); b_lo = sem("b_lo")
        b_tp = sem("b_tp"); b_qt = sem("b_qt"); b_s = sem("b_s"); b_mx = sem("b_mx"); b_e = sem("b_e")
        b_ptp = sem("b_ptp"); b_pt0 = sem("b_pt0"); b_pt1 = sem("b_pt1"); b_o = sem("b_o"); b_rs = sem("b_rs"); b_ao = sem("b_ao")
        b_aop = sem("b_aop"); b_aot = sem("b_aot"); b_out = sem("b_out"); b_res = sem("b_res")
        UN = NH // 2 * TT
        LT, LV = 2, 4
        OUT_BANK = (7, 4, 7, 6)
        NSK = (NH + KVH) // 4

        def b_sync(eng):
            eng.dma_start(WB[:, :, :], a["wqkv"].rearrange("(k p) n -> p k n", p=P)).then_inc(b_w, 16)
            eng.dma_start(WO1[:, :, :], a["wo1"].rearrange("(k p) n -> p k n", p=P)).then_inc(b_wo, 16)

        def b_pool(eng):
            eng.sem_inc(b_sum, 1)
            with eng.Fori(0, NB) as b:
                eng.wait_ge(b_ln, b * 2 * TT + 2 * TT)
                eng.sem_inc(s_alone, 1)
                eng.tensor_scalar(VEPS[:, :], MV[:, :, 1], 1e-5, 1.0, ALU.add, ALU.mult).then_inc(b_lp, 1)
                eng.wait_ge(b_lp, b + 1)
                eng.tensor_tensor(RSTD[:, :], VEPS[:, :], NHALF[:, 0:TT], ALU.pow).then_inc(b_rstd, 1)
                for t in range(TT):
                    n = b * TT + t
                    eng.wait_ge(b_rot, n * 4 + 4)
                    eng.wait_ge(b_lo, n + 1)
                    eng.tensor_tensor(RS[:, :], RA[:, :], RB[:, :], ALU.add).then_inc(b_sum, 1)

        def b_turns(eng, front, units, turn_over, out):
            front(0)
            with eng.Fori(0, NB - 1) as b:
                units(b, True)
                turn_over(b)
            units(NB - 1, False)
            out(NB - 1)

        def b_dve(eng):
            eng.sem_inc(b_lo, 1)
            eng.memset(VB[:, :, :, HD:HD + 1], 1.0).then_inc(b_ones, 1)

            def stats(b, t):
                eng.bn_stats(STAT[:, t, :], hrow(b * TT + t)).then_inc(b_ln, 1)

            def moments(b):
                eng.wait_ge(b_ln, b * 2 * TT + TT)
                eng.sem_inc(s_alone, 1)
                for t in range(TT):
                    eng.bn_aggr(MV[:, t, :], STAT[:, t:t + 1, :]).then_inc(b_ln, 1)

            def fronts(b):
                def norm(t):
                    n = b * TT + t
                    if t >= 2:
                        eng.wait_ge(b_xtp, n - 1)
                    eng.tensor_scalar(BXN[:, t % 2, :], hrow(n), MV[:, t, 0:1], RSTD[:, t:t + 1],
                                      ALU.subtract, ALU.mult).then_inc(b_xn, 1)

                def rotate(t):
                    n = b * TT + t
                    eng.wait_ge(b_pr, n + 1)
                    eng.wait_ge(b_sum, n + 1)
                    for o, nh, src, tab in ((0, NH, PS[:, 1 + 2 * (t % 2), :], C_RQ1),
                                            (D, KVH, PS[:, 2 + 2 * (t % 2), 0:D // 2], C_RK1)):
                        c0 = tab + t * 2 * HD
                        cos = CST[:, c0:c0 + HD].unsqueeze(1).to_broadcast([P, nh, HD])
                        eng.tensor_tensor(RA[:, o:o + nh * HD].rearrange("p (h d) -> p h d", d=HD),
                                          src.rearrange("p (h d) -> p h d", d=HD), cos, ALU.mult).then_inc(b_rot, 1)
                        x = src.rearrange("p (h d e) -> p h d e", d=HD // 2, e=2)
                        y = RB[:, o:o + nh * HD].rearrange("p (h d e) -> p h d e", d=HD // 2, e=2)
                        sn = CST[:, c0 + HD:c0 + 2 * HD].rearrange("p (d e) -> p d e", e=2)
                        for e in range(2):
                            ins = eng.tensor_tensor(y[:, :, :, e], x[:, :, :, 1 - e],
                                                    sn[:, :, e].unsqueeze(1).to_broadcast([P, nh, HD // 2]), ALU.mult)
                        ins.then_inc(b_rot, 1)

                def low(t):
                    n = b * TT + t
                    eng.wait_ge(b_hi, 2 * n + 2)
                    r = RS[:, :].rearrange("p (h d) -> p h d", d=HD)
                    eng.tensor_tensor(STK[:, 0:NH, 2:4, :], r[:, 0:NH, :].unsqueeze(2).to_broadcast([P, NH, 2, HD]),
                                      STK[:, 0:NH, 0:2, :].bitcast(F32), ALU.subtract)
                    k = STK[:, NH:, :, :].rearrange("p h (x y) d -> p h x y d", y=2)
                    for x in range(2):
                        ins = eng.tensor_tensor(k[:, :, x, 1, :], r[:, NH:, :], k[:, :, x, 0, :].bitcast(F32), ALU.subtract)
                    ins.then_inc(b_lo, 1)

                return norm, rotate, low

            def front(b):
                norm, rotate, low = fronts(b)
                for t in range(TT):
                    stats(b, t)
                moments(b)
                eng.wait_ge(b_rstd, b + 1)
                norm(0)
                norm(1)
                for t in range(TT):
                    rotate(t)
                    if t + 2 < TT:
                        norm(t + 2)
                    low(t)

            def units(b, more):
                def top(m):
                    k = b * UN + m
                    eng.wait_ge(b_s, k + 1)
                    eng.tensor_reduce(NM1[:, m % 3, :], PS[:, 2 * (m % 2):2 * (m % 2) + 2, :], AX, ALU.max, negate=True)\
                       .then_inc(b_mx, 1)

                def turned(m):
                    eng.wait_ge(b_ptp, b * UN + m + 1)
                    if m >= 3:
                        eng.wait_ge(b_o, b * UN + m - 2)
                    eng.tensor_copy(PT1[:, m % 3, 0, :], PS[:, 4, :]).then_inc(b_pt0, 1)

                def norm_out(m):
                    hp, t = divmod(m, TT)
                    k = b * UN + m
                    eng.wait_ge(b_o, k + 1)
                    o = PS[:, 6 + m % 2, 0:2 * (HD + 1)].rearrange("p (r d) -> p r d", d=HD + 1)
                    eng.reciprocal(RS1[:, m % 2, :], o[:, :, HD]).then_inc(b_rs, 1)
                    eng.wait_ge(b_rs, k + 1)
                    c = 2 * hp * HD
                    eng.tensor_tensor(AO[:, t, c:c + 2 * HD].rearrange("p (r d) -> p r d", d=HD), o[:, :, 0:HD],
                                      RS1[:, m % 2, :].unsqueeze(2).to_broadcast([P, 2, HD]), ALU.mult).then_inc(b_ao, 1)

                for m in range(UN + LV):
                    if m < UN:
                        top(m)
                    if LT <= m < UN + LT:
                        turned(m - LT)
                    if m >= LV:
                        norm_out(m - LV)
                    if more and 8 <= m < 8 + TT:
                        stats(b + 1, m - 8)
                    if more and m == 8 + TT:
                        moments(b + 1)
                    if more and m == 20:
                        eng.wait_ge(b_rstd, b + 2)
                    if more and m in (20, 22):
                        fronts(b + 1)[0]((m - 20) // 2)

            def residual(b, t):
                n = b * TT + t
                eng.wait_ge(b_out, n + 1)
                eng.tensor_tensor(hrow(n), PS[:, OUT_BANK[t], :], hrow(n), ALU.add).then_inc(b_res, 1)

            def turn_over(b):
                norm, rotate, low = fronts(b + 1)
                residual(b, 0)
                norm(2)
                rotate(0)
                residual(b, 1)
                low(0)
                rotate(1)
                residual(b, 2)
                residual(b, 3)
                norm(3)
                low(1)
                for t in range(2, TT):
                    rotate(t)
                    low(t)

            def out(b):
                for t in range(TT):
                    residual(b, t)
            b_turns(eng, front, units, turn_over, out)

        def b_act(eng):
            eng.sem_inc(b_xt, 1)
            eng.sem_inc(b_qt, 3)

            def fronts(b):
                def inputs(t):
                    n = b * TT + t
                    eng.wait_ge(b_xtp, n + 1)
                    if t >= 2:
                        eng.wait_ge(b_pr, n - 1)
                    eng.activation(flat(BXT[:, t % 2, :, :]), PS[:, 0, :], ACT.Copy).then_inc(b_xt, 1)

                def high(t):
                    n = b * TT + t
                    eng.wait_ge(b_rot, n * 4 + 4)
                    eng.activation(VB[:, t, :, 0:HD], PS[:, 2 + 2 * (t % 2), D // 2:].rearrange("p (h d) -> p h d", d=HD),
                                   ACT.Copy).then_inc(b_v, 1)
                    eng.wait_ge(b_sum, n + 2)
                    eng.wait_ge(b_tp, n * NSK + 1)
                    r = RS[:, :].rearrange("p (h d) -> p h d", d=HD)
                    eng.activation(STK[:, 0:NH, 0:2, :], r[:, 0:NH, :].unsqueeze(2).to_broadcast([P, NH, 2, HD]), ACT.Copy)\
                       .then_inc(b_hi, 1)
                    k = STK[:, NH:, :, :].rearrange("p h (x y) d -> p h x y d", y=2)
                    eng.activation(k[:, :, :, 0, :], r[:, NH:, :].unsqueeze(2).to_broadcast([P, KVH, 2, HD]), ACT.Copy)\
                       .then_inc(b_hi, 1)

                def stacks(t):
                    n = b * TT + t
                    for c in range(NSK):
                        eng.wait_ge(b_tp, n * NSK + c + 2)
                        dst = QT1[:, 4 * c:4 * c + 4, :] if c < 4 else KT1[:, 4 * c - NH:4 * c - NH + 4, :]
                        eng.activation(dst[:, :, t * P:(t + 1) * P], PS[:, 5 + c % 3, :].rearrange("p (g q) -> p g q", q=P),
                                       ACT.Copy).then_inc(b_qt, 1)

                return inputs, high, stacks

            def front(b):
                inputs, high, stacks = fronts(b)
                inputs(0)
                inputs(1)
                for t in range(TT):
                    if t + 2 < TT:
                        inputs(t + 2)
                    high(t)
                    stacks(t)

            def units(b, more):
                def exps(m):
                    k = b * UN + m
                    eng.wait_ge(b_mx, k + 1)
                    if m >= 3:
                        eng.wait_ge(b_ptp, k - 2)
                    for r in range(2):
                        eng.activation(PE1[:, m % 3, r, :], PS[:, 2 * (m % 2) + r, :], ACT.Exp,
                                       bias=NM1[:, m % 3, r:r + 1]).then_inc(b_e, 1)

                def turned(m):
                    eng.wait_ge(b_ptp, b * UN + m + 1)
                    if m >= 3:
                        eng.wait_ge(b_o, b * UN + m - 2)
                    eng.activation(PT1[:, m % 3, 1, :], PS[:, 5, :], ACT.Copy).then_inc(b_pt1, 1)

                for m in range(UN + LT):
                    if m >= LT:
                        turned(m - LT)
                    if m < UN:
                        exps(m)

            def out_turned(b, t):
                eng.wait_ge(b_aop, b * TT + t + 1)
                eng.activation(flat(AOT[:, t % 2, :, :]), PS[:, 5 + t % 2, :], ACT.Copy).then_inc(b_aot, 1)

            def turn_over(b):
                inputs, high, stacks = fronts(b + 1)
                for t in range(2):
                    out_turned(b, t)
                    inputs(t)
                for t in range(2, TT):
                    out_turned(b, t)
                high(0)
                inputs(2)
                stacks(0)
                inputs(3)
                for t in range(1, TT):
                    high(t)
                    stacks(t)

            def out(b):
                for t in range(TT):
                    out_turned(b, t)
            b_turns(eng, front, units, turn_over, out)

        def b_pe(eng):
            eng.sem_inc(b_tp, 1)
            eng.wait_ge(b_ones, 1)

            def fronts(b):
                def inputs(t):
                    n = b * TT + t
                    eng.wait_ge(b_xn, n + 1)
                    eng.wait_ge(b_xt, n + 1)
                    for k in range(KT):
                        mm = eng.transpose(PS[:, 0, k * P:(k + 1) * P], BXN[:, t % 2, k * P:(k + 1) * P], ident)
                    mm.then_inc(b_xtp, 1)

                def products(t):
                    n = b * TT + t
                    eng.wait_ge(b_xt, n + 2)
                    if t >= 2:
                        eng.wait_ge(b_v, n - 1)
                    for k in range(KT):
                        eng.matmul(PS[:, 1 + 2 * (t % 2), :], BXT[:, t % 2, k, :], WB[:, k, 0:D],
                                   start=(k == 0), stop=(k == KT - 1))
                        mm = eng.matmul(PS[:, 2 + 2 * (t % 2), :], BXT[:, t % 2, k, :], WB[:, k, D:],
                                        start=(k == 0), stop=(k == KT - 1))
                    mm.then_inc(b_pr, 1)

                def stacks(t):
                    n = b * TT + t
                    eng.wait_ge(b_lo, n + 2)
                    for c in range(NSK):
                        eng.wait_ge(b_qt, n * NSK + c + 1)
                        for k in range(4):
                            mm = eng.transpose(PS[:, 5 + c % 3, k * P:(k + 1) * P],
                                               STK[:, 4 * c + k, :, :].rearrange("p x d -> p (x d)").bitcast(F32), ident)
                        mm.then_inc(b_tp, 1)

                return inputs, products, stacks

            def all_in(b):
                eng.wait_ge(b_qt, (b * TT + TT) * NSK + 3)
                eng.wait_ge(b_v, b * TT + TT)

            def front(b):
                inputs, products, stacks = fronts(b)
                inputs(0)
                inputs(1)
                eng.wait_ge(b_w, 16)
                products(0)
                for t in range(TT):
                    if t + 2 < TT:
                        inputs(t + 2)
                    if t + 1 < TT:
                        products(t + 1)
                    stacks(t)

            def units(b, more):
                all_in(b)

                def scores(m):
                    hp, t = divmod(m, TT)
                    k = b * UN + m
                    if m >= 2:
                        eng.wait_ge(b_e, 2 * k - 2)
                    for r in range(2):
                        mm = eng.matmul(PS[:, 2 * (m % 2) + r, :], QT1[:, 2 * hp + r, t * P:(t + 1) * P],
                                        KT1[:, hp, :], start=True, stop=True)
                    mm.then_inc(b_s, 1)

                def turn(m):
                    k = b * UN + m
                    eng.wait_ge(b_e, 2 * k + 2)
                    if m >= 1:
                        eng.wait_ge(b_pt0, k)
                        eng.wait_ge(b_pt1, k)
                    for r in range(2):
                        for c in range(TT):
                            mm = eng.transpose(PS[:, 4 + r, c * P:(c + 1) * P], PE1[:, m % 3, r, c * P:(c + 1) * P], ident)
                    mm.then_inc(b_ptp, 1)

                def values(m):
                    hp, t = divmod(m, TT)
                    k = b * UN + m
                    eng.wait_ge(b_pt0, k + 1)
                    eng.wait_ge(b_pt1, k + 1)
                    if m >= 2:
                        eng.wait_ge(b_ao, k - 1)
                    for r in range(2):
                        for c in range(TT):
                            mm = eng.matmul(PS[:, 6 + m % 2, r * (HD + 1):(r + 1) * (HD + 1)],
                                            PT1[:, m % 3, r, c * P:(c + 1) * P], VB[:, c, hp, :],
                                            start=(c == 0), stop=(c == TT - 1))
                    mm.then_inc(b_o, 1)

                for m in range(UN + LV):
                    if m < UN:
                        scores(m)
                    if LT <= m < UN + LT:
                        turn(m - LT)
                    if m >= LV:
                        values(m - LV)
                eng.wait_ge(b_ao, b * UN + UN)
                eng.wait_ge(b_wo, 16)

            def out_turn(b, t):
                n = b * TT + t
                if t >= 2:
                    eng.wait_ge(b_aot, n - 1)
                for k in range(KT):
                    mm = eng.transpose(PS[:, 5 + t % 2, k * P:(k + 1) * P], AO[:, t, k * P:(k + 1) * P], ident)
                mm.then_inc(b_aop, 1)

            def out_product(b, t):
                n = b * TT + t
                eng.wait_ge(b_aot, n + 1)
                if t == 2:
                    eng.wait_ge(b_res, n - 1)
                if t == 3:
                    eng.wait_ge(b_aot, n + 1)
                for k in range(KT):
                    mm = eng.matmul(PS[:, OUT_BANK[t], :], AOT[:, t % 2, k, :], WO1[:, k, :], start=(k == 0), stop=(k == KT - 1))
                mm.then_inc(b_out, 1)

            def turn_over(b):
                inputs, products, stacks = fronts(b + 1)
                for t in range(2):
                    out_turn(b, t)
                    inputs(t)
                out_product(b, 0)
                products(0)
                out_product(b, 1)
                out_turn(b, 2)
                out_turn(b, 3)
                eng.wait_ge(b_res, b * TT + 2)
                products(1)
                out_product(b, 2)
                inputs(2)
                out_product(b, 3)
                eng.wait_ge(b_res, b * TT + TT)
                stacks(0)
                inputs(3)
                products(2)
                stacks(1)
                products(3)
                stacks(2)
                stacks(3)

            def out(b):
                out_turn(b, 0)
                out_turn(b, 1)
                out_product(b, 0)
                out_turn(b, 2)
                out_product(b, 1)
                out_turn(b, 3)
                out_product(b, 2)
                out_product(b, 3)
            b_turns(eng, front, units, turn_over, out)

        FK = FF // P
        CHK = KT
        with Arena() as ar:
            CFQ = sb("CFQ", [P, KT, FF], F32R, ar)
            CPQ = sb("CPQ", [P, FK, D], BF16, ar)
            ONES = sb("ONES", [P, P], F32, ar)
            ABS = sb("ABS", [P, 2 * CHK], F32, ar)
            WSUM = sb("WSUM", [P, 2], F32, ar)
            WSC = sb("WSC", [P, 4], F32, ar)
            with Arena() as tmp:
                CF = sb("CF", [P, CHK, FF], F32, tmp)
                CP = sb("CP", [P, CHK, FF], F32, tmp)
                JUNKG = sb("JUNKG", [P, 2, D], F32, tmp)
            GXN = sb("GXN", [P, 2, D], F32, ar)
            GXH = sb("GXH", [P, 2, D], F32R, ar)
            GXL = sb("GXL", [P, 2, D], F32R, ar)
            GV = sb("GV", [P, 2, 8], F32, ar)
            GR1 = sb("GR1", [P, 2, FF], F32, ar)
            GY = sb("GY", [P, FF], F32, ar)
            GQ = sb("GQ", [P, 2, FF], BF16, ar)
            GT = sb("GT", [P, 2, FK, P], BF16, ar)

        g_w = [sem("g_w%d" % i) for i in range(8)]; g_sq = sem("g_sq"); g_mean = sem("g_mean"); g_xsum = sem("g_xsum"); g_c2 = sem("g_c2"); g_qd = sem("g_qd"); g_abs = sem("g_abs"); g_sum = sem("g_sum"); g_sc = sem("g_sc"); g_t = sem("g_t"); g_one = sem("g_one")
        g_pv = sem("g_pv"); g_rstd = sem("g_rstd"); g_xn = sem("g_xn"); g_xtp = sem("g_xtp"); g_hi = sem("g_hi")
        g_lo = sem("g_lo"); g_mm = sem("g_mm"); g_r = sem("g_r"); g_mx = sem("g_mx"); g_c = sem("g_c"); g_y = sem("g_y"); g_q = sem("g_q")
        g_tp = sem("g_tp"); g_ta = sem("g_ta"); g_tb = sem("g_tb"); g_op = sem("g_op"); g_res = sem("g_res"); g_p1 = sem("g_p1")
        G_C, G_ST = 4, 5

        def gw_sync(eng):
            cf = a["c_fc"].rearrange("(k p) n -> k p n", p=P)
            cp = a["c_projT"].rearrange("(c k p) n -> c p k n", p=P, c=CHK)
            for i in range(CHK):
                eng.dma_start(CF[:, i, :], cf[i]).then_inc(g_w[i], 16)
            for i in range(CHK):
                eng.dma_start(CP[:, i, :].rearrange("p (k n) -> p k n", n=D), cp[i]).then_inc(g_w[CHK + i], 16)

        def w_chunk(i):
            if i < CHK:
                return CF[:, i, :], CFQ[:, i, :]
            return CP[:, i - CHK, :], flat(CPQ[:, (i - CHK) * KT:(i - CHK + 1) * KT, :])

        def gw_dve(eng):
            eng.memset(ONES[:, :], 1.0).then_inc(g_one, 1)

            def total(i):
                eng.wait_ge(g_w[i], 16)
                eng.tensor_reduce(ABS[:, i:i + 1], w_chunk(i)[0], AX, ALU.add, apply_absolute_value=True).then_inc(g_abs, 1)

            def scale(w):
                eng.wait_ge(g_sum, w + 1)
                eng.tensor_reduce(WSUM[:, w:w + 1], PS[:, 0, w * CHK:(w + 1) * CHK], AX, ALU.add).then_inc(g_sc, 1)
                eng.wait_ge(g_sc, 3 * w + 1)
                eng.tensor_scalar(WSC[:, w:w + 1], WSUM[:, w:w + 1], 1.0 / (D * FF), 1e-5, ALU.mult, ALU.max).then_inc(g_sc, 1)
                eng.wait_ge(g_sc, 3 * w + 2)
                eng.reciprocal(WSC[:, 2 + w:3 + w], WSC[:, w:w + 1]).then_inc(g_sc, 1)
                eng.wait_ge(g_sc, 3 * w + 3)

            def cut_low(i):
                w = w_chunk(i)[0]
                eng.tensor_scalar(w, w, WSC[:, 2 + i // CHK:3 + i // CHK], -1.0, ALU.mult, ALU.max).then_inc(g_c2, 1)

            def cut_high(i):
                w = w_chunk(i)[0]
                eng.wait_ge(g_c2, i + 1)
                eng.tensor_scalar(w, w, 1.0, MAGIC, ALU.min, ALU.add).then_inc(g_t, 1)

            for i in range(CHK):
                total(i)
            scale(0)
            for i in range(CHK):
                cut_low(i)
                total(CHK + i)
                cut_high(i)
            scale(1)
            cut_low(CHK)
            for i in range(CHK + 1, 2 * CHK):
                cut_low(i)
                cut_high(i - 1)
            cut_high(2 * CHK - 1)

        def gw_pe(eng):
            eng.wait_ge(g_one, 1)
            for w in range(2):
                c = slice(w * CHK, (w + 1) * CHK)
                eng.wait_ge(g_abs, (w + 1) * CHK)
                eng.matmul(PS[:, 0, c], ONES[:, :], ABS[:, c], start=True, stop=True).then_inc(g_sum, 1)

        def gw_act(eng):
            stats_act(eng, JUNKG, g_xsum, g_mean, g_sq, lambda n: None)
            for i in range(2 * CHK):
                w, q = w_chunk(i)
                eng.wait_ge(g_t, i + 1)
                eng.activation(q, w, ACT.Copy, bias=-MAGIC).then_inc(g_qd, 1)

        def gw_pool(eng):
            mean_pool(eng, g_xsum, g_mean)
            rstd_pool(eng, g_sq, g_pv, g_rstd)
            eng.wait_ge(g_rstd, 1)

        def g_dve(eng):
            def norm(n, u):
                eng.tensor_scalar(GXN[:, u, :], hrow(n), LNS[:, LRSTD, bass.ds(n, 1)], LNS[:, LNM, bass.ds(n, 1)],
                                  ALU.mult, ALU.add).then_inc(g_xn, 1)

            def low(n, u):
                eng.wait_ge(g_hi, n + 1)
                eng.tensor_tensor(GXL[:, u, :], PS[:, 0, :], GXH[:, u, :].bitcast(F32), ALU.subtract).then_inc(g_lo, 1)

            def peak(n, u):
                eng.wait_ge(g_r, 4 * n + 8)
                eng.tensor_reduce(GV[:, u, V_AM:V_AM + 1], GR1[:, u, :], AX, ALU.max).then_inc(g_mx, 1)

            def rounded(n, u):
                eng.wait_ge(g_y, n + 1)
                eng.tensor_scalar(GQ[:, u, :], GY[:, :], MAGIC, MAGIC, ALU.add, ALU.subtract).then_inc(g_q, 1)

            def turned(n, u):
                eng.wait_ge(g_tp, n + 1)
                eng.tensor_copy(flat(GT[:, u, 0:8, :]), PS[:, 5, :].bitcast(BF16)).then_inc(g_ta, 1)

            def fin(n, u):
                eng.wait_ge(g_op, n + 1)
                eng.scalar_tensor_tensor(hrow(n), PS[:, 7, :], GV[:, u, G_ST:G_ST + 1], hrow(n), ALU.mult, ALU.add)\
                   .then_inc(g_res, 1)

            eng.sem_inc(g_lo, 1)
            eng.sem_inc(g_ta, 1)
            eng.sem_inc(g_res, 1)
            eng.sem_inc(g_q, 1)
            norm(0, 0)
            norm(1, 1)
            low(0, 0)

            def step(n, u, on):
                if on(-1):
                    peak(n - 1, 1 - u)
                if on(2):
                    norm(n + 2, u)
                if on(-2):
                    turned(n - 2, u)
                if on(1):
                    low(n + 1, 1 - u)
                if on(-1):
                    rounded(n - 1, 1 - u)
                if on(-2):
                    fin(n - 2, u)
            pipeline(eng, step, 2)

        def g_pool(eng):
            def token_scales(n, u):
                v = GV[:, u, :]
                eng.wait_ge(g_mx, n + 1)
                eng.tensor_tensor(v[:, V_AM:V_AM + 1], v[:, V_AM:V_AM + 1], v[:, V_AM:V_AM + 1], ALU.mult).then_inc(g_p1, 1)
                eng.wait_ge(g_p1, n * 4 + 1)
                eng.sem_inc(s_alone, 1)
                eng.tensor_scalar(v[:, V_AM:V_AM + 1], v[:, V_AM:V_AM + 1], 1e-5, None, ALU.max).then_inc(g_p1, 1)
                eng.wait_ge(g_p1, n * 4 + 2)
                eng.sem_inc(s_alone, 1)
                eng.tensor_scalar(v[:, V_AM:V_AM + 1], v[:, V_AM:V_AM + 1], 1.0 / 255.0, 1.0, ALU.mult, ALU.mult)\
                   .then_inc(g_p1, 1)
                eng.wait_ge(g_p1, n * 4 + 3)
                eng.tensor_tensor(v[:, G_ST:G_ST + 1], v[:, V_AM:V_AM + 1], WSC[:, 1:2], ALU.mult).then_inc(g_p1, 1)
                eng.tensor_tensor(v[:, G_C:G_C + 1], v[:, V_AM:V_AM + 1], NHALF[:, 0:1], ALU.pow).then_inc(g_c, 1)

            def step(n, u, on):
                if on(-1):
                    token_scales(n - 1, 1 - u)
            pipeline(eng, step, 1)

        def g_act(eng):
            def high(n, u):
                eng.wait_ge(g_xtp, n + 1)
                eng.activation(GXH[:, u, :], PS[:, 0, :], ACT.Copy).then_inc(g_hi, 1)

            def relu(n, u, c):
                eng.wait_ge(g_mm, 4 * n + c + 1)
                eng.activation(GR1[:, u, c * 512:(c + 1) * 512], PS[:, 1 + c, :], ACT.Relu, scale=WSC[:, 0:1])\
                   .then_inc(g_r, 1)

            def squared(n, u):
                eng.wait_ge(g_c, n + 1)
                eng.wait_ge(g_q, n + 1)
                eng.activation(GY[:, :], GR1[:, u, :], ACT.Square, scale=GV[:, u, G_C:G_C + 1]).then_inc(g_y, 1)

            def turned(n, u):
                eng.wait_ge(g_tp, n + 1)
                eng.activation(flat(GT[:, u, 8:16, :]), PS[:, 6, :].bitcast(BF16), ACT.Copy).then_inc(g_tb, 1)

            eng.sem_inc(g_r, 4)
            eng.sem_inc(g_tb, 1)
            high(0, 0)

            def step(n, u, on):
                if on(-2):
                    eng.wait_ge(g_q, n)
                for c in range(2):
                    if on(0):
                        relu(n, u, c)
                if on(-2):
                    turned(n - 2, u)
                if on(1):
                    high(n + 1, 1 - u)
                if on(-1):
                    squared(n - 1, 1 - u)
                for c in range(2, 4):
                    if on(0):
                        relu(n, u, c)
            pipeline(eng, step, 2)

        def g_pe(eng):
            def xt(n, u):
                eng.wait_ge(g_xn, n + 1)
                eng.wait_ge(g_lo, n + 1)
                for k in range(KT):
                    mm = eng.transpose(PS[:, 0, k * P:(k + 1) * P], GXN[:, u, k * P:(k + 1) * P], ident)
                mm.then_inc(g_xtp, 1)

            def up(n, u, c):
                if c == 0:
                    eng.wait_ge(g_lo, n + 2)
                eng.wait_ge(g_r, 4 * n + 1 + c)
                for k in range(KT):
                    for x in (GXH, GXL):
                        mm = eng.matmul(PS[:, 1 + c, :], x[:, u, k * P:(k + 1) * P], CFQ[:, k, c * 512:(c + 1) * 512],
                                        start=(k == 0 and x is GXH), stop=(k == KT - 1 and x is GXL))
                mm.then_inc(g_mm, 1)

            def turn(n, u):
                eng.wait_ge(g_q, n + 2)
                eng.wait_ge(g_ta, n + 1)
                eng.wait_ge(g_tb, n + 1)
                for k in range(FK):
                    mm = eng.transpose(PS[:, 5 + k // 8, (k % 8) * 64:(k % 8 + 1) * 64].bitcast(BF16),
                                       GQ[:, u, k * P:(k + 1) * P], IDB[:, :])
                mm.then_inc(g_tp, 1)

            def proj(n, u):
                eng.wait_ge(g_ta, n + 2)
                eng.wait_ge(g_tb, n + 2)
                eng.wait_ge(g_res, n + 1)
                for k in range(FK):
                    mm = eng.matmul(PS[:, 7, :], GT[:, u, k, :], CPQ[:, k, :], start=(k == 0), stop=(k == FK - 1))
                mm.then_inc(g_op, 1)

            xt(0, 0)

            def step(n, u, on):
                if on(0):
                    up(n, u, 0)
                    up(n, u, 1)
                if on(-2):
                    turn(n - 2, u)
                if on(1):
                    xt(n + 1, 1 - u)
                if on(0):
                    up(n, u, 2)
                    up(n, u, 3)
                if on(-2):
                    proj(n - 2, u)
            pipeline(eng, step, 2)

        block = ctx.enter_context(nc.Block())

        @block.sync
        def _(eng):
            sync_eng[0] = eng
            e_sync(eng)
            w_sync(eng)
            barrier(eng)
            l_sync(eng)
            barrier(eng, clears=True)
            a_sync(eng)
            barrier(eng)
            if "F" in stages:
                fw_sync(eng)
                barrier(eng)
                barrier(eng)
            if "B" in stages:
                b_sync(eng)
                barrier(eng)
            if "G" in stages:
                gw_sync(eng)
                barrier(eng)
                barrier(eng)
            eng.dma_start(out.rearrange("b (t p) n -> p (b t) n", p=P), H[:, :, :]).then_inc(s_ids, 16)
            eng.wait_ge(s_ids, 48)

        @block.gpsimd
        def _(eng):
            e_pool(eng)
            barrier(eng)
            l_pool(eng)
            barrier(eng)
            a_pool(eng)
            barrier(eng)
            if "F" in stages:
                fx_pool(eng)
                barrier(eng)
                f_pool(eng)
                barrier(eng)
            if "B" in stages:
                b_pool(eng)
                barrier(eng)
            if "G" in stages:
                gw_pool(eng)
                barrier(eng)
                g_pool(eng)
                barrier(eng)

        @block.scalar
        def _(eng):
            e_act(eng)
            barrier(eng)
            l_act(eng)
            barrier(eng)
            a_act(eng)
            barrier(eng)
            if "F" in stages:
                fx_act(eng)
                barrier(eng)
                f_act(eng)
                barrier(eng)
            if "B" in stages:
                b_act(eng)
                barrier(eng)
            if "G" in stages:
                gw_act(eng)
                barrier(eng)
                g_act(eng)
                barrier(eng)

        @block.vector
        def _(eng):
            e_dve(eng)
            barrier(eng)
            l_dve(eng)
            barrier(eng)
            a_dve(eng)
            barrier(eng)
            if "F" in stages:
                fw_dve(eng)
                barrier(eng)
                f_dve(eng)
                barrier(eng)
            if "B" in stages:
                b_dve(eng)
                barrier(eng)
            if "G" in stages:
                gw_dve(eng)
                barrier(eng)
                g_dve(eng)
                barrier(eng)

        @block.tensor
        def _(eng):
            e_pe(eng)
            barrier(eng)
            l_pe(eng)
            barrier(eng)
            a_pe(eng)
            barrier(eng)
            if "F" in stages:
                fx_pe(eng)
                barrier(eng)
                f_pe(eng)
                barrier(eng)
            if "B" in stages:
                b_pe(eng)
                barrier(eng)
            if "G" in stages:
                gw_pe(eng)
                barrier(eng)
                g_pe(eng)
                barrier(eng)


NAMES = {"L0_tok_ts_w": "ts_w", "L0_tok_pos_w": "pos_w", "L0_attn_q_norm_w": "q_norm_w", "L0_attn_wq_b": "wq_b",
         "L0_attn_kv_norm_w": "kv_norm_w", "L0_attn_wkv_b": "wkv_b",
         "L0_ffn_w_gate_up": "w_gate_up", "L0_ffn_w_down": "w_down", "L1_attn_wo": "wo1", "L1_ffn_c_fc": "c_fc"}


def layouts(inputs):
    g = {v: np.ascontiguousarray(inputs[k]) for k, v in NAMES.items()}
    x = np.asarray(inputs["x"])
    g["x"] = np.ascontiguousarray(x)
    nxt = np.concatenate([x[:, 1:], x[:, -1:]], 1).reshape(NT * 4, 32).T
    g["ext"] = np.ascontiguousarray(np.concatenate([nxt] * 4, 0))
    g["woT"] = np.ascontiguousarray(np.asarray(inputs["L0_attn_wo"]).T)
    g["waT"] = np.ascontiguousarray(np.concatenate([inputs["L0_attn_wq_a"], inputs["L0_attn_wkv_a"]], 0).T)
    wpe = np.asarray(inputs["L0_attn_wq_b"]).reshape(NH, LORA + ROPE, QLORA)[:, LORA:].transpose(0, 2, 1)
    g["wpe"] = np.ascontiguousarray(np.concatenate([wpe, wpe[:, :, ROPE // 2:], wpe[:, :, :ROPE // 2]], 2))
    g["wqkv"] = np.ascontiguousarray(np.concatenate([inputs["L1_attn_wq"], inputs["L1_attn_wk"], inputs["L1_attn_wv"]], 1))
    g["c_projT"] = np.ascontiguousarray(np.asarray(inputs["L1_ffn_c_proj"]).T)
    g["consts"] = constants()
    return g


def kernel(**inputs):
    import concourse.bacc as bacc
    from concourse.bass_utils import run_bass_kernel_spmd

    nc = bacc.Bacc("TRN2", target_bir_lowering=False, num_devices=1)
    arrays, aps = {}, {}
    for name, v in layouts(inputs).items():
        arrays["in_" + name] = v
        aps[name] = nc.dram_tensor("in_" + name, v.shape, mybir.dt.from_np(v.dtype), kind="ExternalInput").ap()
    out = nc.dram_tensor("out_0", (NB, S, D), F32, kind="ExternalOutput").ap()
    tower_kernel(nc, aps, out)
    r = run_bass_kernel_spmd(nc, [arrays], core_ids=[0])
    return r.results[0]["out_0"]
```
